# Optimizing a Trainium2 kernel written in Bass

```python
import numpy as np
import jax
import jax.numpy as jnp

def _softmax(x, axis=-1):
    return jax.nn.softmax(x, axis=axis)

def _gelu(x):
    return jax.nn.gelu(x, approximate=True)

def _silu(x):
    return jax.nn.silu(x)

def _sigmoid(x):
    return jax.nn.sigmoid(x)

def _layernorm(x, axis=-1, eps=1e-05):
    m = jnp.mean(x, axis=axis, keepdims=True)
    v = jnp.var(x, axis=axis, keepdims=True)
    return (x - m) / jnp.sqrt(v + eps)

def _scatter_add(tgt, idx, src, axis=0):
    return tgt.at[idx].add(src)

def _segment_sum(src, seg, n):
    return jax.ops.segment_sum(src, seg, n)
kernel_name = 'mk_flamingo_gated_d4_seqx_r8_9c90d0'

def setup_inputs(seed: int=0):
    np.random.seed(seed)
    _w = jnp.asarray

    def _rec_inputs():
        import jax
        import jax.numpy as jnp
        _rk = jax.random.key(seed)
        x = 7.22e-05 + 1 * jax.random.normal(jax.random.fold_in(_rk, 1), (8, 256, 128), jnp.float32)
        _lenS = 256 - jax.random.randint(jax.random.fold_in(_rk, 7), (8,), 0, max(1, 256 // 4) + 1, jnp.int32)
        _lenS2 = 1601 - jax.random.randint(jax.random.fold_in(_rk, 8), (8,), 0, max(1, 1601 // 4) + 1, jnp.int32)
        _ctx_768P = jax.random.normal(jax.random.fold_in(_rk, 11), (8, 16, 96), jnp.float32)
        _ctx_768c = jax.random.dirichlet(jax.random.fold_in(_rk, 511), 0.3 * jnp.ones((16,), jnp.float32), (8, 1601))
        _ctx_768t = jnp.einsum('bsk,bkd->bsd', _ctx_768c, _ctx_768P)
        _ctx_768t = _ctx_768t * jax.lax.rsqrt(jnp.mean(jnp.square(_ctx_768t)) + 1e-12) * 0.953939
        ctx_768 = -0.000191848 + 0.999787 * (_ctx_768t + 0.3 * jax.random.normal(jax.random.fold_in(_rk, 611), (8, 1601, 96), jnp.float32))
        _validS = jnp.arange(256)[None, :] < _lenS[:, None]
        _validS2 = jnp.arange(1601)[None, :] < _lenS2[:, None]
        _causal = jnp.tril(jnp.ones((256, 256), dtype=bool))
        mask_BxS2_bk0 = jnp.logical_not(jnp.broadcast_to(_validS2[:, :], (8, 1601)))
        _g = jax.random.normal(jax.random.fold_in(_rk, 9001), (2, 4), jnp.float32)
        _g = jnp.sign(_g) * jnp.maximum(jnp.abs(_g), 1.0) + (_g == 0) * 1.0
        g_xattn = _g[0]
        g_ffn = _g[1]
        return (x, ctx_768, mask_BxS2_bk0, g_xattn, g_ffn)
    x, ctx_768, mask_BxS2_bk0, g_xattn, g_ffn = _rec_inputs()

    def _L0_xattn_setup():
        import jax, jax.numpy as jnp
        import numpy as np
        HEADS = 8
        DIM_HEAD = 64
        SCALE = DIM_HEAD ** (-0.5)
        key = jax.random.key(seed)
        ks = jax.random.split(key, 7)
        B, Nq, Nc = (4, 256, 256)
        Dq, Dc = (128, 96)
        inner = HEADS * DIM_HEAD
        x = jax.random.normal(ks[0], (B, Nq, Dq), dtype=jnp.float32)
        context = jax.random.normal(ks[1], (B, Nc, Dc), dtype=jnp.float32)
        Wq = jax.random.normal(ks[2], (Dq, inner), dtype=jnp.float32) * Dq ** (-0.5)
        Wk = jax.random.normal(ks[3], (Dc, inner), dtype=jnp.float32) * Dc ** (-0.5)
        Wv = jax.random.normal(ks[4], (Dc, inner), dtype=jnp.float32) * Dc ** (-0.5)
        Wo = jax.random.normal(ks[5], (inner, Dq), dtype=jnp.float32) * inner ** (-0.5)
        bo = jax.random.normal(ks[6], (Dq,), dtype=jnp.float32) * 0.01
        return {'x': x, 'context': context, 'Wq': Wq, 'Wk': Wk, 'Wv': Wv, 'Wo': Wo, 'bo': bo}
    _L0_xattn_all = _L0_xattn_setup()
    _L0_xattn_in = {k: v for k, v in _L0_xattn_all.items() if k in ('Wq', 'Wk', 'Wv', 'Wo', 'bo')}
    del _L0_xattn_all

    def _L0_ffn_setup():
        import jax, jax.numpy as jnp
        import numpy as np
        DIM = 128
        INTER = 64
        E = 16
        TOPK = 4
        N_GROUPS = 4
        TOPK_GROUPS = 2
        ROUTE_SCALE = 1.0
        INIT_STD = 0.02
        B, S = (2, 128)
        key = jax.random.key(seed)
        ks = jax.random.split(key, 8)
        return {'x': jax.random.normal(ks[0], (B, S, DIM), jnp.float32), 'gate_w': jax.random.normal(ks[1], (E, DIM), jnp.float32) * INIT_STD, 'gate_bias': jnp.zeros((E,), jnp.float32), 'w1': jax.random.normal(ks[2], (E, INTER, DIM), jnp.float32) * INIT_STD, 'w2': jax.random.normal(ks[3], (E, DIM, INTER), jnp.float32) * INIT_STD, 'w3': jax.random.normal(ks[4], (E, INTER, DIM), jnp.float32) * INIT_STD, 'ws1': jax.random.normal(ks[5], (INTER, DIM), jnp.float32) * INIT_STD, 'ws2': jax.random.normal(ks[6], (DIM, INTER), jnp.float32) * INIT_STD, 'ws3': jax.random.normal(ks[7], (INTER, DIM), jnp.float32) * INIT_STD}
    _L0_ffn_all = _L0_ffn_setup()
    _L0_ffn_in = {k: v for k, v in _L0_ffn_all.items() if k in ('gate_w', 'gate_bias', 'w1', 'w2', 'w3', 'ws1', 'ws2', 'ws3')}
    del _L0_ffn_all

    def _L1_xattn_setup():
        import jax, jax.numpy as jnp
        import numpy as np
        NUM_HEADS = 16
        CLAMP = 10000.0
        key = jax.random.key(seed)
        ks = jax.random.split(key, 8)
        B, Nq, Nkv, Cq, Ckv = (4, 256, 256, 128, 96)
        s_q = 1.0 / np.sqrt(Cq)
        s_kv = 1.0 / np.sqrt(Ckv)
        return {'query': jax.random.normal(ks[0], (B, Nq, Cq), jnp.float32), 'key_value': jax.random.normal(ks[1], (B, Nkv, Ckv), jnp.float32), 'Wq': jax.random.normal(ks[2], (Cq, Cq), jnp.float32) * s_q, 'bq': jnp.zeros((Cq,), jnp.float32), 'Wk': jax.random.normal(ks[3], (Ckv, Cq), jnp.float32) * s_kv, 'bk': jnp.zeros((Cq,), jnp.float32), 'Wv': jax.random.normal(ks[4], (Ckv, Cq), jnp.float32) * s_kv, 'bv': jnp.zeros((Cq,), jnp.float32), 'Wo': jax.random.normal(ks[5], (Cq, Cq), jnp.float32) * s_q, 'bo': jnp.zeros((Cq,), jnp.float32)}
    _L1_xattn_all = _L1_xattn_setup()
    _L1_xattn_in = {k: v for k, v in _L1_xattn_all.items() if k in ('Wq', 'bq', 'Wk', 'bk', 'Wv', 'bv', 'Wo', 'bo')}
    del _L1_xattn_all

    def _L1_ffn_setup():
        import jax, jax.numpy as jnp
        import numpy as np
        CAPACITY_FACTOR = 0.5
        NUM_HEADS = 16
        key = jax.random.key(seed)
        ks = jax.random.split(key, 6)
        B, N, D = (4, 512, 128)
        s = 1.0 / np.sqrt(D)
        return {'token_inputs': jax.random.normal(ks[0], (B, N, D), jnp.float32), 'Wg': jax.random.normal(ks[1], (D, 1), jnp.float32) * s, 'Wq': jax.random.normal(ks[2], (D, D), jnp.float32) * s, 'Wk': jax.random.normal(ks[3], (D, D), jnp.float32) * s, 'Wv': jax.random.normal(ks[4], (D, D), jnp.float32) * s, 'Wo': jax.random.normal(ks[5], (D, D), jnp.float32) * s}
    _L1_ffn_all = _L1_ffn_setup()
    _L1_ffn_in = {k: v for k, v in _L1_ffn_all.items() if k in ('Wg', 'Wq', 'Wk', 'Wv', 'Wo')}
    del _L1_ffn_all

    def _L2_xattn_setup():
        import jax, jax.numpy as jnp
        import numpy as np
        IMAGE_DIM = 128
        TEXT_DIM = 96
        NUM_HEADS = 16
        HEAD_DIM = IMAGE_DIM // NUM_HEADS
        key = jax.random.key(seed)
        ks = jax.random.split(key, 14)
        B, N, M = (4, 512, 64)
        s_img = 1.0 / np.sqrt(IMAGE_DIM)
        s_txt = 1.0 / np.sqrt(TEXT_DIM)
        s_ff = 1.0 / np.sqrt(2 * IMAGE_DIM)
        return {'x': jax.random.normal(ks[0], (B, N, IMAGE_DIM), jnp.float32), 'y': jax.random.normal(ks[1], (B, M, TEXT_DIM), jnp.float32), 'Wq': jax.random.normal(ks[2], (IMAGE_DIM, IMAGE_DIM), jnp.float32) * s_img, 'bq': jax.random.normal(ks[3], (IMAGE_DIM,), jnp.float32) * s_img, 'Wk': jax.random.normal(ks[4], (TEXT_DIM, IMAGE_DIM), jnp.float32) * s_txt, 'bk': jax.random.normal(ks[5], (IMAGE_DIM,), jnp.float32) * s_txt, 'Wv': jax.random.normal(ks[6], (TEXT_DIM, IMAGE_DIM), jnp.float32) * s_txt, 'bv': jax.random.normal(ks[7], (IMAGE_DIM,), jnp.float32) * s_txt, 'W1': jax.random.normal(ks[8], (IMAGE_DIM, 2 * IMAGE_DIM), jnp.float32) * s_img, 'b1': jax.random.normal(ks[9], (2 * IMAGE_DIM,), jnp.float32) * s_img, 'W2': jax.random.normal(ks[10], (2 * IMAGE_DIM, IMAGE_DIM), jnp.float32) * s_ff, 'b2': jax.random.normal(ks[11], (IMAGE_DIM,), jnp.float32) * s_ff}
    _L2_xattn_all = _L2_xattn_setup()
    _L2_xattn_in = {k: v for k, v in _L2_xattn_all.items() if k in ('Wq', 'bq', 'Wk', 'bk', 'Wv', 'bv', 'W1', 'b1', 'W2', 'b2')}
    del _L2_xattn_all

    def _L2_ffn_setup():
        import jax, jax.numpy as jnp
        import numpy as np
        B, S, D_MODEL, D_HIDDEN = (4, 256, 128, 512)

        def act_quant(x):
            scale = 127.0 / jnp.clip(jnp.max(jnp.abs(x), axis=-1, keepdims=True), 1e-05)
            return jnp.clip(jnp.round(x * scale), -128, 127) / scale

        def weight_quant(w):
            scale = 1.0 / jnp.clip(jnp.mean(jnp.abs(w)), 1e-05)
            return jnp.clip(jnp.round(w * scale), -1, 1) / scale

        def bit_linear(x, w):
            xq = x + jax.lax.stop_gradient(act_quant(x) - x)
            wq = w + jax.lax.stop_gradient(weight_quant(w) - w)
            return jnp.einsum('bsd,hd->bsh', xq, wq)

        def depthwise_conv1d(x_bcl, w, b):
            y = jax.lax.conv_general_dilated(x_bcl, w, window_strides=(1,), padding=[(1, 1)], dimension_numbers=('NCH', 'OIH', 'NCH'), feature_group_count=x_bcl.shape[1])
            return y + b[None, :, None]
        key = jax.random.key(seed)
        ks = jax.random.split(key, 5)
        lim1 = 1.0 / np.sqrt(D_MODEL)
        lim2 = 1.0 / np.sqrt(D_HIDDEN)
        limc = 1.0 / np.sqrt(3.0)
        return {'x': jax.random.normal(ks[0], (B, S, D_MODEL), dtype=jnp.float32), 'w1': jax.random.uniform(ks[1], (D_HIDDEN, D_MODEL), jnp.float32, -lim1, lim1), 'conv_w': jax.random.uniform(ks[2], (D_HIDDEN, 1, 3), jnp.float32, -limc, limc), 'conv_b': jax.random.uniform(ks[3], (D_HIDDEN,), jnp.float32, -limc, limc), 'w2': jax.random.uniform(ks[4], (D_MODEL, D_HIDDEN), jnp.float32, -lim2, lim2)}
    _L2_ffn_all = _L2_ffn_setup()
    _L2_ffn_in = {k: v for k, v in _L2_ffn_all.items() if k in ('w1', 'conv_w', 'conv_b', 'w2')}
    del _L2_ffn_all

    def _L3_xattn_setup():
        import jax, jax.numpy as jnp
        import numpy as np
        DIM_IN, DIM_LAT, DIM_HEAD = (96, 128, 64)
        INNER = max(DIM_LAT, DIM_IN)
        HEADS = INNER // DIM_HEAD
        SCALE = DIM_HEAD ** (-0.5)
        RMS_EPS = 1e-08
        LN_EPS = 1e-05

        def layernorm(x, g, b):
            mu = jnp.mean(x, axis=-1, keepdims=True)
            var = jnp.mean((x - mu) ** 2, axis=-1, keepdims=True)
            return (x - mu) * jax.lax.rsqrt(var + LN_EPS) * g + b

        def rmsnorm(x, gamma):
            norm = jnp.sqrt(jnp.sum(x * x, axis=-1, keepdims=True)) * x.shape[-1] ** (-0.5)
            return x / jnp.maximum(norm, RMS_EPS) * gamma
        key = jax.random.key(seed)
        ks = jax.random.split(key, 12)
        b, n, m = (4, 512, 64)
        x = jax.random.normal(ks[0], (b, n, DIM_IN), jnp.float32)
        latents = jax.random.normal(ks[1], (b, m, DIM_LAT), jnp.float32)
        mask = jax.random.randint(ks[2], (b, n), 0, 2).astype(bool)
        s = lambda k, sh, fan: jax.random.normal(k, sh, jnp.float32) * fan ** (-0.5)
        return {'x': x, 'latents': latents, 'mask': mask, 'ln_x_g': jnp.ones((DIM_IN,), jnp.float32), 'ln_x_b': jnp.zeros((DIM_IN,), jnp.float32), 'ln_l_g': jnp.ones((DIM_LAT,), jnp.float32), 'ln_l_b': jnp.zeros((DIM_LAT,), jnp.float32), 'qn_g': jnp.ones((DIM_HEAD,), jnp.float32), 'kn_g': jnp.ones((DIM_HEAD,), jnp.float32), 'Wq': s(ks[3], (INNER, DIM_LAT), DIM_LAT), 'Wkv': s(ks[4], (2 * INNER, DIM_IN), DIM_IN), 'Wlkv': s(ks[5], (2 * INNER, DIM_LAT), DIM_LAT), 'Wo': s(ks[6], (DIM_LAT, INNER), INNER), 'bo': jnp.zeros((DIM_LAT,), jnp.float32)}
    _L3_xattn_all = _L3_xattn_setup()
    _L3_xattn_in = {k: v for k, v in _L3_xattn_all.items() if k in ('ln_x_g', 'ln_x_b', 'ln_l_g', 'ln_l_b', 'qn_g', 'kn_g', 'Wq', 'Wkv', 'Wlkv', 'Wo', 'bo')}
    del _L3_xattn_all

    def _L3_ffn_setup():
        import jax, jax.numpy as jnp
        import numpy as np
        B, S, D, E, H, K = (64, 256, 128, 32, 512, 8)
        key = jax.random.key(seed)
        k0, k1, k2, k3 = jax.random.split(key, 4)
        x = jax.random.normal(k0, (B, S, D), jnp.float32)
        gate_w = jax.random.normal(k1, (E, D), jnp.float32) * (1.0 / np.sqrt(D))
        gate_b = jnp.zeros((E,), jnp.float32)
        w1 = jax.random.normal(k2, (E, D + 1, H), jnp.float32) * (1.0 / np.sqrt(D + 1))
        w2 = jax.random.normal(k3, (E, H + 1, D), jnp.float32) * (1.0 / np.sqrt(H + 1))
        return {'x': x, 'gate_w': gate_w, 'gate_b': gate_b, 'w1': w1, 'w2': w2}
    _L3_ffn_all = _L3_ffn_setup()
    _L3_ffn_in = {k: v for k, v in _L3_ffn_all.items() if k in ('gate_w', 'gate_b', 'w1', 'w2')}
    del _L3_ffn_all
    return {'x': x, 'ctx_768': ctx_768, 'mask_BxS2_bk0': mask_BxS2_bk0, 'g_xattn': g_xattn, 'g_ffn': g_ffn, 'L0_xattn_Wq': _L0_xattn_in['Wq'], 'L0_xattn_Wk': _L0_xattn_in['Wk'], 'L0_xattn_Wv': _L0_xattn_in['Wv'], 'L0_xattn_Wo': _L0_xattn_in['Wo'], 'L0_xattn_bo': _L0_xattn_in['bo'], 'L0_ffn_gate_w': _L0_ffn_in['gate_w'], 'L0_ffn_gate_bias': _L0_ffn_in['gate_bias'], 'L0_ffn_w1': _L0_ffn_in['w1'], 'L0_ffn_w2': _L0_ffn_in['w2'], 'L0_ffn_w3': _L0_ffn_in['w3'], 'L0_ffn_ws1': _L0_ffn_in['ws1'], 'L0_ffn_ws2': _L0_ffn_in['ws2'], 'L0_ffn_ws3': _L0_ffn_in['ws3'], 'L1_xattn_Wq': _L1_xattn_in['Wq'], 'L1_xattn_bq': _L1_xattn_in['bq'], 'L1_xattn_Wk': _L1_xattn_in['Wk'], 'L1_xattn_bk': _L1_xattn_in['bk'], 'L1_xattn_Wv': _L1_xattn_in['Wv'], 'L1_xattn_bv': _L1_xattn_in['bv'], 'L1_xattn_Wo': _L1_xattn_in['Wo'], 'L1_xattn_bo': _L1_xattn_in['bo'], 'L1_ffn_Wg': _L1_ffn_in['Wg'], 'L1_ffn_Wq': _L1_ffn_in['Wq'], 'L1_ffn_Wk': _L1_ffn_in['Wk'], 'L1_ffn_Wv': _L1_ffn_in['Wv'], 'L1_ffn_Wo': _L1_ffn_in['Wo'], 'L2_xattn_Wq': _L2_xattn_in['Wq'], 'L2_xattn_bq': _L2_xattn_in['bq'], 'L2_xattn_Wk': _L2_xattn_in['Wk'], 'L2_xattn_bk': _L2_xattn_in['bk'], 'L2_xattn_Wv': _L2_xattn_in['Wv'], 'L2_xattn_bv': _L2_xattn_in['bv'], 'L2_xattn_W1': _L2_xattn_in['W1'], 'L2_xattn_b1': _L2_xattn_in['b1'], 'L2_xattn_W2': _L2_xattn_in['W2'], 'L2_xattn_b2': _L2_xattn_in['b2'], 'L2_ffn_w1': _L2_ffn_in['w1'], 'L2_ffn_conv_w': _L2_ffn_in['conv_w'], 'L2_ffn_conv_b': _L2_ffn_in['conv_b'], 'L2_ffn_w2': _L2_ffn_in['w2'], 'L3_xattn_ln_x_g': _L3_xattn_in['ln_x_g'], 'L3_xattn_ln_x_b': _L3_xattn_in['ln_x_b'], 'L3_xattn_ln_l_g': _L3_xattn_in['ln_l_g'], 'L3_xattn_ln_l_b': _L3_xattn_in['ln_l_b'], 'L3_xattn_qn_g': _L3_xattn_in['qn_g'], 'L3_xattn_kn_g': _L3_xattn_in['kn_g'], 'L3_xattn_Wq': _L3_xattn_in['Wq'], 'L3_xattn_Wkv': _L3_xattn_in['Wkv'], 'L3_xattn_Wlkv': _L3_xattn_in['Wlkv'], 'L3_xattn_Wo': _L3_xattn_in['Wo'], 'L3_xattn_bo': _L3_xattn_in['bo'], 'L3_ffn_gate_w': _L3_ffn_in['gate_w'], 'L3_ffn_gate_b': _L3_ffn_in['gate_b'], 'L3_ffn_w1': _L3_ffn_in['w1'], 'L3_ffn_w2': _L3_ffn_in['w2']}

def reference(x, ctx_768, mask_BxS2_bk0, g_xattn, g_ffn, L0_xattn_Wq, L0_xattn_Wk, L0_xattn_Wv, L0_xattn_Wo, L0_xattn_bo, L0_ffn_gate_w, L0_ffn_gate_bias, L0_ffn_w1, L0_ffn_w2, L0_ffn_w3, L0_ffn_ws1, L0_ffn_ws2, L0_ffn_ws3, L1_xattn_Wq, L1_xattn_bq, L1_xattn_Wk, L1_xattn_bk, L1_xattn_Wv, L1_xattn_bv, L1_xattn_Wo, L1_xattn_bo, L1_ffn_Wg, L1_ffn_Wq, L1_ffn_Wk, L1_ffn_Wv, L1_ffn_Wo, L2_xattn_Wq, L2_xattn_bq, L2_xattn_Wk, L2_xattn_bk, L2_xattn_Wv, L2_xattn_bv, L2_xattn_W1, L2_xattn_b1, L2_xattn_W2, L2_xattn_b2, L2_ffn_w1, L2_ffn_conv_w, L2_ffn_conv_b, L2_ffn_w2, L3_xattn_ln_x_g, L3_xattn_ln_x_b, L3_xattn_ln_l_g, L3_xattn_ln_l_b, L3_xattn_qn_g, L3_xattn_kn_g, L3_xattn_Wq, L3_xattn_Wkv, L3_xattn_Wlkv, L3_xattn_Wo, L3_xattn_bo, L3_ffn_gate_w, L3_ffn_gate_b, L3_ffn_w1, L3_ffn_w2):
    import jax
    import jax.numpy as jnp

    def _L0_xattn_ref(x, context, Wq, Wk, Wv, Wo, bo):
        import jax, jax.numpy as jnp
        import numpy as np
        HEADS = 8
        DIM_HEAD = 64
        SCALE = DIM_HEAD ** (-0.5)
        B, Nq, _ = x.shape
        q = (x @ Wq).reshape(B, Nq, HEADS, DIM_HEAD)
        k = (context @ Wk).reshape(B, context.shape[1], HEADS, DIM_HEAD)
        v = (context @ Wv).reshape(B, context.shape[1], HEADS, DIM_HEAD)
        sim = jnp.einsum('bihd,bjhd->bhij', q, k) * SCALE
        attn = jax.nn.softmax(sim, axis=-1)
        out = jnp.einsum('bhij,bjhd->bihd', attn, v)
        out = out.reshape(B, Nq, HEADS * DIM_HEAD)
        return out @ Wo + bo

    def _L0_ffn_ref(x, gate_w, gate_bias, w1, w2, w3, ws1, ws2, ws3):
        import jax, jax.numpy as jnp
        import numpy as np
        DIM = 128
        INTER = 64
        E = 16
        TOPK = 4
        N_GROUPS = 4
        TOPK_GROUPS = 2
        ROUTE_SCALE = 1.0
        INIT_STD = 0.02
        B, S = (2, 128)
        Bx, Sx, D = x.shape
        T = Bx * Sx
        xf = x.reshape(T, D)
        scores = jax.nn.sigmoid(xf @ gate_w.T)
        original_scores = scores
        s = scores + gate_bias
        sg = s.reshape(T, N_GROUPS, E // N_GROUPS)
        group_scores = sg.max(axis=-1)
        _, gidx = jax.lax.top_k(group_scores, TOPK_GROUPS)
        keep = jnp.zeros((T, N_GROUPS), bool).at[jnp.arange(T)[:, None], gidx].set(True)
        s_masked = jnp.where(keep[:, :, None], sg, -jnp.inf).reshape(T, E)
        _, idx = jax.lax.top_k(s_masked, TOPK)
        weights = jnp.take_along_axis(original_scores, idx, axis=1) * ROUTE_SCALE
        comb = jnp.zeros((T, E), x.dtype).at[jnp.arange(T)[:, None], idx].add(weights)
        h1 = jnp.einsum('td,eid->tei', xf, w1)
        h3 = jnp.einsum('td,eid->tei', xf, w3)
        h = jax.nn.silu(h1) * h3
        y = jnp.einsum('tei,edi,te->td', h, w2, comb)
        z = jax.nn.silu(xf @ ws1.T) * (xf @ ws3.T) @ ws2.T
        return (y + z).reshape(Bx, Sx, D)

    def _L1_xattn_ref(query, key_value, Wq, bq, Wk, bk, Wv, bv, Wo, bo):
        import jax, jax.numpy as jnp
        import numpy as np
        NUM_HEADS = 16
        CLAMP = 10000.0
        B, Nq, Cq = query.shape
        Nkv = key_value.shape[1]
        H = NUM_HEADS
        D = Cq // H
        scale = D ** (-0.5)
        q = (query @ Wq + bq).reshape(B, Nq, H, D).transpose(0, 2, 1, 3)
        k = (key_value @ Wk + bk).reshape(B, Nkv, H, D).transpose(0, 2, 1, 3)
        v = (key_value @ Wv + bv).reshape(B, Nkv, H, D).transpose(0, 2, 1, 3)
        attn = jnp.einsum('bhqd,bhkd->bhqk', q, k) * scale
        attn = jnp.clip(attn, -CLAMP, CLAMP)
        attn = jax.nn.softmax(attn, axis=-1)
        attn = jnp.where(jnp.any(jnp.isnan(attn)), jnp.asarray(1.0 / Nkv, attn.dtype), attn)
        x = jnp.einsum('bhqk,bhkd->bqhd', attn, v).reshape(B, Nq, Cq)
        return x @ Wo + bo

    def _L1_ffn_ref(token_inputs, Wg, Wq, Wk, Wv, Wo):
        import jax, jax.numpy as jnp
        import numpy as np
        CAPACITY_FACTOR = 0.5
        NUM_HEADS = 16
        B, N, D = token_inputs.shape
        C = int(N * CAPACITY_FACTOR)
        H = NUM_HEADS
        dh = D // H
        gate = jax.nn.sigmoid((token_inputs @ Wg)[..., 0])
        _, idx = jax.lax.top_k(gate, C)
        attn_in = jnp.take_along_axis(token_inputs, idx[..., None], axis=1)
        q = (attn_in @ Wq).reshape(B, C, H, dh)
        k = (attn_in @ Wk).reshape(B, C, H, dh)
        v = (attn_in @ Wv).reshape(B, C, H, dh)
        scores = jnp.einsum('bqhd,bkhd->bhqk', q, k) / jnp.sqrt(jnp.float32(dh))
        attn = jax.nn.softmax(scores, axis=-1)
        o = jnp.einsum('bhqk,bkhd->bqhd', attn, v).reshape(B, C, D) @ Wo
        gate_sel = jnp.take_along_axis(gate, idx, axis=1)
        out = jnp.zeros_like(token_inputs)
        out = out.at[jnp.arange(B)[:, None], idx].set(o * gate_sel[..., None])
        return out

    def _L2_xattn_ref(x, y, Wq, bq, Wk, bk, Wv, bv, W1, b1, W2, b2):
        import jax, jax.numpy as jnp
        import numpy as np
        IMAGE_DIM = 128
        TEXT_DIM = 96
        NUM_HEADS = 16
        HEAD_DIM = IMAGE_DIM // NUM_HEADS
        B, N, _ = x.shape
        M = y.shape[1]
        q = (x @ Wq + bq).reshape(B, N, NUM_HEADS, HEAD_DIM)
        k = (y @ Wk + bk).reshape(B, M, NUM_HEADS, HEAD_DIM)
        v = (y @ Wv + bv).reshape(B, M, NUM_HEADS, HEAD_DIM)
        scale = 1.0 / np.sqrt(HEAD_DIM)
        scores = jnp.einsum('bnhd,bmhd->bhnm', q, k) * scale
        attn = jax.nn.softmax(scores, axis=-1)
        out = jnp.einsum('bhnm,bmhd->bnhd', attn, v).reshape(B, N, IMAGE_DIM)
        h = jax.nn.relu(out @ W1 + b1)
        return h @ W2 + b2

    def _L2_ffn_ref(x, w1, conv_w, conv_b, w2):
        import jax, jax.numpy as jnp
        import numpy as np
        B, S, D_MODEL, D_HIDDEN = (4, 256, 128, 512)

        def act_quant(x):
            scale = 127.0 / jnp.clip(jnp.max(jnp.abs(x), axis=-1, keepdims=True), 1e-05)
            return jnp.clip(jnp.round(x * scale), -128, 127) / scale

        def weight_quant(w):
            scale = 1.0 / jnp.clip(jnp.mean(jnp.abs(w)), 1e-05)
            return jnp.clip(jnp.round(w * scale), -1, 1) / scale

        def bit_linear(x, w):
            xq = x + jax.lax.stop_gradient(act_quant(x) - x)
            wq = w + jax.lax.stop_gradient(weight_quant(w) - w)
            return jnp.einsum('bsd,hd->bsh', xq, wq)

        def depthwise_conv1d(x_bcl, w, b):
            y = jax.lax.conv_general_dilated(x_bcl, w, window_strides=(1,), padding=[(1, 1)], dimension_numbers=('NCH', 'OIH', 'NCH'), feature_group_count=x_bcl.shape[1])
            return y + b[None, :, None]
        h = bit_linear(x, w1)
        h = depthwise_conv1d(h.transpose(0, 2, 1), conv_w, conv_b)
        h = h.transpose(0, 2, 1)
        h = jax.nn.silu(h)
        return bit_linear(h, w2)

    def _L3_xattn_ref(x, latents, mask, ln_x_g, ln_x_b, ln_l_g, ln_l_b, qn_g, kn_g, Wq, Wkv, Wlkv, Wo, bo):
        import jax, jax.numpy as jnp
        import numpy as np
        DIM_IN, DIM_LAT, DIM_HEAD = (96, 128, 64)
        INNER = max(DIM_LAT, DIM_IN)
        HEADS = INNER // DIM_HEAD
        SCALE = DIM_HEAD ** (-0.5)
        RMS_EPS = 1e-08
        LN_EPS = 1e-05

        def layernorm(x, g, b):
            mu = jnp.mean(x, axis=-1, keepdims=True)
            var = jnp.mean((x - mu) ** 2, axis=-1, keepdims=True)
            return (x - mu) * jax.lax.rsqrt(var + LN_EPS) * g + b

        def rmsnorm(x, gamma):
            norm = jnp.sqrt(jnp.sum(x * x, axis=-1, keepdims=True)) * x.shape[-1] ** (-0.5)
            return x / jnp.maximum(norm, RMS_EPS) * gamma
        b, n, _ = x.shape
        m = latents.shape[1]
        xn = layernorm(x, ln_x_g, ln_x_b)
        ln = layernorm(latents, ln_l_g, ln_l_b)
        q = ln @ Wq.T
        kv = jnp.concatenate([xn @ Wkv.T, ln @ Wlkv.T], axis=1)
        k, v = (kv[..., :INNER], kv[..., INNER:])
        split_heads = lambda t: t.reshape(t.shape[0], t.shape[1], HEADS, DIM_HEAD).transpose(0, 2, 1, 3)
        q, k, v = (split_heads(q), split_heads(k), split_heads(v))
        qn = rmsnorm(q, qn_g) * SCALE
        kn = rmsnorm(k, kn_g)
        attn = jnp.einsum('bhid,bhjd->bhij', qn, kn)
        full_mask = jnp.pad(mask, ((0, 0), (0, m)), constant_values=True)
        attn = jnp.where(full_mask[:, None, None, :], attn, -jnp.finfo(attn.dtype).max)
        attn = jax.nn.softmax(attn, axis=-1)
        out = jnp.einsum('bhij,bhjd->bhid', attn, v)
        out = out.transpose(0, 2, 1, 3).reshape(b, m, INNER)
        return out @ Wo.T + bo

    def _L3_ffn_ref(x, gate_w, gate_b, w1, w2):
        import jax, jax.numpy as jnp
        import numpy as np
        B, S, D, E, H, K = (64, 256, 128, 32, 512, 8)
        b, s, d = x.shape
        logits = jnp.einsum('bsd,ed->bse', x, gate_w) + gate_b
        probs = jax.nn.softmax(logits, axis=-2)
        vals_t, idx_t = jax.lax.top_k(probs.transpose(0, 2, 1), K)
        vals = vals_t.transpose(0, 2, 1)
        idx = idx_t.transpose(0, 2, 1)
        flat_idx = idx.reshape(b, K * E)
        tok = jnp.take_along_axis(x, flat_idx[:, :, None], axis=1)
        tok = tok.reshape(b, K, E, d)
        merged = jnp.einsum('bked,bke->bed', tok, vals)
        ones = jnp.ones(merged.shape[:-1] + (1,), merged.dtype)
        h = jnp.einsum('bei,eih->beh', jnp.concatenate([merged, ones], -1), w1)
        h = jax.nn.gelu(h, approximate=False)
        o = jnp.einsum('bej,ejo->beo', jnp.concatenate([h, ones], -1), w2)
        out_tok = jnp.einsum('beo,bke->bkeo', o, vals).reshape(b, K * E, d)
        out = jnp.zeros_like(x).at[jnp.arange(b)[:, None], flat_idx].add(out_tok)
        return out
    x = x + jnp.tanh(g_xattn[0]) * _L0_xattn_ref(_layernorm(x, axis=-1), ctx_768, L0_xattn_Wq, L0_xattn_Wk, L0_xattn_Wv, L0_xattn_Wo, L0_xattn_bo)
    x = x + jnp.tanh(g_ffn[0]) * _L0_ffn_ref(_layernorm(x, axis=-1), L0_ffn_gate_w, L0_ffn_gate_bias, L0_ffn_w1, L0_ffn_w2, L0_ffn_w3, L0_ffn_ws1, L0_ffn_ws2, L0_ffn_ws3)
    x = x + jnp.tanh(g_xattn[1]) * _L1_xattn_ref(_layernorm(x, axis=-1), ctx_768, L1_xattn_Wq, L1_xattn_bq, L1_xattn_Wk, L1_xattn_bk, L1_xattn_Wv, L1_xattn_bv, L1_xattn_Wo, L1_xattn_bo)
    x = x + jnp.tanh(g_ffn[1]) * _L1_ffn_ref(_layernorm(x, axis=-1), L1_ffn_Wg, L1_ffn_Wq, L1_ffn_Wk, L1_ffn_Wv, L1_ffn_Wo)
    x = x + jnp.tanh(g_xattn[2]) * _L2_xattn_ref(_layernorm(x, axis=-1), ctx_768, L2_xattn_Wq, L2_xattn_bq, L2_xattn_Wk, L2_xattn_bk, L2_xattn_Wv, L2_xattn_bv, L2_xattn_W1, L2_xattn_b1, L2_xattn_W2, L2_xattn_b2)
    x = x + jnp.tanh(g_ffn[2]) * _L2_ffn_ref(_layernorm(x, axis=-1), L2_ffn_w1, L2_ffn_conv_w, L2_ffn_conv_b, L2_ffn_w2)
    x = x + jnp.tanh(g_xattn[3]) * _L3_xattn_ref(ctx_768, _layernorm(x, axis=-1), mask_BxS2_bk0, L3_xattn_ln_x_g, L3_xattn_ln_x_b, L3_xattn_ln_l_g, L3_xattn_ln_l_b, L3_xattn_qn_g, L3_xattn_kn_g, L3_xattn_Wq, L3_xattn_Wkv, L3_xattn_Wlkv, L3_xattn_Wo, L3_xattn_bo)
    x = x + jnp.tanh(g_ffn[3]) * _L3_ffn_ref(_layernorm(x, axis=-1), L3_ffn_gate_w, L3_ffn_gate_b, L3_ffn_w1, L3_ffn_w2)
    return x

_drawn_inputs = setup_inputs


def setup_inputs(seed=0):
    import zlib

    import numpy as np

    out = dict(_drawn_inputs(seed))
    spreads = {'L0_ffn_gate_bias': (0.0, 0.8),
     'L1_xattn_bq': (0.0, 0.349),
     'L1_xattn_bk': (0.0, 2.0),
     'L1_xattn_bv': (0.0, 0.1),
     'L1_xattn_bo': (0.0, 0.1),
     'L3_xattn_ln_x_g': (1.0, 0.543),
     'L3_xattn_ln_x_b': (0.0, 0.35),
     'L3_xattn_ln_l_g': (1.0, 0.2),
     'L3_xattn_ln_l_b': (0.0, 0.347),
     'L3_xattn_qn_g': (1.0, 0.6),
     'L3_xattn_kn_g': (1.0, 0.6),
     'L3_xattn_bo': (0.0, 0.1),
     'L3_ffn_gate_b': (0.0, 2.0)}
    factors = {'g_ffn': 7.232,
     'L0_xattn_bo': 7.989,
     'L0_ffn_gate_w': 5.792,
     'L0_ffn_w1': 6.793,
     'L0_ffn_w2': 5.73,
     'L0_ffn_w3': 5.757,
     'L0_ffn_ws1': 6.554,
     'L0_ffn_ws2': 4.86,
     'L0_ffn_ws3': 5.271,
     'L2_xattn_bq': 6.067,
     'L2_xattn_bk': 64.0,
     'L3_ffn_gate_w': 8.0,
     'L3_ffn_w1': 6.488,
     'L3_ffn_w2': 6.054}
    for name, (base, spread) in spreads.items():
        noise = np.random.default_rng([zlib.crc32(name.encode()), seed]).standard_normal(out[name].shape)
        drawn = base * np.exp(spread * noise) if base else spread * noise
        out[name] = jnp.asarray(drawn.astype(out[name].dtype))
    for name, factor in factors.items():
        out[name] = (out[name] * factor).astype(out[name].dtype)
    return out
```

```python
from collections import namedtuple
from contextlib import ExitStack

import numpy as np

import concourse.bass as bass
from concourse import mybir

ALU = mybir.AluOpType
ACT = mybir.ActivationFunctionType
F32 = mybir.dt.float32
BF16 = mybir.dt.bfloat16
U8 = mybir.dt.uint8
AX = mybir.AxisListType

B, S, D = 8, 256, 128
SC, DC = 1601, 96
NT = B * S // 128
TPB = S // 128
KT = -(-SC // 128)
KL = SC - (KT - 1) * 128
EPS = 1e-5
CHUNKS = [(0, 401), (401, 400), (801, 400), (1201, 400)]
GROUPS = [(0, 4), (4, 4), (8, 4), (12, 1)]


def key_rows(j):
    return KL if j == KT - 1 else 128


class Link:

    def __init__(self, eng, sem):
        self.eng, self.sem, self.base, self.n = eng, sem, 0, 0

    def __call__(self, ins):
        ins.then_inc(self.sem, 1)
        self.n += 1
        self.eng.wait_ge(self.sem, self.base + self.n)

    def enter(self, i, per):
        self.outer = (self.base, self.n)
        self.base, self.n, self.per = self.base + self.n + i * per, 0, per

    def leave(self, rounds):
        assert self.n == self.per, (self.n, self.per)
        base, n = self.outer
        self.base, self.n = base, n + rounds * self.per


class Chip:
    pass


NAMES = {}
USED = []


def uniq(name):
    NAMES[name] = NAMES.get(name, 0) + 1
    return name if NAMES[name] == 1 else f"{name}_{NAMES[name]}"


def sems(ctx, nc, names):
    names = names.split()
    made = [nc.alloc_semaphore(name=uniq(name)) for name in names]
    USED.extend(made)
    return namedtuple("Semaphores", names)(*made)


def clear_semaphores(nc):
    nc.clear_and_free_semaphores(list(USED))
    nc.all_engine_barrier()
    USED.clear()


def bcast(ap, shape):
    return ap.unsqueeze(len(ap.shape)).to_broadcast(shape)


def start(nc, c, d):
    with ExitStack() as ctx:
        s = sems(ctx, nc, "st_x st_gates st_zero st_ident st_negh")
        graw = ctx.enter_context(nc.sbuf_tensor(uniq("graw"), [128, 8], F32))
        block = ctx.enter_context(nc.Block())

        @block.sync
        def _(sp):
            sp.dma_start(c.x_res[:], d["x_tok"]).then_inc(s.st_x, 16)
            sp.dma_start(graw[:], d["gates"].partition_broadcast(128)).then_inc(s.st_gates, 16)
            sp.wait_ge(s.st_x, 16)

        @block.gpsimd
        def _(pool):
            nc.gpsimd.memset(c.ident[:], 0.0).then_inc(s.st_zero, 1)
            nc.gpsimd.memset(c.neg_half[:], -0.5)
            pool.wait_ge(s.st_zero, 1)
            nc.gpsimd.affine_select(out=c.ident[:], in_=c.ident[:], compare_op=ALU.not_equal, fill=1.0,
                                    base=0, pattern=[[-1, 128]], channel_multiplier=1).then_inc(s.st_ident, 1)

        @block.vector
        def _(dve):
            nc.vector.memset(c.ones_row[:], 1.0)
            dve.wait_ge(s.st_ident, 1)
            nc.vector.tensor_copy(c.ident_b[:], c.ident[:])
            nc.vector.reduce_sum(c.strip_sum[:], c.ident[:].rearrange("p (y n) -> p n y", y=4), AX.X)

        @block.scalar
        def _(act):
            act.wait_ge(s.st_gates, 16)
            nc.scalar.activation(c.tanh_g[:], graw[:], ACT.Tanh)


def finish(nc, c, d):
    with ExitStack() as ctx:
        s = sems(ctx, nc, "fin_out")
        block = ctx.enter_context(nc.Block())

        @block.sync
        def _(sp):
            sp.dma_start(d["out"], c.x_res[:]).then_inc(s.fin_out, 16)
            sp.wait_ge(s.fin_out, 16)


def layer_norm(nc, c, src, dst, dstT, gain=None, shift=None):
    with ExitStack() as ctx:
        s = sems(ctx, nc, "ln_link ln_var ln_rstd ln_xn ln_turned ln_copied")
        stat = ctx.enter_context(nc.sbuf_tensor(uniq("ln_stat"), [128, 4, NT], F32))
        turned = ctx.enter_context(nc.psum_tensor(uniq("ln_ps"), [128, 4, 512], F32))
        block = ctx.enter_context(nc.Block())
        shape = [128, NT, D]

        @block.vector
        def _(dve):
            link = Link(dve, s.ln_link)
            link(nc.vector.reduce_sum(stat[:, 0, :], src[:], AX.X))
            link(nc.vector.tensor_scalar(stat[:, 0, :], stat[:, 0, :], 1.0 / D, None, ALU.mult))
            link(nc.vector.tensor_tensor(dst[:], src[:], bcast(stat[:, 0, :], shape), ALU.subtract))
            link(nc.vector.tensor_tensor(c.scratch[:], dst[:], dst[:], ALU.mult))
            link(nc.vector.reduce_sum(stat[:, 1, :], c.scratch[:], AX.X))
            nc.vector.tensor_scalar(stat[:, 2, :], stat[:, 1, :], 1.0 / D, EPS, ALU.mult,
                                    ALU.add).then_inc(s.ln_var, 1)
            dve.wait_ge(s.ln_rstd, 1)
            for k in range(4):
                t = slice(4 * k, 4 * k + 4)
                ins = nc.vector.tensor_tensor(dst[:, t, :], dst[:, t, :],
                                              bcast(stat[:, 3, t], [128, 4, D]), ALU.mult)
                if gain is not None:
                    link(ins)
                    link(nc.vector.tensor_tensor(dst[:, t, :], dst[:, t, :],
                                                 gain.unsqueeze(1).to_broadcast([128, 4, D]), ALU.mult))
                    ins = nc.vector.tensor_tensor(dst[:, t, :], dst[:, t, :],
                                                  shift.unsqueeze(1).to_broadcast([128, 4, D]), ALU.add)
                ins.then_inc(s.ln_xn, 1)

        @block.gpsimd
        def _(pool):
            pool.wait_ge(s.ln_var, 1)
            nc.gpsimd.tensor_tensor(stat[:, 3, :], stat[:, 2, :], c.neg_half[:, 0:NT],
                                    ALU.pow).then_inc(s.ln_rstd, 1)

        @block.tensor
        def _(pe):
            for k in range(4):
                pe.wait_ge(s.ln_xn, k + 1)
                for j in range(4):
                    ins = nc.tensor.transpose(turned[:, k, 128 * j:128 * j + 128], dst[:, 4 * k + j, :],
                                              c.ident[:])
                ins.then_inc(s.ln_turned, 1)

        @block.scalar
        def _(act):
            for k in range(4):
                act.wait_ge(s.ln_turned, k + 1)
                nc.scalar.copy(dstT[:, 512 * k:512 * k + 512], turned[:, k, :])


H0, DH0 = 8, 64


def l0_attention(nc, c, d):
    SCALE = DH0 ** -0.5
    with ExitStack() as ctx:
        def sb(name, shape, dt=F32):
            return ctx.enter_context(nc.sbuf_tensor(uniq(name), shape, dt))
        qp = sb("l0_qp", [DC + 1, B, H0, S])
        qpb = sb("l0_qpb", [DC, B, H0, S], BF16)
        w_vo = sb("l0_wvo", [DC + 1, H0, D + 1])
        bo = sb("l0_bo", [1, D])
        with ExitStack() as cx:
            _l0_project(nc, c, d, qp, qpb, w_vo, bo, cx)
        with ExitStack() as cx:
            _l0_core(nc, c, d, qp, qpb, cx, SCALE)
        with ExitStack() as cx:
            heads_out(nc, c, qp, w_vo, bo, cx, DC, H0, 0)


def _l0_project(nc, c, d, qp, qpb, w_vo, bo, ctx):
    s = sems(ctx, nc, "l0_w l0_wps l0_wcopied l0_qps l0_qcopied")
    wT = ctx.enter_context(nc.sbuf_tensor(uniq("l0_wT"), [DH0, H0, 4, 128], F32))
    w_qk = ctx.enter_context(nc.sbuf_tensor(uniq("l0_wqk"), [D, H0, DC], F32))
    pw = ctx.enter_context(nc.psum_tensor(uniq("l0_pw"), [128, 4, 512], F32))
    pq = ctx.enter_context(nc.psum_tensor(uniq("l0_pq"), [128, 4, 512], F32))
    block = ctx.enter_context(nc.Block())

    @block.sync
    def _(sp):
        sp.dma_start(wT[:], d["l0_wT"]).then_inc(s.l0_w, 16)
        sp.dma_start(bo[:], d["l0_bo"]).then_inc(s.l0_w, 16)
        sp.wait_ge(s.l0_w, 32)

    @block.tensor
    def _(pe):
        pe.wait_ge(s.l0_w, 32)
        for h in range(H0):
            nc.tensor.matmul(pw[:, h // 4, 128 * (h % 4):128 * (h % 4) + DC], wT[:, h, 0, :],
                             wT[:, h, 1, 0:DC], start=True, stop=True)
            ins = nc.tensor.matmul(pw[0:DC, 2 + h // 4, 128 * (h % 4):128 * (h % 4) + 128], wT[:, h, 2, 0:DC],
                                   wT[:, h, 3, :], start=True, stop=True)
        ins.then_inc(s.l0_wps, 1)
        pe.wait_ge(s.l0_wcopied, 1)
        for n in range(4 * H0):
            h, k = n // 4, n % 4
            if n >= 4:
                pe.wait_ge(s.l0_qcopied, n - 3)
            nc.tensor.matmul(pq[0:DC, n % 4, :], w_qk[:, h, :], c.xnT[:, 512 * k:512 * k + 512],
                             start=True, stop=True).then_inc(s.l0_qps, 1)

    @block.scalar
    def _(act):
        act.wait_ge(s.l0_wps, 1)
        for g in range(2):
            nc.scalar.copy(w_vo[0:DC, 4 * g:4 * g + 4, 0:D],
                           pw[0:DC, 2 + g, :].rearrange("p (h n) -> p h n", h=4))
        for n in range(4 * H0):
            h, k = n // 4, n % 4
            act.wait_ge(s.l0_qps, n + 1)
            nc.scalar.copy(qp[0:DC, 2 * k:2 * k + 2, h, :],
                           pq[0:DC, n % 4, :].rearrange("p (b t) -> p b t", b=2)).then_inc(s.l0_qcopied, 1)

    @block.vector
    def _(dve):
        dve.wait_ge(s.l0_wps, 1)
        for g in range(2):
            ins = nc.vector.tensor_copy(w_qk[:, 4 * g:4 * g + 4, :],
                                        pw[:, g, :].rearrange("p (h n) -> p h n", h=4)[:, :, 0:DC])
        ins.then_inc(s.l0_wcopied, 1)

    @block.gpsimd
    def _(pool):
        nc.gpsimd.memset(w_vo[0:DC, :, D:D + 1], 0.0)
        nc.gpsimd.memset(w_vo[DC:DC + 1, :, 0:D], 0.0)
        nc.gpsimd.memset(w_vo[DC:DC + 1, :, D:D + 1], 1.0)
        for h in range(H0):
            pool.wait_ge(s.l0_qcopied, 4 * h + 4)
            nc.gpsimd.tensor_copy(qpb[:, :, h, :], qp[0:DC, :, h, :])


class At:
    def __init__(self, cfg, p, i, h):
        self.p, self.i, self.h = p, i, h
        self.b = cfg.parities * i + p
        self.n = self.b * cfg.heads + h


class Core:

    def __init__(self, nc, ctx, c, cfg):
        self.nc, self.cfg, self.c = nc, cfg, c
        self.s = sems(ctx, nc, "max_made max_read max_found max_turned shift_ready "
                               "scores_made exp_done values_used heads_out")
        self.NCH, self.NG = len(cfg.chunks), len(cfg.groups)
        dt = cfg.row_dt
        self.max_cols = ctx.enter_context(nc.sbuf_tensor(uniq("max_cols"), [128, TPB, self.NCH], F32))
        self.neg_max = ctx.enter_context(nc.sbuf_tensor(uniq("neg_max"), [128, TPB], F32))
        self.shift_cols = ctx.enter_context(nc.sbuf_tensor(uniq("shift_cols"), [128, TPB, cfg.row + cfg.rows], dt))
        self.probs = ctx.enter_context(nc.sbuf_tensor(uniq("probs"), [128, 2, 4 * S], F32))
        self.ps_max = ctx.enter_context(nc.psum_tensor(uniq("ps_max"), [128, 2, 512], F32))
        self.ps_scores = ctx.enter_context(nc.psum_tensor(uniq("ps_scores"), [128, 2, 4 * S], F32))
        self.ps_out = ctx.enter_context(nc.psum_tensor(uniq("ps_out"), [128, 512], F32))
        self.ps_turn = ctx.enter_context(nc.psum_tensor(uniq("ps_turn"), [128, 2, 256], F32))
        turn = self.ps_turn[:, 0, :]
        if dt != F32:
            turn = turn.bitcast(dt)[:, 0:TPB * 128]
        self.shift_turn = turn.rearrange("p (t q) -> p t q", t=TPB)

    def begin_dve(self, dve):
        dve.sem_inc(self.s.max_read, 2)

    def begin_act(self, act):
        act.sem_inc(self.s.exp_done, 2)

    def begin_pe(self, pe):
        pe.sem_inc(self.s.values_used, 2)
        pe.sem_inc(self.cfg.out_copied, 1)

    def pe_max(self, pe, at, which):
        s, n = self.s, 2 * self.NCH
        for k in which:
            t, chunk = k // self.NCH, k % self.NCH
            k0, size = self.cfg.chunks[chunk]
            pe.wait_ge(s.max_read, at.n * n + k + 1)
            self.nc.tensor.matmul(self.ps_max[:, k % 2, 0:size], self.cfg.max_q(at, t),
                                  self.cfg.max_k(at, k0, size), start=True, stop=True).then_inc(s.max_made, 1)

    def pe_turn(self, pe, at):
        cfg, s = self.cfg, self.s
        pe.wait_ge(s.max_found, at.n + 1)
        ident = self.c.ident if cfg.row_dt == F32 else self.c.ident_b
        for t in range(TPB):
            ins = self.nc.tensor.transpose(self.shift_turn[0:cfg.row + cfg.rows, t, :],
                                           self.shift_cols[:, t, :], ident[:])
        ins.then_inc(s.max_turned, 1)

    def pe_scores(self, pe, at, g):
        cfg, s = self.cfg, self.s
        if g == 0:
            pe.wait_ge(s.shift_ready, at.n + 1)
        pe.wait_ge(s.exp_done, at.n * self.NG + g + 1)
        j0, nj = cfg.groups[g]
        for j in range(j0, j0 + nj):
            ins = self.nc.tensor.matmul(self.ps_scores[0:cfg.keys(j), self.buf(at, g), (j - j0) * S:(j - j0 + 1) * S],
                                        cfg.score_k(at, j), cfg.score_q(at), start=True, stop=True)
        ins.then_inc(s.scores_made, 1)

    def pe_values(self, pe, at, g):
        cfg, s = self.cfg, self.s
        pe.wait_ge(s.exp_done, at.n * self.NG + g + 3)
        if g == 0:
            pe.wait_ge(cfg.out_copied, at.n + 1)
        j0, nj = cfg.groups[g]
        last = cfg.groups[-1][0] + cfg.groups[-1][1] - 1
        for j in range(j0, j0 + nj):
            ins = self.nc.tensor.matmul(cfg.out(at, j), cfg.value(at, j),
                                        self.probs[0:cfg.keys(j), self.buf(at, g), (j - j0) * S:(j - j0 + 1) * S],
                                        start=(j < cfg.strips), stop=(j + cfg.strips > last), skip_group_check=True)
        ins.then_inc(s.values_used, 1)

    def buf(self, at, g):
        return g % 2 if self.NG % 2 == 0 else (at.p * self.cfg.heads + at.h + g) % 2

    def pe_step(self, pe, at, nxt):
        total = 2 * self.NCH
        slots = max(1, self.NG - 1)
        for g in range(self.NG):
            self.pe_scores(pe, at, g)
            if nxt is not None and g < slots:
                self.pe_max(pe, nxt, range(total * g // slots, total * (g + 1) // slots))
            if g >= 1:
                self.pe_values(pe, at, g - 1)
        if nxt is not None:
            self.pe_turn(pe, nxt)
        self.pe_values(pe, at, self.NG - 1)

    def dve_max(self, dve, at, link):
        cfg, s, nc = self.cfg, self.s, self.nc
        n = 2 * self.NCH
        for k in range(n):
            t, chunk = k // self.NCH, k % self.NCH
            dve.wait_ge(s.max_made, at.n * n + k + 1)
            nc.vector.reduce_max(self.max_cols[:, t, chunk:chunk + 1], self.ps_max[:, k % 2, 0:cfg.chunks[chunk][1]],
                                 AX.X).then_inc(s.max_read, 1)
        dve.wait_ge(s.max_read, at.n * n + n + 2)
        if cfg.rows == 1:
            nc.vector.tensor_reduce(self.shift_cols[:, :, cfg.row], self.max_cols[:], axis=AX.X, op=ALU.max,
                                    negate=True).then_inc(s.max_found, 1)
        else:
            link(nc.vector.tensor_reduce(self.neg_max[:], self.max_cols[:], axis=AX.X, op=ALU.max, negate=True))
            link(nc.vector.tensor_copy(self.shift_cols[:, :, cfg.row], self.neg_max[:]))
            nc.vector.tensor_tensor(self.shift_cols[:, :, cfg.row + 1], self.neg_max[:],
                                    self.shift_cols[:, :, cfg.row], ALU.subtract).then_inc(s.max_found, 1)
        dve.wait_ge(s.max_turned, at.n + 1)
        nc.vector.tensor_copy(cfg.shift_rows(at), self.shift_turn[cfg.row:cfg.row + cfg.rows, :, :]
                              .rearrange("p t q -> p (t q)")).then_inc(s.shift_ready, 1)

    def act_exp(self, act, at, groups=None):
        cfg, s = self.cfg, self.s
        for g in (range(self.NG) if groups is None else groups):
            j0, nj = cfg.groups[g]
            rows = cfg.keys(j0)
            act.wait_ge(s.scores_made, at.n * self.NG + g + 1)
            act.wait_ge(s.values_used, at.n * self.NG + g + 1)
            self.nc.scalar.activation(self.probs[0:rows, self.buf(at, g), 0:nj * S],
                                      self.ps_scores[0:rows, self.buf(at, g), 0:nj * S], ACT.Exp,
                                      scale=cfg.scale).then_inc(s.exp_done, 1)

    def heads(self, eng, p, i, first, step):
        cfg, H = self.cfg, self.cfg.heads
        if first is not None:
            first(At(cfg, p, i, 0))
        step(At(cfg, p, i, 0), At(cfg, p, i, 1), True)
        if cfg.loop:
            with eng.Fori(1, H - 1) as h:
                step(At(cfg, p, i, h), At(cfg, p, i, h + 1), False)
        else:
            for h in range(1, H - 1):
                step(At(cfg, p, i, h), At(cfg, p, i, h + 1), False)
        step(At(cfg, p, i, H - 1), None, False)


class Cfg:
    parities = 2


def _l0_core(nc, c, d, qp, qpb, ctx, scale):
    s = sems(ctx, nc, "l0_ctx0 l0_ctx1 l0_ctxb l0_batch l0_link l0_out l0_zero")
    loaded = [s.l0_ctx0, s.l0_ctx1]
    ctxT = [ctx.enter_context(nc.sbuf_tensor(uniq(f"l0_ctxT{p}"), [DC + 1, SC], F32)) for p in range(2)]
    ctxk = [ctx.enter_context(nc.sbuf_tensor(uniq(f"l0_ctxk{p}"), [128, KT, DC + 1], F32)) for p in range(2)]
    ctxb = [ctx.enter_context(nc.sbuf_tensor(uniq(f"l0_ctxb{p}"), [DC, SC], BF16)) for p in range(2)]
    qpn = qp[:].rearrange("p b h t -> p (b h) t")
    qpbn = qpb[:].rearrange("p b h t -> p (b h) t")

    cfg = Cfg()
    cfg.heads, cfg.loop, cfg.chunks, cfg.groups, cfg.keys, cfg.scale = H0, False, CHUNKS, GROUPS, key_rows, scale
    cfg.row, cfg.rows, cfg.row_dt = DC, 1, F32
    cfg.max_q = lambda at, t: qpbn[:, bass.ds(at.n, 1), 128 * t:128 * t + 128].rearrange("p a t -> p (a t)")
    cfg.max_k = lambda at, k0, size: ctxb[at.p][:, k0:k0 + size]
    cfg.score_k = lambda at, j: ctxT[at.p][:, 128 * j:128 * j + key_rows(j)]
    cfg.score_q = lambda at: qpn[:, bass.ds(at.n, 1), :].rearrange("p a t -> p (a t)")
    cfg.shift_rows = lambda at: qpn[DC:DC + 1, bass.ds(at.n, 1), :].rearrange("p a t -> p (a t)")
    cfg.value = lambda at, j: ctxk[at.p][0:key_rows(j), j, :]
    core = Core(nc, ctx, c, cfg)
    cfg.strips = 1
    cfg.out = lambda at, j: core.ps_out[0:DC + 1, 0:S]
    cfg.out_copied = s.l0_out
    block = ctx.enter_context(nc.Block())

    @block.sync
    def _(sp):
        sp.sem_inc(s.l0_batch, 2)
        with sp.Fori(0, B // 2) as i:
            for p in range(2):
                sp.wait_ge(s.l0_batch, 2 * i + p + 1)
                sp.dma_start(ctxT[p][:], d["ctxT"][bass.ds(2 * i + p, 1)].rearrange("b p n -> (b p) n")) \
                    .then_inc(loaded[p], 16)
                sp.dma_start(ctxk[p][:], d["ctx_tok"][bass.ds(2 * i + p, 1)].rearrange("b p j n -> (b p) j n")) \
                    .then_inc(loaded[p], 16)

    @block.gpsimd
    def _(pool):
        nc.gpsimd.memset(core.shift_cols[:], 0.0).then_inc(s.l0_zero, 1)

    @block.tensor
    def _(pe):
        core.begin_pe(pe)

        def first(at):
            core.pe_max(pe, at, range(2 * core.NCH))
            core.pe_turn(pe, at)

        with pe.Fori(0, B // 2) as i:
            for p in range(2):
                pe.wait_ge(loaded[p], 32 * i + 32)
                pe.wait_ge(s.l0_ctxb, 2 * i + p + 1)
                core.heads(pe, p, i, first, lambda at, nxt, is_first: core.pe_step(pe, at, nxt))

    @block.vector
    def _(dve):
        core.begin_dve(dve)
        link = Link(dve, s.l0_link)
        dve.wait_ge(s.l0_zero, 1)

        def step(at, nxt, is_first):
            if nxt is not None:
                core.dve_max(dve, nxt, link)

        with dve.Fori(0, B // 2) as i:
            for p in range(2):
                dve.wait_ge(loaded[p], 32 * i + 32)
                nc.vector.tensor_copy(ctxb[p][:], ctxT[p][0:DC, :]).then_inc(s.l0_ctxb, 1)
                core.heads(dve, p, i, lambda at: core.dve_max(dve, at, link), step)

    @block.scalar
    def _(act):
        core.begin_act(act)

        def copy_out(n):
            act.wait_ge(core.s.values_used, (n + 1) * core.NG + 2)
            nc.scalar.copy(qpn[:, bass.ds(n, 1), :].rearrange("p a t -> p (a t)"),
                           core.ps_out[0:DC + 1, 0:S]).then_inc(s.l0_out, 1)

        def step(at, nxt, is_first):
            core.act_exp(act, at, range(0, 1))
            if not is_first:
                copy_out(at.n - 1)
            core.act_exp(act, at, range(1, core.NG))

        with act.Fori(0, B // 2) as i:
            for p in range(2):
                core.heads(act, p, i, None, step)
                copy_out((2 * i + p) * H0 + H0 - 1)
                act.sem_inc(s.l0_batch, 1)


def heads_out(nc, c, heads, w_o, bo, ctx, dh, H, gate):
    s = sems(ctx, nc, "ho_y ho_inv ho_sum ho_bias")
    py = ctx.enter_context(nc.psum_tensor(uniq("ho_py"), [128, 4, 2, 256], F32))
    pb = ctx.enter_context(nc.psum_tensor(uniq("ho_pb"), [128, 512], F32))
    inv = ctx.enter_context(nc.sbuf_tensor(uniq("ho_inv_t"), [128, NT, H], F32))
    total = ctx.enter_context(nc.sbuf_tensor(uniq("ho_total"), [128, NT, D], F32))
    PAIRS = H // 2
    block = ctx.enter_context(nc.Block())

    @block.tensor
    def _(pe):
        nc.tensor.matmul(pb[:, 0:D], c.ones_row[:], bo[:], start=True, stop=True).then_inc(s.ho_bias, 1)
        for x in range(NT * PAIRS):
            n, t = x // PAIRS, 128 * (x // PAIRS % 2)
            if x >= 4:
                pe.wait_ge(s.ho_sum, 2 * x - 5)
            for y in range(2):
                h = 2 * (x % PAIRS) + y
                ins = nc.tensor.matmul(py[:, x % 4, y, 0:D + 1], heads[0:dh + 1, n // 2, h, t:t + 128], w_o[:, h, :],
                                       start=True, stop=True)
            ins.then_inc(s.ho_y, 1)

    @block.vector
    def _(dve):
        dve.wait_ge(s.ho_bias, 1)
        nc.vector.tensor_copy(total[:], pb[:, 0:D].unsqueeze(1).to_broadcast([128, NT, D])).then_inc(s.ho_sum, 1)
        for x in range(NT * PAIRS):
            n, h = x // PAIRS, 2 * (x % PAIRS)
            dve.wait_ge(s.ho_y, x + 1)
            nc.vector.reciprocal(inv[:, n, h:h + 2], py[:, x % 4, :, D]).then_inc(s.ho_inv, 1)
            dve.wait_ge(s.ho_inv, x + 1)
            for y in range(2):
                dve.wait_ge(s.ho_sum, 1 + 2 * x + y)
                nc.vector.scalar_tensor_tensor(out=total[:, n, :], in0=py[:, x % 4, y, 0:D], scalar=inv[:, n, h + y:h + y + 1],
                                               in1=total[:, n, :], op0=ALU.mult, op1=ALU.add).then_inc(s.ho_sum, 1)
        dve.wait_ge(s.ho_sum, 1 + 2 * NT * PAIRS)
        nc.vector.scalar_tensor_tensor(out=c.x_res[:], in0=total[:], scalar=c.tanh_g[:, gate:gate + 1], in1=c.x_res[:],
                                       op0=ALU.mult, op1=ALU.add)


H8, DH8 = 16, 8
VCOLS = (H8 - 1) * (DH8 + 1) + 32
Q_PIECES = [0, 0, 0, 1, 1, 2]
K_PIECES = [0, 1, 2, 0, 1, 0]
ROW_MASK, ROW_SHIFT, ROWS8 = 48, 64, 66
NP = 3


class Strips:

    def __init__(self, nc, ctx, c, core, strips):
        self.nc, self.c, self.core, self.rows = nc, c, core, 32 * strips
        self.s = sems(ctx, nc, "strips_link strips_copied strips_made strips_summed strips_parts strips_normed "
                               "strips_turned strips_out")

        def sb(n, shape):
            return ctx.enter_context(nc.sbuf_tensor(uniq(f"strips_{n}_t"), shape, F32))
        self.product = sb("product", [128, H8, S])
        self.summed = sb("summed", [128, H8 // 4, S])
        self.rden = sb("rden", [128, TPB, H8])
        self.heads = sb("heads", [128, TPB, H8, DH8])
        cfg = core.cfg
        cfg.strips = strips
        cfg.out = lambda at, j: core.ps_out[32 * (j % strips):32 * (j % strips) + 32, 0:S]
        cfg.out_copied = self.s.strips_copied
        self.turn = core.ps_turn[:, 1, :].rearrange("p (t q) -> p t q", t=TPB)
        self.ps_sum = core.ps_scores[:, 0, :].rearrange("p (x q) -> p x q", x=H8 // 4)
        self.ps_parts = core.ps_scores[:, 1, :].rearrange("p (t x n) -> p t x n", t=TPB, x=H8 // 4)

    def begin_pe(self, pe):
        self.core.begin_pe(pe)
        pe.sem_inc(self.s.strips_out, 1)

    def begin_dve(self, dve):
        self.core.begin_dve(dve)
        dve.sem_inc(self.s.strips_turned, 1)

    def pe_turn_free(self, pe, b):
        pe.wait_ge(self.s.strips_out, b + 1)

    def pe(self, pe, b):
        s, core, nc, c = self.s, self.core, self.nc, self.c
        pe.wait_ge(s.strips_copied, H8 * (b + 1) + 1)
        pe.wait_ge(core.s.exp_done, H8 * core.NG * (b + 1) + 2)
        for x in range(H8 // 4):
            for y in range(4):
                ins = nc.tensor.matmul(self.ps_sum[32 * y:32 * y + 32, x, :], c.strip_sum[:],
                                       self.product[:, 4 * x + y, :], start=True, stop=True)
        ins.then_inc(s.strips_made, 1)
        pe.wait_ge(s.strips_summed, b + 1)
        for x in range(H8 // 4):
            for t in range(TPB):
                ins = nc.tensor.transpose(self.ps_parts[:, t, x, :], self.summed[:, x, 128 * t:128 * t + 128], c.ident[:])
        ins.then_inc(s.strips_parts, 1)
        pe.wait_ge(s.strips_normed, b + 1)
        for t in range(TPB):
            ins = nc.tensor.transpose(self.turn[:, t, :], self.heads[:, t, :, :].rearrange("p h n -> p (h n)"), c.ident[:])
        ins.then_inc(s.strips_turned, 1)

    def act(self, act, p, i, b):
        s, core, nc = self.s, self.core, self.nc

        def copy_out(h):
            act.wait_ge(core.s.values_used, (b * H8 + h + 1) * core.NG + 2)
            nc.scalar.copy(self.product[0:self.rows, h, :], core.ps_out[0:self.rows, 0:S]).then_inc(s.strips_copied, 1)

        def step(at, nxt, is_first):
            core.act_exp(act, at, range(0, 1))
            if not is_first:
                copy_out(at.h - 1)
            core.act_exp(act, at, range(1, core.NG))
        core.heads(act, p, i, None, step)
        copy_out(H8 - 1)
        act.wait_ge(s.strips_made, b + 1)
        nc.scalar.copy(self.summed[:], self.ps_sum).then_inc(s.strips_summed, 1)
        act.wait_ge(s.strips_turned, b + 2)
        nc.scalar.copy(self.c.xnT[:, bass.ds(b * S, S)], core.ps_turn[:, 1, :]).then_inc(s.strips_out, 1)

    def dve(self, dve, p, i, b):
        s, core, nc = self.s, self.core, self.nc
        LINKS = 2 * H8 + 1

        def counted(at):
            link = Link(dve, s.strips_link)
            link.base = b * LINKS + 2 * at.h
            return link

        def step(at, nxt, is_first):
            if nxt is not None:
                core.dve_max(dve, nxt, counted(nxt))
        core.heads(dve, p, i, lambda at: core.dve_max(dve, at, counted(at)), step)
        dve.wait_ge(s.strips_parts, b + 1)
        heads_of = self.ps_parts.rearrange("p t x (y n) -> p t (x y) n", y=4)
        nc.vector.reciprocal(self.rden[:], heads_of[:, :, :, DH8]).then_inc(s.strips_link, 1)
        dve.wait_ge(s.strips_link, (b + 1) * LINKS)
        dve.wait_ge(s.strips_turned, b + 1)
        for t in range(TPB):
            ins = nc.vector.tensor_tensor(self.heads[:, t, :, :], heads_of[:, t, :, 0:DH8],
                                          bcast(self.rden[:, t, :], [128, H8, DH8]), ALU.mult)
        ins.then_inc(s.strips_normed, 1)


def l8_attention(nc, c, d, name, finish_layer):
    with ExitStack() as ctx:
        q_pieces = nc.dram_tensor(f"{name}_qpieces", (NP, 128, NT * 128), BF16, kind="Internal").ap()
        with ExitStack() as cx:
            _l8_queries(nc, c, d, name, q_pieces, cx)
        with ExitStack() as cx:
            _l8_core(nc, c, d, name, q_pieces, cx)
        with ExitStack() as cx:
            finish_layer(nc, c, d, cx)


def _l8_queries(nc, c, d, name, q_pieces, ctx, biased=True):
    s = sems(ctx, nc, "q_w q_made q_biased q_high q_rest q_middle q_low q_out")
    wq = ctx.enter_context(nc.sbuf_tensor(uniq("q_wq"), [D, 128], F32))
    bq = ctx.enter_context(nc.sbuf_tensor(uniq("q_bq"), [128, 1], F32))
    qf = ctx.enter_context(nc.sbuf_tensor(uniq("q_f"), [128, 4, 512], F32))
    rest = ctx.enter_context(nc.sbuf_tensor(uniq("q_rest"), [128, 4, 512], F32))
    piece = [ctx.enter_context(nc.sbuf_tensor(uniq(f"q_piece{i}"), [128, 4, 512], BF16)) for i in range(NP)]
    pq = ctx.enter_context(nc.psum_tensor(uniq("q_ps"), [128, 4, 512], F32))
    block = ctx.enter_context(nc.Block())

    @block.sync
    def _(sp):
        sp.dma_start(wq[:], d[f"{name}_Wq"]).then_inc(s.q_w, 16)
        if biased:
            sp.dma_start(bq[:], d[f"{name}_bq"]).then_inc(s.q_w, 16)
        for i, done in enumerate([s.q_high, s.q_middle, s.q_low]):
            sp.wait_ge(done, 4)
            sp.dma_start(q_pieces[i], piece[i][:].rearrange("p k n -> p (k n)")).then_inc(s.q_out, 16)
        sp.wait_ge(s.q_out, 16 * NP)

    @block.tensor
    def _(pe):
        pe.wait_ge(s.q_w, 32 if biased else 16)
        for k in range(4):
            nc.tensor.matmul(pq[:, k, :], wq[:], c.xnT[:, 512 * k:512 * k + 512],
                             start=True, stop=True).then_inc(s.q_made, 1)

    @block.scalar
    def _(act):
        act.wait_ge(s.q_w, 32 if biased else 16)
        for k in range(4):
            act.wait_ge(s.q_made, k + 1)
            if biased:
                ins = nc.scalar.activation(qf[:, k, :], pq[:, k, :], ACT.Identity, bias=bq[:])
            else:
                ins = nc.scalar.copy(qf[:, k, :], pq[:, k, :])
            ins.then_inc(s.q_biased, 1)
        for k in range(4):
            act.wait_ge(s.q_biased, k + 1)
            nc.scalar.copy(piece[0][:, k, :], qf[:, k, :]).then_inc(s.q_high, 1)
        for k in range(4):
            act.wait_ge(s.q_rest, k + 1)
            nc.scalar.copy(piece[1][:, k, :], rest[:, k, :]).then_inc(s.q_middle, 1)

    @block.vector
    def _(dve):
        for k in range(4):
            dve.wait_ge(s.q_high, k + 1)
            nc.vector.tensor_tensor(rest[:, k, :], qf[:, k, :], piece[0][:, k, :], ALU.subtract).then_inc(s.q_rest, 1)
        for k in range(4):
            dve.wait_ge(s.q_middle, k + 1)
            nc.vector.tensor_tensor(piece[2][:, k, :], rest[:, k, :], piece[1][:, k, :],
                                    ALU.subtract).then_inc(s.q_low, 1)


KCH = [(0, 512), (512, 512), (1024, 512), (1536, SC - 1536)]


def _l8_core(nc, c, d, name, q_pieces, ctx):
    s = sems(ctx, nc, "a8_w a8_ctx a8_init a8_k_made a8_high a8_rest a8_middle a8_low a8_v_made a8_v_copied "
                      "a8_pieces_out a8_rows0 a8_rows1 a8_batch")
    rows_in = [s.a8_rows0, s.a8_rows1]

    def sb(n, shape, dt=F32, count=2):
        return [ctx.enter_context(nc.sbuf_tensor(uniq(f"a8_{n}{p}"), shape, dt)) for p in range(count)]
    ctxT, = sb("ctxT", [DC + 1, SC], F32, 1)
    kaug = sb("kaug", [ROWS8, H8, SC], BF16)
    qaug = sb("qaug", [ROWS8, H8, S], BF16)
    vaug = sb("vaug", [128, KT, VCOLS])
    wk, wv = sb("w", [DC + 1, 128])
    rest, = sb("rest", [128, SC], F32, 1)
    piece = sb("piece", [128, SC], BF16, NP)
    zero_rows, = sb("zero", [2, S], BF16, 1)
    k_pieces = nc.dram_tensor(f"{name}_kpieces", (NP, 128, SC), BF16, kind="Internal").ap()
    N_ROWS = 2 * len(K_PIECES) + 1

    def head(x, at, cols):
        return x[:, at.h, cols]

    cfg = Cfg()
    cfg.heads, cfg.loop, cfg.chunks, cfg.groups, cfg.keys, cfg.scale = H8, False, CHUNKS, GROUPS, key_rows, DH8 ** -0.5
    cfg.row, cfg.rows, cfg.row_dt = ROW_SHIFT, 2, BF16
    cfg.max_q = lambda at, t: head(qaug[at.p], at, slice(128 * t, 128 * t + 128))
    cfg.max_k = lambda at, k0, size: head(kaug[at.p], at, slice(k0, k0 + size))
    cfg.score_k = lambda at, j: head(kaug[at.p], at, slice(128 * j, 128 * j + key_rows(j)))
    cfg.score_q = lambda at: head(qaug[at.p], at, slice(0, S))
    cfg.shift_rows = lambda at: qaug[at.p][ROW_SHIFT:ROW_SHIFT + 2, at.h, :]
    cfg.value = lambda at, j: vaug[at.p][0:key_rows(j), j, 9 * at.h:9 * at.h + 32]
    core = Core(nc, ctx, c, cfg)
    strips = Strips(nc, ctx, c, core, 4)
    ps_v = core.ps_scores[:].rearrange("p a (k n) -> p (a k) n", n=512)
    block = ctx.enter_context(nc.Block())

    def batches(eng, prep, run):
        prep(0, 0, True)
        with eng.Fori(0, B // 2 - 1) as i:
            prep(1, i, False)
            run(0, i)
            prep(0, i + 1, False)
            run(1, i)
        i = B // 2 - 1
        prep(1, i, False)
        run(0, i)
        run(1, i)

    @block.sync
    def _(sp):
        sp.dma_start(wk[:], d[f"{name}_Wk"]).then_inc(s.a8_w, 16)
        sp.dma_start(wv[:], d[f"{name}_Wv"]).then_inc(s.a8_w, 16)
        sp.wait_ge(s.a8_init, 12)
        sp.sem_inc(s.a8_batch, 2)

        def prep(p, i, first):
            b = 2 * i + p
            sp.wait_ge(s.a8_batch, b + 1)
            if not first:
                sp.wait_ge(s.a8_v_made, 4 * b)
            sp.dma_start(ctxT[:], d["ctxT"][b]).then_inc(s.a8_ctx, 16)
            if not first:
                sp.wait_ge(rows_in[1 - p], 16 * N_ROWS * (i + p))
            for x, done in enumerate([s.a8_high, s.a8_middle, s.a8_low]):
                sp.wait_ge(done, 4 * b + 4)
                sp.dma_start(k_pieces[x], piece[x][:]).then_inc(s.a8_pieces_out, 16)
            for x, y in enumerate(Q_PIECES):
                sp.dma_start(qaug[p][8 * x:8 * x + 8, :, :],
                             q_pieces[y].rearrange("(h e) n -> e h n", e=DH8)[:, :, b * S:(b + 1) * S]) \
                    .then_inc(rows_in[p], 16)
            sp.dma_start(qaug[p][ROW_SHIFT:ROW_SHIFT + 2, :, :], zero_rows[:].unsqueeze(1).to_broadcast([2, H8, S])) \
                .then_inc(rows_in[p], 16)
            sp.wait_ge(s.a8_pieces_out, 16 * NP * (b + 1))
            for x, y in enumerate(K_PIECES):
                sp.dma_start(kaug[p][8 * x:8 * x + 8, :, :],
                             k_pieces[y].rearrange("(h e) n -> e h n", e=DH8)).then_inc(rows_in[p], 16)
        for b in range(B):
            prep(b % 2, b // 2, b == 0)

    @block.gpsimd
    def _(pool):
        link = Link(pool, s.a8_init)
        for p in range(2):
            link(nc.gpsimd.memset(kaug[p][32:64, :, :], 0.0))
            link(nc.gpsimd.memset(qaug[p][32:64, :, :], 0.0))
            link(nc.gpsimd.memset(kaug[p][64:66, :, :], 1.0))
            link(nc.gpsimd.memset(vaug[p][:, :, H8 * 9:], 0.0))
            link(nc.gpsimd.memset(vaug[p][:, :, 0:H8 * 9].rearrange("p j (h n) -> p j h n", n=9)[:, :, :, DH8:], 1.0))
        link(nc.gpsimd.memset(zero_rows[:], 0.0))
        link(nc.gpsimd.memset(core.shift_cols[:], 0.0))

    @block.tensor
    def _(pe):
        strips.begin_pe(pe)
        pe.wait_ge(s.a8_w, 32)

        def prep(p, i, first):
            b = 2 * i + p
            pe.wait_ge(s.a8_ctx, 16 * b + 16)
            for x, (k0, size) in enumerate(KCH):
                if x >= 2:
                    pe.wait_ge(s.a8_rest, 4 * b + x - 1)
                nc.tensor.matmul(core.ps_max[:, x % 2, 0:size], wk[:], ctxT[:, k0:k0 + size],
                                 start=True, stop=True).then_inc(s.a8_k_made, 1)
            for x, (j0, nj) in enumerate(GROUPS):
                for j in range(j0, j0 + nj):
                    ins = nc.tensor.matmul(ps_v[0:key_rows(j), x, 128 * (j - j0):128 * (j - j0) + 128],
                                           ctxT[:, 128 * j:128 * j + key_rows(j)], wv[:], start=True, stop=True)
                ins.then_inc(s.a8_v_made, 1)
            pe.wait_ge(s.a8_rest, 4 * b + 4)
            pe.wait_ge(s.a8_v_copied, 4 * b + 4)

        def first(at):
            core.pe_max(pe, at, range(2 * core.NCH))
            strips.pe_turn_free(pe, at.b)
            core.pe_turn(pe, at)

        def run(p, i):
            b = 2 * i + p
            pe.wait_ge(rows_in[p], 16 * N_ROWS * (i + 1))
            core.heads(pe, p, i, first, lambda at, nxt, is_first: core.pe_step(pe, at, nxt))
            strips.pe(pe, b)
        batches(pe, prep, run)

    @block.scalar
    def _(act):
        core.begin_act(act)
        act.wait_ge(s.a8_init, 12)

        def prep(p, i, first):
            b = 2 * i + p
            if not first:
                act.wait_ge(s.a8_pieces_out, 16 * NP * b)
            for x, (k0, size) in enumerate(KCH):
                act.wait_ge(s.a8_k_made, 4 * b + x + 1)
                nc.scalar.copy(piece[0][:, k0:k0 + size], core.ps_max[:, x % 2, 0:size]).then_inc(s.a8_high, 1)
            for x, (k0, size) in enumerate(KCH):
                act.wait_ge(s.a8_rest, 4 * b + x + 1)
                nc.scalar.copy(piece[1][:, k0:k0 + size], rest[:, k0:k0 + size]).then_inc(s.a8_middle, 1)
            for x, (j0, nj) in enumerate(GROUPS):
                rows = key_rows(j0)
                act.wait_ge(s.a8_v_made, 4 * b + x + 1)
                nc.scalar.copy(vaug[p][0:rows, j0:j0 + nj, 0:H8 * 9].rearrange("p j (h n) -> p j h n", n=9)[:, :, :, 0:DH8],
                               ps_v[0:rows, x, 0:128 * nj].rearrange("p (j h n) -> p j h n", j=nj, n=DH8)) \
                    .then_inc(s.a8_v_copied, 1)

        def run(p, i):
            strips.act(act, p, i, 2 * i + p)
            act.sem_inc(s.a8_batch, 1)
        batches(act, prep, run)

    @block.vector
    def _(dve):
        strips.begin_dve(dve)
        dve.wait_ge(s.a8_init, 12)

        def prep(p, i, first):
            b = 2 * i + p
            if not first:
                dve.wait_ge(s.a8_pieces_out, 16 * NP * b)
            for x, (k0, size) in enumerate(KCH):
                dve.wait_ge(s.a8_high, 4 * b + x + 1)
                nc.vector.tensor_tensor(rest[:, k0:k0 + size], core.ps_max[:, x % 2, 0:size],
                                        piece[0][:, k0:k0 + size], ALU.subtract).then_inc(s.a8_rest, 1)
            for x, (k0, size) in enumerate(KCH):
                dve.wait_ge(s.a8_middle, 4 * b + x + 1)
                nc.vector.tensor_tensor(piece[2][:, k0:k0 + size], rest[:, k0:k0 + size], piece[1][:, k0:k0 + size],
                                        ALU.subtract).then_inc(s.a8_low, 1)

        batches(dve, prep, lambda p, i: strips.dve(dve, p, i, 2 * i + p))


def add_tiles(nc, c, s_made, s_added, py, gate, dve):
    for n in range(NT):
        dve.wait_ge(s_made, n + 1)
        nc.vector.scalar_tensor_tensor(out=c.x_res[:, n, :], in0=py[:, n % 4, 0:D], scalar=c.tanh_g[:, gate:gate + 1],
                                       in1=c.x_res[:, n, :], op0=ALU.mult, op1=ALU.add).then_inc(s_added, 1)


def l1_attention(nc, c, d):
    def out(nc, c, d, ctx):
        s = sems(ctx, nc, "o_w o_made o_added")
        wo = ctx.enter_context(nc.sbuf_tensor(uniq("o_w"), [128, D], F32))
        bo = ctx.enter_context(nc.sbuf_tensor(uniq("o_b"), [1, D], F32))
        py = ctx.enter_context(nc.psum_tensor(uniq("o_py"), [128, 4, 512], F32))
        block = ctx.enter_context(nc.Block())

        @block.sync
        def _(sp):
            sp.dma_start(wo[:], d["l1_Wo"]).then_inc(s.o_w, 16)
            sp.dma_start(bo[:], d["l1_bo"]).then_inc(s.o_w, 16)

        @block.tensor
        def _(pe):
            pe.wait_ge(s.o_w, 32)
            for n in range(NT):
                if n >= 4:
                    pe.wait_ge(s.o_added, n - 3)
                nc.tensor.matmul(py[:, n % 4, 0:D], c.xnT[:, 128 * n:128 * n + 128], wo[:], start=True, stop=False)
                nc.tensor.matmul(py[:, n % 4, 0:D], c.ones_row[:], bo[:], start=False, stop=True).then_inc(s.o_made, 1)

        @block.vector
        def _(dve):
            add_tiles(nc, c, s.o_made, s.o_added, py, 1, dve)
    l8_attention(nc, c, d, "l1", out)


def l2_attention(nc, c, d):
    def mlp(nc, c, d, ctx):
        s = sems(ctx, nc, "o_w o_hmade o_hidden o_made o_added")
        w1 = ctx.enter_context(nc.sbuf_tensor(uniq("o_w1"), [128, 2, 128], F32))
        b1 = ctx.enter_context(nc.sbuf_tensor(uniq("o_b1"), [128, 2], F32))
        w2 = ctx.enter_context(nc.sbuf_tensor(uniq("o_w2"), [128, 2, D], F32))
        b2 = ctx.enter_context(nc.sbuf_tensor(uniq("o_b2"), [1, D], F32))
        hid = ctx.enter_context(nc.sbuf_tensor(uniq("o_hid"), [128, 2, 4, 512], F32))
        ph = ctx.enter_context(nc.psum_tensor(uniq("o_ph"), [128, 4, 512], F32))
        py = ctx.enter_context(nc.psum_tensor(uniq("o_py"), [128, 4, 512], F32))
        block = ctx.enter_context(nc.Block())

        @block.sync
        def _(sp):
            for dst, src in ((w1, "l2_W1"), (b1, "l2_b1"), (w2, "l2_W2"), (b2, "l2_b2")):
                sp.dma_start(dst[:], d[src]).then_inc(s.o_w, 16)

        @block.tensor
        def _(pe):
            pe.wait_ge(s.o_w, 64)
            for x in range(8):
                k, j = x // 2, x % 2
                if x >= 4:
                    pe.wait_ge(s.o_hidden, x - 3)
                nc.tensor.matmul(ph[:, x % 4, :], w1[:, j, :], c.xnT[:, 512 * k:512 * k + 512],
                                 start=True, stop=True).then_inc(s.o_hmade, 1)
            for n in range(NT):
                pe.wait_ge(s.o_hidden, 2 * (n // 4) + 2)
                if n >= 4:
                    pe.wait_ge(s.o_added, n - 3)
                for j in range(2):
                    nc.tensor.matmul(py[:, n % 4, 0:D], hid[:, j, n // 4, 128 * (n % 4):128 * (n % 4) + 128],
                                     w2[:, j, :], start=(j == 0), stop=False)
                nc.tensor.matmul(py[:, n % 4, 0:D], c.ones_row[:], b2[:], start=False, stop=True).then_inc(s.o_made, 1)

        @block.scalar
        def _(act):
            act.wait_ge(s.o_w, 64)
            for x in range(8):
                act.wait_ge(s.o_hmade, x + 1)
                nc.scalar.activation(hid[:, x % 2, x // 2, :], ph[:, x % 4, :], ACT.Relu,
                                     bias=b1[:, x % 2:x % 2 + 1]).then_inc(s.o_hidden, 1)

        @block.vector
        def _(dve):
            add_tiles(nc, c, s.o_made, s.o_added, py, 2, dve)
    l8_attention(nc, c, d, "l2", mlp)


E0, I0, NG0, TOPG, TOPK = 16, 64, 4, 2, 4
BIG = 1e30


def l0_ffn(nc, c, d):
    with ExitStack() as ctx:
        comb = ctx.enter_context(nc.sbuf_tensor(uniq("f0_comb"), [128, NT, E0], F32))
        with ExitStack() as cx:
            _l0_route(nc, c, d, comb, cx)
        with ExitStack() as cx:
            _l0_experts(nc, c, d, comb, cx)


def _l0_route(nc, c, d, comb, ctx):
    s = sems(ctx, nc, "r_in r_made r_scored r_link")

    def sb(name, shape):
        return ctx.enter_context(nc.sbuf_tensor(uniq(name), shape, F32))
    gate, bias = sb("r_gate", [D, E0]), sb("r_bias", [128, E0])
    before_e, before_g = sb("r_before_e", [128, E0, E0]), sb("r_before_g", [128, NG0, NG0])
    scores, biased = sb("r_scores", [128, NT, E0]), sb("r_biased", [128, NT, E0])
    gmax, grank, penalty = sb("r_gmax", [128, NT, NG0]), sb("r_grank", [128, NT, NG0]), sb("r_pen", [128, NT, NG0])
    g_more, g_same = sb("r_gmore", [128, NT, NG0, NG0]), sb("r_gsame", [128, NT, NG0, NG0])
    more, same, rank = sb("r_more", [128, NT, E0, E0]), sb("r_same", [128, NT, E0, E0]), sb("r_rank", [128, NT, E0])
    ps = ctx.enter_context(nc.psum_tensor(uniq("r_ps"), [128, NT, E0], F32))
    block = ctx.enter_context(nc.Block())

    @block.sync
    def _(sp):
        for dst, src in ((gate[:], d["f0_gate"]), (bias[:], d["f0_bias"].partition_broadcast(128)),
                         (before_e[:], d["before_e"].partition_broadcast(128)),
                         (before_g[:], d["before_g"].partition_broadcast(128))):
            sp.dma_start(dst, src).then_inc(s.r_in, 16)

    @block.tensor
    def _(pe):
        pe.wait_ge(s.r_in, 64)
        for n in range(NT):
            ins = nc.tensor.matmul(ps[:, n, :], c.xnT[:, 128 * n:128 * n + 128], gate[:], start=True, stop=True)
        ins.then_inc(s.r_made, 1)

    @block.scalar
    def _(act):
        act.wait_ge(s.r_made, 1)
        nc.scalar.activation(scores[:], ps[:], ACT.Sigmoid).then_inc(s.r_scored, 1)

    @block.vector
    def _(dve):
        link = Link(dve, s.r_link)

        def ranks(v, n, before, more, same, rank):
            shape = [128, NT, n, n]
            rival, own = v[:].unsqueeze(2).to_broadcast(shape), v[:].unsqueeze(3).to_broadcast(shape)
            nc.vector.tensor_tensor(more[:], rival, own, ALU.is_gt)
            link(nc.vector.tensor_tensor(same[:], rival, own, ALU.is_equal))
            link(nc.vector.tensor_tensor(same[:], same[:], before[:].unsqueeze(1).to_broadcast(shape), ALU.mult))
            link(nc.vector.tensor_tensor(more[:], more[:], same[:], ALU.add))
            link(nc.vector.reduce_sum(rank[:], more[:], AX.X))

        dve.wait_ge(s.r_in, 64)
        dve.wait_ge(s.r_scored, 1)
        link(nc.vector.tensor_tensor(biased[:], scores[:], bias[:].unsqueeze(1).to_broadcast([128, NT, E0]), ALU.add))
        grouped = biased[:].rearrange("p n (g e) -> p n g e", g=NG0)
        link(nc.vector.reduce_max(gmax[:], grouped, AX.X))
        ranks(gmax, NG0, before_g, g_more, g_same, grank)
        link(nc.vector.tensor_scalar(penalty[:], grank[:], float(TOPG), -BIG, ALU.is_ge, ALU.mult))
        link(nc.vector.tensor_tensor(grouped, grouped, bcast(penalty[:], [128, NT, NG0, E0 // NG0]), ALU.add))
        ranks(biased, E0, before_e, more, same, rank)
        link(nc.vector.tensor_scalar(rank[:], rank[:], float(TOPK), None, ALU.is_lt))
        nc.vector.tensor_tensor(comb[:], rank[:], scores[:], ALU.mult)


def _l0_experts(nc, c, d, comb, ctx):
    s = sems(ctx, nc, "e_in e_combT e_comb_copied e_made e_silu e_mul e_hidden e_y e_ycopied e_yT e_added")
    NM = E0 // 2 + 1
    w13 = ctx.enter_context(nc.sbuf_tensor(uniq("e_w13"), [D, NM, 2, 128], F32))
    w2 = ctx.enter_context(nc.sbuf_tensor(uniq("e_w2"), [128, NM, D], F32))
    sel = ctx.enter_context(nc.sbuf_tensor(uniq("e_sel"), [E0, E0 // 2, 128], F32))
    combT = ctx.enter_context(nc.sbuf_tensor(uniq("e_combT"), [E0, NT * 128], F32))
    silu = ctx.enter_context(nc.sbuf_tensor(uniq("e_silu_t"), [128, 2, 512], F32))
    hid = ctx.enter_context(nc.sbuf_tensor(uniq("e_hid"), [128, 2, 512], F32))
    yT = ctx.enter_context(nc.sbuf_tensor(uniq("e_yT_t"), [D, 2, 512], F32))
    p1 = ctx.enter_context(nc.psum_tensor(uniq("e_p1"), [128, 2, 512], F32))
    p3 = ctx.enter_context(nc.psum_tensor(uniq("e_p3"), [128, 2, 512], F32))
    pc = ctx.enter_context(nc.psum_tensor(uniq("e_pc"), [128, 2, 512], F32))
    py = ctx.enter_context(nc.psum_tensor(uniq("e_py"), [128, 512], F32))
    pt = ctx.enter_context(nc.psum_tensor(uniq("e_pt"), [128, 512], F32))
    steps = [(k, m) for k in range(4) for m in range(NM)]
    rows = lambda m: 128 if m < NM - 1 else I0
    block = ctx.enter_context(nc.Block())

    @block.sync
    def _(sp):
        for dst, src in ((w13, "f0_w13"), (w2, "f0_w2"), (sel, "f0_sel")):
            sp.dma_start(dst[:], d[src]).then_inc(s.e_in, 16)

    @block.tensor
    def _(pe):
        for k in range(4):
            if k:
                pe.wait_ge(s.e_comb_copied, k)
            for n in range(4 * k, 4 * k + 4):
                ins = nc.tensor.transpose(pt[0:E0, 128 * (n % 4):128 * (n % 4) + 128], comb[:, n, :], c.ident[:])
            ins.then_inc(s.e_combT, 1)
        pe.wait_ge(s.e_in, 48)
        pe.wait_ge(s.e_comb_copied, 4)

        def down(x):
            k, m = steps[x]
            pe.wait_ge(s.e_hidden, x + 1)
            if m == 0 and k:
                pe.wait_ge(s.e_ycopied, k)
            ins = nc.tensor.matmul(py[:], w2[0:rows(m), m, :], hid[0:rows(m), x % 2, :], start=(m == 0), stop=(m == NM - 1))
            if m == NM - 1:
                ins.then_inc(s.e_y, 1)

        def turn(k):
            pe.wait_ge(s.e_ycopied, k + 1)
            if k:
                pe.wait_ge(s.e_added, 4 * k)
            for j in range(4):
                ins = nc.tensor.transpose(pt[:, 128 * j:128 * j + 128], yT[:, k % 2, 128 * j:128 * j + 128], c.ident[:])
            ins.then_inc(s.e_yT, 1)
        for x, (k, m) in enumerate(steps):
            r, tok = rows(m), slice(512 * k, 512 * k + 512)
            if x >= 2:
                pe.wait_ge(s.e_hidden, x - 1)
            nc.tensor.matmul(p1[0:r, x % 2, :], w13[:, m, 0, 0:r], c.xnT[:, tok], start=True, stop=True)
            ins = nc.tensor.matmul(p3[0:r, x % 2, :], w13[:, m, 1, 0:r], c.xnT[:, tok], start=True, stop=True)
            if m < NM - 1:
                ins = nc.tensor.matmul(pc[:, x % 2, :], sel[:, m, :], combT[:, tok], start=True, stop=True)
            ins.then_inc(s.e_made, 1)
            if x:
                down(x - 1)
            if m == 2 and k:
                turn(k - 1)
        down(len(steps) - 1)
        turn(3)

    @block.scalar
    def _(act):
        for k in range(4):
            act.wait_ge(s.e_combT, k + 1)
            nc.scalar.copy(combT[:, 512 * k:512 * k + 512], pt[0:E0, :]).then_inc(s.e_comb_copied, 1)
        for x, (k, m) in enumerate(steps):
            act.wait_ge(s.e_made, x + 1)
            if x >= 2:
                act.wait_ge(s.e_mul, x - 1)
            nc.scalar.activation(silu[0:rows(m), x % 2, :], p1[0:rows(m), x % 2, :], ACT.Silu).then_inc(s.e_silu, 1)
            if m == 1 and k:
                act.wait_ge(s.e_y, k)
                nc.scalar.copy(yT[:, (k - 1) % 2, :], py[:]).then_inc(s.e_ycopied, 1)
        act.wait_ge(s.e_y, 4)
        nc.scalar.copy(yT[:, 1, :], py[:]).then_inc(s.e_ycopied, 1)

    @block.vector
    def _(dve):
        def add(k):
            dve.wait_ge(s.e_yT, k + 1)
            for j in range(4):
                n = 4 * k + j
                nc.vector.scalar_tensor_tensor(out=c.x_res[:, n, :], in0=pt[:, 128 * j:128 * j + 128],
                                               scalar=c.tanh_g[:, 4:5], in1=c.x_res[:, n, :], op0=ALU.mult,
                                               op1=ALU.add).then_inc(s.e_added, 1)
        for x, (k, m) in enumerate(steps):
            r = rows(m)
            dve.wait_ge(s.e_silu, x + 1)
            nc.vector.tensor_tensor(silu[0:r, x % 2, :], silu[0:r, x % 2, :], p3[0:r, x % 2, :],
                                    ALU.mult).then_inc(s.e_mul, 1)
            dve.wait_ge(s.e_mul, x + 1)
            if m < NM - 1:
                ins = nc.vector.tensor_tensor(hid[0:r, x % 2, :], silu[0:r, x % 2, :], pc[0:r, x % 2, :], ALU.mult)
            else:
                ins = nc.vector.tensor_copy(hid[0:r, x % 2, :], silu[0:r, x % 2, :])
            ins.then_inc(s.e_hidden, 1)
            if m == 3 and k:
                add(k - 1)
        add(3)


HID, NJ = 512, 4
ROUND = 1.5 * 2 ** 23


def l2_ffn(nc, c, d):
    with ExitStack() as ctx:
        def sb(name, shape, dt=F32):
            return ctx.enter_context(nc.sbuf_tensor(uniq(name), shape, dt))
        w1q, w2q = sb("b_w1q", [D, HID]), sb("b_w2q", [128, NJ, D], BF16)
        wmean = sb("b_wmean", [128, 2])
        hidden = sb("b_hidden", [128, NJ, B, S])
        taps = sb("b_taps", [128, NJ, 4])
        with ExitStack() as cx:
            _l2_quantise(nc, c, d, w1q, w2q, wmean, taps, cx)
        with ExitStack() as cx:
            _l2_conv(nc, c, w1q, hidden, taps, cx)
        with ExitStack() as cx:
            _l2_down(nc, c, w2q, wmean, hidden, cx)


def _l2_quantise(nc, c, d, w1q, w2q, wmean, taps, ctx):
    s = sems(ctx, nc, "b_in b_sums b_total b_link b_round b_xq b_turned b_xnT")

    def sb(name, shape):
        return ctx.enter_context(nc.sbuf_tensor(uniq(name), shape, F32))
    w1, w2 = sb("b_w1", [D, HID]), sb("b_w2", [128, NJ * D])
    ones, part = sb("b_ones", [128, 128]), sb("b_part", [128, 2])
    wscale, xmax, xscale, xinv = sb("b_ws", [128, 2]), sb("b_xm", [128, NT]), sb("b_xs", [128, NT]), sb("b_xi", [128, NT])
    ps = ctx.enter_context(nc.psum_tensor(uniq("b_ps"), [128, 2], F32))
    pt = ctx.enter_context(nc.psum_tensor(uniq("b_pt"), [128, 4, 512], F32))
    block = ctx.enter_context(nc.Block())

    @block.sync
    def _(sp):
        for dst, src in ((w1, "b_w1"), (w2, "b_w2"), (taps, "b_taps")):
            sp.dma_start(dst[:], d[src]).then_inc(s.b_in, 16)

    @block.tensor
    def _(pe):
        pe.wait_ge(s.b_sums, 1)
        nc.tensor.matmul(ps[:], ones[:], part[:], start=True, stop=True).then_inc(s.b_total, 1)
        for k in range(4):
            pe.wait_ge(s.b_xq, k + 1)
            for j in range(4):
                ins = nc.tensor.transpose(pt[:, k, 128 * j:128 * j + 128], c.xn[:, 4 * k + j, :], c.ident[:])
            ins.then_inc(s.b_turned, 1)

    @block.scalar
    def _(act):
        for k in range(4):
            act.wait_ge(s.b_turned, k + 1)
            nc.scalar.copy(c.xnT[:, 512 * k:512 * k + 512], pt[:, k, :]).then_inc(s.b_xnT, 1)

    @block.vector
    def _(dve):
        link = Link(dve, s.b_link)
        link(nc.vector.tensor_reduce(xmax[:], c.xn[:], axis=AX.X, op=ALU.max, apply_absolute_value=True))
        link(nc.vector.tensor_scalar(xmax[:], xmax[:], 1e-5, None, ALU.max))
        link(nc.vector.reciprocal(xscale[:], xmax[:]))
        link(nc.vector.tensor_scalar(xscale[:], xscale[:], 127.0, None, ALU.mult))
        link(nc.vector.reciprocal(xinv[:], xscale[:]))
        link(nc.vector.tensor_tensor(c.xn[:], c.xn[:], bcast(xscale[:], [128, NT, D]), ALU.mult))
        link(nc.vector.tensor_scalar(c.xn[:], c.xn[:], ROUND, -ROUND, ALU.add, ALU.add))
        link(nc.vector.tensor_scalar(c.xn[:], c.xn[:], -128.0, 127.0, ALU.max, ALU.min))
        for k in range(4):
            t = slice(4 * k, 4 * k + 4)
            nc.vector.tensor_tensor(c.xn[:, t, :], c.xn[:, t, :], bcast(xinv[:, t], [128, 4, D]),
                                    ALU.mult).then_inc(s.b_xq, 1)
        dve.wait_ge(s.b_in, 48)
        nc.vector.memset(ones[:], 1.0)
        nc.vector.tensor_reduce(part[:, 0:1], w1[:], axis=AX.X, op=ALU.add, apply_absolute_value=True)
        nc.vector.tensor_reduce(part[:, 1:2], w2[:], axis=AX.X, op=ALU.add,
                                apply_absolute_value=True).then_inc(s.b_sums, 1)
        dve.wait_ge(s.b_total, 1)
        link(nc.vector.tensor_scalar(wmean[:], ps[:], 1.0 / (D * HID), 1e-5, ALU.mult, ALU.max))
        link(nc.vector.reciprocal(wscale[:], wmean[:]))
        link(nc.vector.reciprocal(wmean[:], wscale[:]))
        for x, (w, q) in enumerate(((w1, None), (w2, None))):
            link(nc.vector.tensor_scalar(w[:], w[:], wscale[:, x:x + 1], None, ALU.mult))
            link(nc.vector.tensor_scalar(w[:], w[:], ROUND, -ROUND, ALU.add, ALU.add))
            link(nc.vector.tensor_scalar(w[:], w[:], -1.0, 1.0, ALU.max, ALU.min))
        nc.vector.tensor_scalar(w1q[:], w1[:], wmean[:, 0:1], None, ALU.mult)
        nc.vector.tensor_copy(w2q[:].rearrange("p j n -> p (j n)"), w2[:])


def _l2_conv(nc, c, w1q, hidden, taps, ctx):
    s = sems(ctx, nc, "c_zero c_made c_copied c_middle c_left c_right c_silu")
    padded = ctx.enter_context(nc.sbuf_tensor(uniq("c_pad"), [128, 2, B, S + 2], F32))
    ph = ctx.enter_context(nc.psum_tensor(uniq("c_ph"), [128, 2, 4, 512], F32))
    block = ctx.enter_context(nc.Block())

    @block.tensor
    def _(pe):
        for j in range(NJ):
            if j >= 2:
                pe.wait_ge(s.c_copied, j - 1)
            for k in range(4):
                ins = nc.tensor.matmul(ph[:, j % 2, k, :], w1q[:, 128 * j:128 * j + 128],
                                       c.xnT[:, 512 * k:512 * k + 512], start=True, stop=True)
            ins.then_inc(s.c_made, 1)

    @block.scalar
    def _(act):
        act.wait_ge(s.c_zero, 1)
        for j in range(NJ):
            act.wait_ge(s.c_made, j + 1)
            if j >= 2:
                act.wait_ge(s.c_right, j - 1)
            nc.scalar.copy(padded[:, j % 2, :, 1:S + 1],
                           ph[:, j % 2, :, :].rearrange("p k (b t) -> p (k b) t", b=2)).then_inc(s.c_copied, 1)
            act.wait_ge(s.c_copied, j + 1)
            nc.scalar.activation(hidden[:, j, :, :], padded[:, j % 2, :, 1:S + 1], ACT.Identity,
                                 scale=taps[:, j, 1:2], bias=taps[:, j, 3:4]).then_inc(s.c_middle, 1)
        for j in range(NJ):
            act.wait_ge(s.c_right, j + 1)
            nc.scalar.activation(hidden[:, j, :, :], hidden[:, j, :, :], ACT.Silu).then_inc(s.c_silu, 1)

    @block.vector
    def _(dve):
        for p in range(2):
            nc.vector.memset(padded[:, p, :, 0:1], 0.0)
            ins = nc.vector.memset(padded[:, p, :, S + 1:S + 2], 0.0)
        ins.then_inc(s.c_zero, 1)
        for j in range(NJ):
            dve.wait_ge(s.c_middle, j + 1)
            nc.vector.scalar_tensor_tensor(out=hidden[:, j, :, :], in0=padded[:, j % 2, :, 0:S], scalar=taps[:, j, 0:1],
                                           in1=hidden[:, j, :, :], op0=ALU.mult, op1=ALU.add).then_inc(s.c_left, 1)
            dve.wait_ge(s.c_left, j + 1)
            nc.vector.scalar_tensor_tensor(out=hidden[:, j, :, :], in0=padded[:, j % 2, :, 2:S + 2], scalar=taps[:, j, 2:3],
                                           in1=hidden[:, j, :, :], op0=ALU.mult, op1=ALU.add).then_inc(s.c_right, 1)


def _l2_down(nc, c, w2q, wmean, hidden, ctx):
    s = sems(ctx, nc, "d_turned d_scaled d_rounded d_clipped d_q d_back d_copied d_y d_added d_link")

    def sb(name, shape, dt=F32):
        return ctx.enter_context(nc.sbuf_tensor(uniq(name), shape, dt))
    hmax, hscale, hinv = sb("d_max", [128, NT]), sb("d_scale", [128, NT]), sb("d_inv", [128, NT])
    rounded, q = sb("d_r", [128, 2, HID]), sb("d_qt", [128, 2, HID], BF16)
    qT = sb("d_qT", [128, 2, NJ, 128], BF16)
    factor, rnd, neg_rnd = sb("d_factor", [128, 1]), sb("d_rnd", [128, 1]), sb("d_nrnd", [128, 1])
    pt = ctx.enter_context(nc.psum_tensor(uniq("d_pt"), [128, 2, HID], F32))
    pb = ctx.enter_context(nc.psum_tensor(uniq("d_pb"), [128, 2, 2 * HID], BF16))
    py = ctx.enter_context(nc.psum_tensor(uniq("d_py"), [128, 2, 512], F32))
    hid = hidden[:].rearrange("p j b t -> p j (b t)")
    block = ctx.enter_context(nc.Block())

    @block.tensor
    def _(pe):
        def turn(n):
            if n >= 2:
                pe.wait_ge(s.d_rounded, n - 1)
            for j in range(NJ):
                ins = nc.tensor.transpose(pt[:, n % 2, 128 * j:128 * j + 128], hid[:, j, 128 * n:128 * n + 128], c.ident[:])
            ins.then_inc(s.d_turned, 1)
        turn(0)
        for n in range(NT):
            if n + 1 < NT:
                turn(n + 1)
            pe.wait_ge(s.d_q, n + 1)
            if n >= 2:
                pe.wait_ge(s.d_copied, n - 1)
            for j in range(NJ):
                ins = nc.tensor.transpose(pb[:, n % 2, 128 * j:128 * j + 128], q[:, n % 2, 128 * j:128 * j + 128], c.ident_b[:])
            ins.then_inc(s.d_back, 1)
            pe.wait_ge(s.d_copied, n + 1)
            if n >= 2:
                pe.wait_ge(s.d_added, n - 1)
            for j in range(NJ):
                ins = nc.tensor.matmul(py[:, n % 2, 0:D], qT[:, n % 2, j, :], w2q[:, j, :], start=(j == 0), stop=(j == NJ - 1))
            ins.then_inc(s.d_y, 1)

    @block.scalar
    def _(act):
        for n in range(NT):
            act.wait_ge(s.d_scaled, n + 1)
            nc.scalar.activation(rounded[:, n % 2, :], pt[:, n % 2, :], ACT.Identity, scale=hscale[:, n:n + 1],
                                 bias=rnd[:]).then_inc(s.d_rounded, 1)
            act.wait_ge(s.d_clipped, n + 1)
            nc.scalar.activation(q[:, n % 2, :], rounded[:, n % 2, :], ACT.Identity, bias=neg_rnd[:]).then_inc(s.d_q, 1)
            act.wait_ge(s.d_back, n + 1)
            nc.scalar.copy(qT[:, n % 2, :, :].rearrange("p j n -> p (j n)"), pb[:, n % 2, 0:HID]).then_inc(s.d_copied, 1)

    @block.vector
    def _(dve):
        link = Link(dve, s.d_link)
        nc.vector.memset(rnd[:], ROUND)
        nc.vector.memset(neg_rnd[:], -ROUND)
        link(nc.vector.tensor_tensor(factor[:], wmean[:, 1:2], c.tanh_g[:, 6:7], ALU.mult))

        def scale(n):
            t = slice(n, n + 1)
            dve.wait_ge(s.d_turned, n + 1)
            link(nc.vector.tensor_reduce(hmax[:, t], pt[:, n % 2, :], axis=AX.X, op=ALU.max, apply_absolute_value=True))
            link(nc.vector.tensor_scalar(hmax[:, t], hmax[:, t], 1e-5, None, ALU.max))
            link(nc.vector.reciprocal(hscale[:, t], hmax[:, t]))
            nc.vector.tensor_scalar(hscale[:, t], hscale[:, t], 127.0, None, ALU.mult).then_inc(s.d_scaled, 1)
            dve.wait_ge(s.d_scaled, n + 1)
            link(nc.vector.reciprocal(hinv[:, t], hscale[:, t]))
            nc.vector.tensor_scalar(hinv[:, t], hinv[:, t], factor[:], None, ALU.mult)
            dve.wait_ge(s.d_rounded, n + 1)
            nc.vector.tensor_scalar(rounded[:, n % 2, :], rounded[:, n % 2, :], ROUND - 128.0, ROUND + 127.0, ALU.max,
                                    ALU.min).then_inc(s.d_clipped, 1)

        def add(n):
            dve.wait_ge(s.d_y, n + 1)
            nc.vector.scalar_tensor_tensor(out=c.x_res[:, n, :], in0=py[:, n % 2, 0:D], scalar=hinv[:, n:n + 1],
                                           in1=c.x_res[:, n, :], op0=ALU.mult, op1=ALU.add).then_inc(s.d_added, 1)
        for n in range(NT):
            scale(n)
            if n:
                add(n - 1)
        add(NT - 1)


CAP = S // 2


def l1_ffn(nc, c, d):
    with ExitStack() as ctx:
        gate = ctx.enter_context(nc.sbuf_tensor(uniq("m_gate"), [128, NT], F32))
        values = ctx.enter_context(nc.sbuf_tensor(uniq("m_values"), [128, NT, VCOLS], F32))
        pieces = [nc.dram_tensor(f"m_{x}pieces", (NP, 128, NT * 128), BF16, kind="Internal").ap() for x in "qk"]
        mask = nc.dram_tensor("m_mask", (NT, 128), BF16, kind="Internal").ap()
        with ExitStack() as cx:
            _l1_choose(nc, c, d, gate, values, mask, cx)
        for x, name in enumerate(("m_q", "m_k")):
            with ExitStack() as cx:
                _l8_queries(nc, c, d, name, pieces[x], cx, biased=False)
        with ExitStack() as cx:
            _l1_core(nc, c, d, values, pieces, mask, cx)
        with ExitStack() as cx:
            _l1_out(nc, c, d, gate, cx)


def _l1_choose(nc, c, d, gate, values, mask, ctx):
    s = sems(ctx, nc, "h_in h_made h_gates h_link h_chosen h_turned h_masked h_out h_vmade h_vcopied")

    def sb(name, shape, dt=F32):
        return ctx.enter_context(nc.sbuf_tensor(uniq(name), shape, dt))
    wg, wv, before = sb("h_wg", [D, 128]), sb("h_wv", [D, 128]), sb("h_before", [128, TPB, S])
    rows, diag = sb("h_rows", [128, B, S]), sb("h_diag", [128, NT, 128])
    own, rank, chosen = sb("h_own", [128, NT]), sb("h_rank", [128, NT]), sb("h_chosen_t", [128, NT])
    more, same = sb("h_more", [128, B, TPB, S]), sb("h_same", [128, B, TPB, S])
    masked = sb("h_masked_t", [NT, 128], BF16)
    ps = ctx.enter_context(nc.psum_tensor(uniq("h_ps"), [128, 4, 512], F32))
    pv = ctx.enter_context(nc.psum_tensor(uniq("h_pv"), [128, 2, 512], F32))
    pm = ctx.enter_context(nc.psum_tensor(uniq("h_pm"), [NT, 128], F32))
    block = ctx.enter_context(nc.Block())

    @block.sync
    def _(sp):
        for dst, src in ((wg[:], d["m_Wg"]), (wv[:], d["m_Wv"]), (before[:], d["m_before"])):
            sp.dma_start(dst, src).then_inc(s.h_in, 16)
        sp.wait_ge(s.h_masked, 1)
        sp.dma_start(mask, masked[:]).then_inc(s.h_out, 16)
        sp.wait_ge(s.h_out, 16)

    @block.tensor
    def _(pe):
        pe.wait_ge(s.h_in, 48)
        for k in range(4):
            nc.tensor.matmul(ps[:, k, :], wg[:], c.xnT[:, 512 * k:512 * k + 512], start=True,
                             stop=True).then_inc(s.h_made, 1)
        for k in range(4):
            if k >= 2:
                pe.wait_ge(s.h_vcopied, k - 1)
            for j in range(4):
                n = 4 * k + j
                ins = nc.tensor.matmul(pv[:, k % 2, 128 * j:128 * j + 128], c.xnT[:, 128 * n:128 * n + 128], wv[:],
                                       start=True, stop=True)
            ins.then_inc(s.h_vmade, 1)
        pe.wait_ge(s.h_chosen, 1)
        nc.tensor.transpose(pm[:], chosen[:], c.ident[:]).then_inc(s.h_turned, 1)

    @block.scalar
    def _(act):
        for k in range(4):
            act.wait_ge(s.h_made, k + 1)
            nc.scalar.activation(rows[:, 2 * k:2 * k + 2, :], ps[:, k, :].rearrange("p (b t) -> p b t", b=2),
                                 ACT.Sigmoid).then_inc(s.h_gates, 1)
        for k in range(4):
            act.wait_ge(s.h_vmade, k + 1)
            nc.scalar.copy(values[:, 4 * k:4 * k + 4, 0:H8 * 9].rearrange("p j (h n) -> p j h n", n=9)[:, :, :, 0:DH8],
                           pv[:, k % 2, :].rearrange("p (j h n) -> p j h n", j=4, n=DH8)).then_inc(s.h_vcopied, 1)

    @block.gpsimd
    def _(pool):
        nc.gpsimd.memset(values[:, :, H8 * 9:], 0.0)
        nc.gpsimd.memset(values[:, :, 0:H8 * 9].rearrange("p j (h n) -> p j h n", n=9)[:, :, :, DH8:], 1.0)

    @block.vector
    def _(dve):
        link = Link(dve, s.h_link)
        dve.wait_ge(s.h_in, 48)
        dve.wait_ge(s.h_gates, 4)
        link(nc.vector.tensor_tensor(diag[:], rows[:].rearrange("p b (t n) -> p (b t) n", t=TPB),
                                     c.ident[:].unsqueeze(1).to_broadcast([128, NT, 128]), ALU.mult))
        link(nc.vector.reduce_sum(own[:], diag[:], AX.X))
        shape = [128, B, TPB, S]
        rival = rows[:].unsqueeze(2).to_broadcast(shape)
        mine = own[:].rearrange("p (b t) -> p b t", t=TPB).unsqueeze(3).to_broadcast(shape)
        nc.vector.tensor_tensor(more[:], rival, mine, ALU.is_gt)
        link(nc.vector.tensor_tensor(same[:], rival, mine, ALU.is_equal))
        link(nc.vector.tensor_tensor(same[:], same[:], before[:].unsqueeze(1).to_broadcast(shape), ALU.mult))
        link(nc.vector.tensor_tensor(more[:], more[:], same[:], ALU.add))
        link(nc.vector.reduce_sum(rank[:], more[:].rearrange("p b t n -> p (b t) n"), AX.X))
        nc.vector.tensor_scalar(chosen[:], rank[:], float(CAP), None, ALU.is_lt).then_inc(s.h_chosen, 1)
        dve.wait_ge(s.h_chosen, 1)
        nc.vector.tensor_tensor(gate[:], chosen[:], own[:], ALU.mult)
        dve.wait_ge(s.h_turned, 1)
        nc.vector.tensor_scalar(masked[:], pm[:], 1.0, BIG, ALU.subtract, ALU.mult).then_inc(s.h_masked, 1)


def _l1_core(nc, c, d, values, pieces, mask, ctx):
    s = sems(ctx, nc, "g_init g_rows g_link")

    def sb(n, shape, dt=F32):
        return ctx.enter_context(nc.sbuf_tensor(uniq(f"g_{n}"), shape, dt))
    kaug, qaug = sb("kaug", [ROWS8, H8, B * S], BF16), sb("qaug", [ROWS8, H8, B * S], BF16)
    one_row = sb("one", [1, S], BF16)

    def head(x, at, k0, size):
        return x[:, at.h, bass.ds(at.b * S + k0, size)]
    cfg = Cfg()
    cfg.heads, cfg.loop, cfg.scale = H8, False, DH8 ** -0.5
    cfg.chunks, cfg.groups, cfg.keys = [(0, S)], [(0, 1), (1, 1)], lambda j: 128
    cfg.row, cfg.rows, cfg.row_dt = ROW_SHIFT, 2, BF16
    cfg.max_q = lambda at, t: head(qaug, at, 128 * t, 128)
    cfg.max_k = lambda at, k0, size: head(kaug, at, k0, size)
    cfg.score_k = lambda at, j: head(kaug, at, 128 * j, 128)
    cfg.score_q = lambda at: head(qaug, at, 0, S)
    cfg.shift_rows = lambda at: qaug[ROW_SHIFT:ROW_SHIFT + 2, at.h, bass.ds(at.b * S, S)]
    cfg.value = lambda at, j: stage[:, j, 9 * at.h:9 * at.h + 32]
    stage = sb("stage", [128, TPB, VCOLS])
    sv = sems(ctx, nc, "g_staged")
    core = Core(nc, ctx, c, cfg)
    strips = Strips(nc, ctx, c, core, TPB)
    block = ctx.enter_context(nc.Block())

    @block.gpsimd
    def _(pool):
        link = Link(pool, s.g_init)
        link(nc.gpsimd.memset(kaug[32:64, :, :], 0.0))
        link(nc.gpsimd.memset(qaug[32:64, :, :], 0.0))
        link(nc.gpsimd.memset(kaug[64:66, :, :], 1.0))
        link(nc.gpsimd.memset(qaug[64:66, :, :], 0.0))
        link(nc.gpsimd.memset(one_row[:], 1.0))
        link(nc.gpsimd.memset(strips.product[64:128, :, :], 0.0))
        link(nc.gpsimd.memset(core.shift_cols[:], 0.0))

    N_ROWS = 12 + 1 + B

    @block.sync
    def _(sp):
        sp.wait_ge(s.g_init, 7)
        for aug, src, order in ((kaug, pieces[1], K_PIECES), (qaug, pieces[0], Q_PIECES)):
            for x, y in enumerate(order):
                sp.dma_start(aug[8 * x:8 * x + 8, :, :], src[y].rearrange("(h e) n -> e h n", e=DH8)).then_inc(s.g_rows, 16)
        sp.dma_start(kaug[ROW_MASK:ROW_MASK + 1, :, :],
                     mask.rearrange("n t -> (n t)").unsqueeze(0).unsqueeze(0).to_broadcast([1, H8, B * S])) \
            .then_inc(s.g_rows, 16)
        for b in range(B):
            sp.dma_start(qaug[ROW_MASK:ROW_MASK + 1, :, b * S:(b + 1) * S],
                         one_row[:].unsqueeze(1).to_broadcast([1, H8, S])).then_inc(s.g_rows, 16)

    @block.tensor
    def _(pe):
        strips.begin_pe(pe)
        pe.wait_ge(s.g_init, 7)
        pe.wait_ge(s.g_rows, 16 * N_ROWS)

        def first(at):
            core.pe_max(pe, at, range(2 * core.NCH))
            strips.pe_turn_free(pe, at.b)
            core.pe_turn(pe, at)
        with pe.Fori(0, B // 2) as i:
            for p in range(2):
                pe.wait_ge(sv.g_staged, 2 * i + p + 1)
                core.heads(pe, p, i, first, lambda at, nxt, is_first: core.pe_step(pe, at, nxt))
                strips.pe(pe, 2 * i + p)

    @block.scalar
    def _(act):
        core.begin_act(act)
        with act.Fori(0, B // 2) as i:
            for p in range(2):
                strips.act(act, p, i, 2 * i + p)

    @block.vector
    def _(dve):
        strips.begin_dve(dve)
        dve.wait_ge(s.g_init, 7)
        with dve.Fori(0, B // 2) as i:
            for p in range(2):
                b = 2 * i + p
                dve.wait_ge(core.s.values_used, b * H8 * core.NG + 2)
                nc.vector.tensor_copy(stage[:], values[:, bass.ds(TPB * b, TPB), :]).then_inc(sv.g_staged, 1)
                strips.dve(dve, p, i, b)


def _l1_out(nc, c, d, gate, ctx):
    s = sems(ctx, nc, "j_w j_gated j_made j_added")
    wo = ctx.enter_context(nc.sbuf_tensor(uniq("j_w_t"), [128, D], F32))
    factor = ctx.enter_context(nc.sbuf_tensor(uniq("j_factor"), [128, NT], F32))
    py = ctx.enter_context(nc.psum_tensor(uniq("j_py"), [128, 4, 512], F32))
    block = ctx.enter_context(nc.Block())

    @block.sync
    def _(sp):
        sp.dma_start(wo[:], d["m_Wo"]).then_inc(s.j_w, 16)

    @block.tensor
    def _(pe):
        pe.wait_ge(s.j_w, 16)
        for n in range(NT):
            if n >= 4:
                pe.wait_ge(s.j_added, n - 3)
            nc.tensor.matmul(py[:, n % 4, 0:D], c.xnT[:, 128 * n:128 * n + 128], wo[:], start=True,
                             stop=True).then_inc(s.j_made, 1)

    @block.vector
    def _(dve):
        nc.vector.tensor_scalar(factor[:], gate[:], c.tanh_g[:, 5:6], None, ALU.mult).then_inc(s.j_gated, 1)
        dve.wait_ge(s.j_gated, 1)
        for n in range(NT):
            dve.wait_ge(s.j_made, n + 1)
            nc.vector.scalar_tensor_tensor(out=c.x_res[:, n, :], in0=py[:, n % 4, 0:D], scalar=factor[:, n:n + 1],
                                           in1=c.x_res[:, n, :], op0=ALU.mult, op1=ALU.add).then_inc(s.j_added, 1)


H3, DH3 = 2, 64
S3 = S + SC
KT3 = TPB + KT
GROUPS3 = [(0, 4), (4, 4), (8, 4), (12, 2), (14, 1)]
CHUNKS3 = [(0, 465), (465, 464), (929, 464), (1393, 464)]
R_ONE, R_MASK = DH3, DH3 + 1


def rows3(j):
    return KL if j == KT3 - 1 else 128


def l3_attention(nc, c, d):
    with ExitStack() as ctx:
        def sb(name, shape, dt=F32):
            return ctx.enter_context(nc.sbuf_tensor(uniq(name), shape, dt))
        qf, qb = sb("y_qf", [DH3 + 2, B, H3, S]), sb("y_qb", [DH3 + 1, B, H3, S], BF16)
        kv_own = sb("y_kvown", [128, NT, 2, H3, DH3])
        mask_rows = nc.dram_tensor("y_mask", (B, S3), F32, kind="Internal").ap()
        gains = sb("y_gains", [128, 2 * DC + 2 * D + 2 * DH3])
        w_all = sb("y_wall", [D, 3 * 128])
        w_kv = sb("y_wkv", [DC, 2 * 128])
        w_o = sb("y_wo", [DH3 + 1, H3, D + 1])
        bo = sb("y_bo", [1, D])
        at, views = 0, []
        for n in (DC, DC, D, D, DH3, DH3):
            views.append(gains[:, at:at + n])
            at += n
        gx, bx, gl, bl, gq, gk = views
        with ExitStack() as cx:
            _l3_load(nc, c, d, gains, w_all, w_kv, w_o, bo, mask_rows, cx)
        layer_norm(nc, c, c.xn, c.xn, c.xnT, gl, bl)
        with ExitStack() as cx:
            _l3_own(nc, c, w_all, gq, qf, qb, kv_own, cx)
        with ExitStack() as cx:
            _l3_core(nc, c, d, qf, qb, kv_own, mask_rows, gx, bx, gk, w_kv, cx)
        with ExitStack() as cx:
            heads_out(nc, c, qf, w_o, bo, cx, DH3, H3, 3)


def _l3_load(nc, c, d, gains, w_all, w_kv, w_o, bo, mask_rows, ctx):
    s = sems(ctx, nc, "y_in y_m y_masked y_mout")
    m32 = ctx.enter_context(nc.sbuf_tensor(uniq("y_m32"), [B, -(-SC // 4)], mybir.dt.int32))
    mf = ctx.enter_context(nc.sbuf_tensor(uniq("y_mf"), [B, S3], F32))
    block = ctx.enter_context(nc.Block())

    @block.sync
    def _(sp):
        sp.dma_start(m32[:], d["mask"]).then_inc(s.y_m, 16)
        sp.dma_start(gains[:], d["y_gains"].partition_broadcast(128)).then_inc(s.y_in, 16)
        for dst, src in ((w_all, "y_wall"), (w_kv, "y_wkv"), (w_o, "y_wo"), (bo, "y_bo")):
            sp.dma_start(dst[:], d[src]).then_inc(s.y_in, 16)
        sp.wait_ge(s.y_masked, 2)
        sp.dma_start(mask_rows, mf[:]).then_inc(s.y_mout, 16)
        sp.wait_ge(s.y_mout, 16)
        sp.wait_ge(s.y_in, 80)

    @block.vector
    def _(dve):
        nc.vector.memset(mf[:, 0:S], 0.0).then_inc(s.y_masked, 1)
        dve.wait_ge(s.y_m, 16)
        nc.vector.tensor_scalar(mf[:, S:S3], m32[:].bitcast(U8)[:, 0:SC], 1.0, BIG, ALU.subtract, ALU.mult).then_inc(s.y_masked, 1)


def _l3_own(nc, c, w_all, gq, qf, qb, kv_own, ctx):
    s = sems(ctx, nc, "z_made z_copied z_link z_ss z_root z_q z_turned z_qf z_init")

    def sb(name, shape, dt=F32):
        return ctx.enter_context(nc.sbuf_tensor(uniq(name), shape, dt))
    q, sq, ss, root = sb("z_q_t", [128, NT, H3, DH3]), sb("z_sq", [128, NT, H3, DH3]), sb("z_ss_t", [128, NT * H3]), sb("z_r", [128, NT * H3])
    ps = ctx.enter_context(nc.psum_tensor(uniq("z_ps"), [128, 4, 512], F32))
    pt = ctx.enter_context(nc.psum_tensor(uniq("z_pt"), [128, 4, 512], F32))
    block = ctx.enter_context(nc.Block())

    @block.tensor
    def _(pe):
        for n in range(NT):
            if n >= 4:
                pe.wait_ge(s.z_copied, 2 * (n - 3))
            nc.tensor.matmul(ps[:, n % 4, 0:384], c.xnT[:, 128 * n:128 * n + 128], w_all[:], start=True,
                             stop=True).then_inc(s.z_made, 1)
        pe.wait_ge(s.z_q, 1)
        for b in range(B):
            if b >= 4:
                pe.wait_ge(s.z_qf, b - 3)
            for t in range(TPB):
                for h in range(H3):
                    ins = nc.tensor.transpose(pt[0:DH3, b % 4, h * S + 128 * t:h * S + 128 * t + 128],
                                              q[:, 2 * b + t, h, :], c.ident[:])
            ins.then_inc(s.z_turned, 1)

    @block.scalar
    def _(act):
        for n in range(NT):
            act.wait_ge(s.z_made, n + 1)
            nc.scalar.copy(q[:, n, :, :].rearrange("p h n -> p (h n)"), ps[:, n % 4, 0:128]).then_inc(s.z_copied, 1)
            nc.scalar.copy(kv_own[:, n, :, :, :].rearrange("p a h n -> p (a h n)"), ps[:, n % 4, 128:384]).then_inc(s.z_copied, 1)
        act.wait_ge(s.z_init, 2)
        for b in range(B):
            act.wait_ge(s.z_turned, b + 1)
            nc.scalar.copy(qf[0:DH3, b, :, :].rearrange("p h t -> p (h t)"), pt[0:DH3, b % 4, :]).then_inc(s.z_qf, 1)

    @block.gpsimd
    def _(pool):
        nc.gpsimd.memset(qf[DH3:DH3 + 2, :, :, :], 1.0).then_inc(s.z_init, 1)
        pool.wait_ge(s.z_init, 1)
        nc.gpsimd.memset(qb[DH3:DH3 + 1, :, :, :], 1.0).then_inc(s.z_init, 1)
        pool.wait_ge(s.z_init, 2)
        pool.wait_ge(s.z_ss, 1)
        nc.gpsimd.tensor_tensor(root[:], ss[:], c.neg_half[:, 0:NT * H3], ALU.pow).then_inc(s.z_root, 1)

    @block.vector
    def _(dve):
        link = Link(dve, s.z_link)
        flat = q[:].rearrange("p n h e -> p (n h) e")
        dve.wait_ge(s.z_copied, 2 * NT)
        link(nc.vector.tensor_tensor(sq[:], q[:], q[:], ALU.mult))
        link(nc.vector.reduce_sum(ss[:], sq[:].rearrange("p n h e -> p (n h) e"), AX.X))
        nc.vector.tensor_scalar(ss[:], ss[:], 1.0 / DH3, None, ALU.mult).then_inc(s.z_ss, 1)
        dve.wait_ge(s.z_root, 1)
        link(nc.vector.tensor_scalar(root[:], root[:], 1e8, None, ALU.min))
        link(nc.vector.tensor_tensor(flat, flat, bcast(root[:], [128, NT * H3, DH3]), ALU.mult))
        nc.vector.tensor_tensor(flat, flat, gq.unsqueeze(1).to_broadcast([128, NT * H3, DH3]), ALU.mult).then_inc(s.z_q, 1)
        for b in range(B):
            dve.wait_ge(s.z_qf, b + 1)
            nc.vector.tensor_copy(qb[0:DH3, b, :, :], qf[0:DH3, b, :, :])


def _l3_core(nc, c, d, qf, qb, kv_own, mask_rows, gx, bx, gk, w_kv, ctx):
    s = sems(ctx, nc, "x_ctx x_mask x_init x_sq x_link x_var x_rstd x_normed x_turned x_xT x_kv x_kvcopied "
                      "x_ss x_root x_k x_kturned x_kT x_kb x_batch x_out x_ksq")

    def sb(name, shape, dt=F32):
        return ctx.enter_context(nc.sbuf_tensor(uniq(name), shape, dt))
    raw = sb("x_raw", [128, KT, DC + 1])
    xc, sq = sb("x_xc", [128, KT, DC]), sb("x_sq_t", [128, KT3 * H3, DH3])
    stat = sb("x_stat", [128, 4, KT])
    xT = sb("x_xT_t", [DC, KT * 128])
    k = sb("x_k_t", [128, KT3, H3, DH3])
    v = sb("x_v", [128, KT3, H3, DH3 + 1])
    ss, root = sb("x_ss_t", [128, KT3 * H3]), sb("x_root_t", [128, KT3 * H3])
    kT, kb = sb("x_kT_t", [DH3 + 2, H3, KT3 * 128]), sb("x_kb_t", [DH3 + 1, H3, S3], BF16)
    mrow = sb("x_mrow", [DH3 + 1, S3])
    cfg = Cfg()
    cfg.heads, cfg.loop, cfg.parities, cfg.scale = H3, False, 1, DH3 ** -0.5
    cfg.chunks, cfg.groups, cfg.keys = CHUNKS3, GROUPS3, rows3
    cfg.row, cfg.rows, cfg.row_dt = R_ONE, 1, F32
    cfg.max_q = lambda at, t: qb[:, bass.ds(at.b, 1), at.h, 128 * t:128 * t + 128].rearrange("p b t -> p (b t)")
    cfg.max_k = lambda at, k0, size: kb[:, at.h, k0:k0 + size]
    cfg.score_k = lambda at, j: kT[:, at.h, 128 * j:128 * j + rows3(j)]
    cfg.score_q = lambda at: qf[:, bass.ds(at.b, 1), at.h, :].rearrange("p b t -> p (b t)")
    cfg.shift_rows = lambda at: qf[R_ONE:R_ONE + 1, bass.ds(at.b, 1), at.h, :].rearrange("p b t -> p (b t)")
    cfg.value = lambda at, j: v[0:rows3(j), j, at.h, :]
    core = Core(nc, ctx, c, cfg)
    cfg.strips = 1
    cfg.out = lambda at, j: core.ps_out[0:DH3 + 1, 0:S]
    cfg.out_copied = s.x_out
    banks = core.ps_scores[:].rearrange("p a (x n) -> p (a x) n", n=512)
    NKV = -(-KT // 2)
    tiles4 = [range(4 * x, min(4 * x + 4, KT)) for x in range(4)]
    tiles3 = [range(4 * x, min(4 * x + 4, KT3)) for x in range(4)]
    block = ctx.enter_context(nc.Block())

    @block.sync
    def _(sp):
        sp.wait_ge(s.x_init, 1)
        for b in range(B):
            if b:
                sp.wait_ge(s.x_normed, b)
            sp.dma_start(raw[:], d["ctx_tok"][b]).then_inc(s.x_ctx, 16)
            if b:
                sp.wait_ge(s.x_batch, b)
            sp.dma_start(mrow[DH3:DH3 + 1, :], mask_rows[b:b + 1, :]).then_inc(s.x_mask, 16)
            for h in range(H3):
                sp.dma_start(kT[R_MASK:R_MASK + 1, h, 0:S3], mask_rows[b:b + 1, :]).then_inc(s.x_mask, 16)

    @block.gpsimd
    def _(pool):
        link = Link(pool, s.x_init)
        link(nc.gpsimd.memset(kT[DH3:DH3 + 2, :, :], 1.0))
        link(nc.gpsimd.memset(v[:, :, :, DH3:DH3 + 1], 1.0))
        link(nc.gpsimd.memset(core.shift_cols[:], 0.0))
        with pool.Fori(0, B) as b:
            pool.wait_ge(s.x_var, b + 1)
            nc.gpsimd.tensor_tensor(stat[:, 3, :], stat[:, 2, :], c.neg_half[:, 0:KT], ALU.pow).then_inc(s.x_rstd, 1)
            pool.wait_ge(s.x_ss, b + 1)
            nc.gpsimd.tensor_tensor(root[:], ss[:], c.neg_half[:, 0:KT3 * H3], ALU.pow).then_inc(s.x_root, 1)

    @block.tensor
    def _(pe):
        core.begin_pe(pe)
        pe.wait_ge(s.x_init, 3)

        def first(at):
            core.pe_max(pe, at, range(2 * core.NCH))
            core.pe_turn(pe, at)
        with pe.Fori(0, B) as b:
            pe.wait_ge(core.s.exp_done, b * H3 * core.NG + 2)
            pe.wait_ge(s.x_normed, b + 1)
            for x in range(4):
                for y, j in enumerate(tiles4[x]):
                    ins = nc.tensor.transpose(banks[0:DC, x, 128 * y:128 * y + 128], xc[:, j, :], c.ident[:])
                ins.then_inc(s.x_turned, 1)
            for x in range(NKV):
                if x < 4:
                    pe.wait_ge(s.x_xT, 4 * b + 4)
                else:
                    pe.wait_ge(s.x_kvcopied, 2 * (NKV * b + x - 3))
                for y, j in enumerate(range(2 * x, min(2 * x + 2, KT))):
                    ins = nc.tensor.matmul(banks[:, x % 4, 256 * y:256 * y + 256], xT[:, 128 * j:128 * j + 128], w_kv[:],
                                           start=True, stop=True)
                ins.then_inc(s.x_kv, 1)
            pe.wait_ge(s.x_k, b + 1)
            for x in range(4):
                for y, j in enumerate(tiles3[x]):
                    ins = nc.tensor.transpose(banks[:, x, 128 * y:128 * y + 128],
                                              k[:, j, :, :].rearrange("p h e -> p (h e)"), c.ident[:])
                ins.then_inc(s.x_kturned, 1)
            pe.wait_ge(s.x_mask, 48 * (b + 1))
            pe.wait_ge(s.x_kT, 8 * (b + 1))
            pe.wait_ge(s.x_kb, b + 1)
            core.heads(pe, 0, b, first, lambda at, nxt, is_first: core.pe_step(pe, at, nxt))

    @block.scalar
    def _(act):
        core.begin_act(act)
        act.wait_ge(s.x_init, 3)

        def copy_out(n, b, h):
            act.wait_ge(core.s.values_used, (n + 1) * core.NG + 2)
            nc.scalar.copy(qf[0:DH3 + 1, bass.ds(b, 1), h, :].rearrange("p b t -> p (b t)"),
                           core.ps_out[0:DH3 + 1, 0:S]).then_inc(s.x_out, 1)

        def step(at, nxt, is_first):
            core.act_exp(act, at, range(0, 1))
            if not is_first:
                copy_out(at.n - 1, at.b, at.h - 1)
            core.act_exp(act, at, range(1, core.NG))
        with act.Fori(0, B) as b:
            nc.scalar.copy(k[:, 0:TPB, :, :], kv_own[:, bass.ds(TPB * b, TPB), 0, :, :])
            nc.scalar.copy(v[:, 0:TPB, :, 0:DH3], kv_own[:, bass.ds(TPB * b, TPB), 1, :, :])
            act.wait_ge(s.x_sq, 2 * b + 1)
            nc.scalar.activation(sq[:].rearrange("p a e -> p (a e)")[:, 0:KT * DC].rearrange("p (j n) -> p j n", j=KT),
                                 xc[:], ACT.Square).then_inc(s.x_sq, 1)
            for x in range(4):
                act.wait_ge(s.x_turned, 4 * b + x + 1)
                n = 128 * len(tiles4[x])
                nc.scalar.copy(xT[:, 512 * x:512 * x + n], banks[0:DC, x, 0:n]).then_inc(s.x_xT, 1)
            for x in range(NKV):
                act.wait_ge(s.x_kv, NKV * b + x + 1)
                n = min(2, KT - 2 * x)
                both = banks[:, x % 4, 0:256 * n].rearrange("p (j a h e) -> p j a h e", j=n, a=2, h=H3)
                j = slice(TPB + 2 * x, TPB + 2 * x + n)
                nc.scalar.copy(k[:, j, :, :].rearrange("p j h e -> p j (h e)"),
                               both[:, :, 0, :, :].rearrange("p j h e -> p j (h e)")).then_inc(s.x_kvcopied, 1)
                nc.scalar.copy(v[:, j, :, 0:DH3], both[:, :, 1, :, :]).then_inc(s.x_kvcopied, 1)
            act.wait_ge(s.x_kvcopied, 2 * NKV * (b + 1))
            nc.scalar.activation(sq[:], k[:].rearrange("p j h e -> p (j h) e"), ACT.Square).then_inc(s.x_ksq, 1)
            for x in range(4):
                act.wait_ge(s.x_kturned, 4 * b + x + 1)
                n = 128 * len(tiles3[x])
                for h in range(H3):
                    nc.scalar.copy(kT[0:DH3, h, 512 * x:512 * x + n],
                                   banks[DH3 * h:DH3 * h + DH3, x, 0:n]).then_inc(s.x_kT, 1)
            core.heads(act, 0, b, None, step)
            copy_out(H3 * b + 1, b, 1)
            act.sem_inc(s.x_batch, 1)

    @block.vector
    def _(dve):
        core.begin_dve(dve)
        dve.wait_ge(s.x_init, 3)
        link = Link(dve, s.x_link)
        with dve.Fori(0, B) as b:
            link.enter(b, 9)
            dve.wait_ge(s.x_ctx, 16 * (b + 1))
            link(nc.vector.reduce_sum(stat[:, 0, :], raw[:, :, 0:DC], AX.X))
            link(nc.vector.tensor_scalar(stat[:, 0, :], stat[:, 0, :], 1.0 / DC, None, ALU.mult))
            nc.vector.tensor_tensor(xc[:], raw[:, :, 0:DC], bcast(stat[:, 0, :], [128, KT, DC]), ALU.subtract).then_inc(s.x_sq, 1)
            dve.wait_ge(s.x_sq, 2 * b + 2)
            link(nc.vector.reduce_sum(stat[:, 1, :], sq[:].rearrange("p a e -> p (a e)")[:, 0:KT * DC]
                                      .rearrange("p (j n) -> p j n", j=KT), AX.X))
            nc.vector.tensor_scalar(stat[:, 2, :], stat[:, 1, :], 1.0 / DC, EPS, ALU.mult, ALU.add).then_inc(s.x_var, 1)
            dve.wait_ge(s.x_rstd, b + 1)
            link(nc.vector.tensor_tensor(xc[:], xc[:], bcast(stat[:, 3, :], [128, KT, DC]), ALU.mult))
            link(nc.vector.tensor_tensor(xc[:], xc[:], gx.unsqueeze(1).to_broadcast([128, KT, DC]), ALU.mult))
            nc.vector.tensor_tensor(xc[:], xc[:], bx.unsqueeze(1).to_broadcast([128, KT, DC]), ALU.add).then_inc(s.x_normed, 1)
            dve.wait_ge(s.x_ksq, b + 1)
            link(nc.vector.reduce_sum(ss[:], sq[:], AX.X))
            nc.vector.tensor_scalar(ss[:], ss[:], 1.0 / DH3, None, ALU.mult).then_inc(s.x_ss, 1)
            dve.wait_ge(s.x_root, b + 1)
            link(nc.vector.tensor_scalar(root[:], root[:], 1e8, None, ALU.min))
            flat = k[:].rearrange("p j h e -> p (j h) e")
            link(nc.vector.tensor_tensor(flat, flat, bcast(root[:], [128, KT3 * H3, DH3]), ALU.mult))
            nc.vector.tensor_tensor(flat, flat, gk.unsqueeze(1).to_broadcast([128, KT3 * H3, DH3]), ALU.mult).then_inc(s.x_k, 1)
            dve.wait_ge(s.x_mask, 48 * (b + 1))
            for h in range(H3):
                nc.vector.tensor_copy(kb[DH3:DH3 + 1, h, :], mrow[DH3:DH3 + 1, :])
            dve.wait_ge(s.x_kT, 8 * (b + 1))
            link(nc.vector.tensor_copy(kb[0:DH3, :, :], kT[0:DH3, :, 0:S3]))
            dve.sem_inc(s.x_kb, 1)
            link.leave(B)
            core.heads(dve, 0, b, lambda at: core.dve_max(dve, at, None),
                       lambda at, nxt, is_first: core.dve_max(dve, nxt, None) if nxt is not None else None)


E3, I3, K3 = 32, 512, 8
NJ3 = I3 // 128


def l3_ffn(nc, c, d):
    with ExitStack() as ctx:
        def sb(name, shape, dt=F32):
            return ctx.enter_context(nc.sbuf_tensor(uniq(name), shape, dt))
        s = sems(ctx, nc, "w_in w_w1a w_w1b w_w2a w_w2b w_logit w_biased w_link w_exp w_top w_parts w_aT w_aTcopied w_mix "
                          "w_mixcopied w_h w_hbias w_gelu w_o w_ocopied w_oT w_oTcopied w_y w_ycopied")
        gate, gate_b = sb("w_gate", [D, E3]), sb("w_gateb", [E3, 1])
        b1, b2 = sb("w_b1", [128, NJ3, E3]), sb("w_b2", [D, E3])
        w1, w2 = sb("w_w1", [128, 2, I3]), sb("w_w2", [128, 2, NJ3, D])
        logits = sb("w_logits", [E3, B, S])
        probs, rest, parts = sb("w_probs", [E3, B, S]), sb("w_rest", [E3, B, S]), sb("w_parts_t", [E3, B, S])
        top = sb("w_top_t", [E3, B, K3])
        stat = sb("w_stat", [E3, 4, B])
        aT = sb("w_aT_t", [128, NT, E3])
        mixed = sb("w_mixed", [D, E3, B])
        hidden = sb("w_hid", [128, NJ3, E3, B])
        hact = sb("w_hact", [128, NJ3, E3, B])
        oT, o = sb("w_oT_t", [D, E3, B]), sb("w_o_t", [E3, B, D])
        ps = ctx.enter_context(nc.psum_tensor(uniq("w_ps"), [128, 4, 512], F32))
        ph = ctx.enter_context(nc.psum_tensor(uniq("w_ph"), [128, 2, 512], F32))
        po = ctx.enter_context(nc.psum_tensor(uniq("w_po"), [128, 512], F32))
        pa = ctx.enter_context(nc.psum_tensor(uniq("w_pa"), [128, 512], F32))
        phv = ph[:].rearrange("p x (y e b) -> p (x y) e b", y=2, e=E3)
        pov = po[:, 0:E3 * B].rearrange("p (e b) -> p e b", b=B)
        w_sems = [[s.w_w1a, s.w_w1b], [s.w_w2a, s.w_w2b]]
        block = ctx.enter_context(nc.Block())

        @block.sync
        def _(sp):
            for dst, src in ((gate, "w_gate"), (gate_b, "w_gateb"), (b1, "w_b1"), (b2, "w_b2")):
                sp.dma_start(dst[:], d[src]).then_inc(s.w_in, 16)
            for e in range(E3):
                if e >= 2:
                    sp.wait_ge(s.w_h, e - 1)
                sp.dma_start(w1[:, e % 2, :], d["w_w1"][e]).then_inc(w_sems[0][e % 2], 16)
            for e in range(E3):
                if e >= 2:
                    sp.wait_ge(s.w_o, e - 1)
                sp.dma_start(w2[:, e % 2, :, :], d["w_w2"][e]).then_inc(w_sems[1][e % 2], 16)

        @block.tensor
        def _(pe):
            pe.wait_ge(s.w_in, 64)
            for k in range(4):
                nc.tensor.matmul(ps[0:E3, k, :], gate[:], c.xnT[:, 512 * k:512 * k + 512], start=True,
                                 stop=True).then_inc(s.w_logit, 1)
            pe.wait_ge(s.w_parts, 1)
            for n in range(NT):
                ins = nc.tensor.transpose(pa[:, E3 * n:E3 * n + E3], parts[:, n // 2, 128 * (n % 2):128 * (n % 2) + 128],
                                          c.ident[0:E3, 0:E3])
            ins.then_inc(s.w_aT, 1)
            pe.wait_ge(s.w_aTcopied, 1)
            for b in range(B):
                for t in range(TPB):
                    n = TPB * b + t
                    ins = nc.tensor.matmul(po[:, E3 * b:E3 * b + E3], c.xn[:, n, :], aT[:, n, :], start=(t == 0), stop=(t == 1))
            ins.then_inc(s.w_mix, 1)
            pe.wait_ge(s.w_mixcopied, 1)
            for e in range(E3):
                pe.wait_ge(w_sems[0][e % 2], 16 * (e // 2 + 1))
                for j in range(NJ3):
                    ins = nc.tensor.matmul(phv[:, j, e, :], w1[:, e % 2, 128 * j:128 * j + 128], mixed[:, e, :],
                                           start=True, stop=True)
                ins.then_inc(s.w_h, 1)
            pe.wait_ge(s.w_gelu, 1)
            for e in range(E3):
                pe.wait_ge(w_sems[1][e % 2], 16 * (e // 2 + 1))
                for j in range(NJ3):
                    ins = nc.tensor.matmul(pov[:, e, :], w2[:, e % 2, j, :], hact[:, j, e, :], start=(j == 0), stop=(j == NJ3 - 1))
                ins.then_inc(s.w_o, 1)
            pe.wait_ge(s.w_ocopied, 1)
            for b in range(B):
                ins = nc.tensor.transpose(ps[0:E3, b // 4, 128 * (b % 4):128 * (b % 4) + 128], oT[:, :, b], c.ident[:])
            ins.then_inc(s.w_oT, 1)
            pe.wait_ge(s.w_oTcopied, 1)
            for n in range(NT):
                if n >= 2:
                    pe.wait_ge(s.w_ycopied, n - 1)
                nc.tensor.matmul(ps[:, 2 + n % 2, 0:D], parts[:, n // 2, 128 * (n % 2):128 * (n % 2) + 128], o[:, n // 2, :],
                                 start=True, stop=True).then_inc(s.w_y, 1)

        @block.scalar
        def _(act):
            act.wait_ge(s.w_in, 64)
            for k in range(4):
                act.wait_ge(s.w_logit, k + 1)
                nc.scalar.activation(logits[:, 2 * k:2 * k + 2, :], ps[0:E3, k, :].rearrange("p (b t) -> p b t", b=2),
                                     ACT.Identity, bias=gate_b[:]).then_inc(s.w_biased, 1)
            act.wait_ge(s.w_link, 2)
            nc.scalar.activation(probs[:], logits[:], ACT.Exp).then_inc(s.w_exp, 1)
            act.wait_ge(s.w_hbias, 1)
            nc.scalar.activation(hact[:], hidden[:], ACT.Gelu).then_inc(s.w_gelu, 1)

        @block.vector
        def _(dve):
            link = Link(dve, s.w_link)
            dve.wait_ge(s.w_biased, 4)
            link(nc.vector.reduce_max(stat[:, 0, :], logits[:], AX.X))
            link(nc.vector.tensor_tensor(logits[:], logits[:], bcast(stat[:, 0, :], [E3, B, S]), ALU.subtract))
            dve.wait_ge(s.w_exp, 1)
            link(nc.vector.reduce_sum(stat[:, 1, :], probs[:], AX.X))
            link(nc.vector.reciprocal(stat[:, 2, :], stat[:, 1, :]))
            link(nc.vector.tensor_tensor(probs[:], probs[:], bcast(stat[:, 2, :], [E3, B, S]), ALU.mult))
            for b in range(B):
                ins = nc.vector.max(top[:, b, :], probs[:, b, :])
            link(ins)
            for b in range(B):
                ins = nc.vector.match_replace(rest[:, b, :], top[:, b, :], probs[:, b, :], -1.0)
            link(ins)
            nc.vector.scalar_tensor_tensor(out=parts[:], in0=rest[:], scalar=0.0, in1=probs[:], op0=ALU.is_lt,
                                           op1=ALU.mult).then_inc(s.w_parts, 1)
            dve.wait_ge(s.w_aT, 1)
            nc.vector.tensor_copy(aT[:].rearrange("p n e -> p (n e)"), pa[:]).then_inc(s.w_aTcopied, 1)
            dve.wait_ge(s.w_mix, 1)
            nc.vector.tensor_copy(mixed[:], po[:, 0:E3 * B].rearrange("p (b e) -> p e b", b=B)).then_inc(s.w_mixcopied, 1)
            dve.wait_ge(s.w_h, E3)
            for j in range(NJ3):
                ins = nc.vector.tensor_tensor(hidden[:, j, :, :], phv[:, j, :, :], bcast(b1[:, j, :], [128, E3, B]), ALU.add)
            ins.then_inc(s.w_hbias, 1)
            dve.wait_ge(s.w_o, E3)
            nc.vector.tensor_tensor(oT[:], pov, bcast(b2[:], [D, E3, B]), ALU.add).then_inc(s.w_ocopied, 1)
            dve.wait_ge(s.w_oT, 1)
            nc.vector.tensor_copy(o[:].rearrange("p b n -> p (b n)"), ps[0:E3, 0:2, :].rearrange("p x n -> p (x n)")) \
                .then_inc(s.w_oTcopied, 1)
            for n in range(NT):
                dve.wait_ge(s.w_y, n + 1)
                nc.vector.scalar_tensor_tensor(out=c.x_res[:, n, :], in0=ps[:, 2 + n % 2, 0:D], scalar=c.tanh_g[:, 7:8],
                                               in1=c.x_res[:, n, :], op0=ALU.mult, op1=ALU.add).then_inc(s.w_ycopied, 1)


def build(nc, d, stages=None):
    NAMES.clear()
    USED.clear()
    with ExitStack() as ctx:
        c = Chip()
        def sb(name, shape, dt=F32):
            return ctx.enter_context(nc.sbuf_tensor(uniq(name), shape, dt))
        c.x_res = sb("x_res", [128, NT, D])
        c.ident = sb("ident", [128, 128])
        c.ident_b = sb("ident_b", [128, 128], BF16)
        c.ones_row = sb("ones_row", [1, 128])
        c.strip_sum = sb("strip_sum", [128, 32])
        c.neg_half = sb("neg_half", [128, 128])
        c.tanh_g = sb("tanh_g", [128, 8])
        def normed(layer, *more):
            with ExitStack() as cx:
                c.xnT = cx.enter_context(nc.sbuf_tensor(uniq("xnT"), [D, NT * 128], F32))
                with ExitStack() as cy:
                    c.xn = (cx if layer in needs_xn else cy).enter_context(nc.sbuf_tensor(uniq("xn"), [128, NT, D], F32))
                    c.scratch = (cx if layer is l3_attention else cy).enter_context(
                        nc.sbuf_tensor(uniq("scratch"), [128, NT, D], F32))
                    layer_norm(nc, c, c.x_res, c.xn, c.xnT)
                layer(nc, c, d)
        needs_xn = [l2_ffn, l3_attention, l3_ffn]
        todo = [l0_attention, l0_ffn, l1_attention, l1_ffn, l2_attention, l2_ffn, l3_attention, l3_ffn]
        start(nc, c, d)
        for layer in todo[stages or slice(None)]:
            normed(layer)
            clear_semaphores(nc)
        finish(nc, c, d)


def _layouts(inp):
    f = {k: np.asarray(v) for k, v in inp.items()}
    t = {}
    t["x_tok"] = f["x"].reshape(NT, 128, D).transpose(1, 0, 2)
    t["gates"] = np.concatenate([f["g_xattn"], f["g_ffn"]]).reshape(1, 8)
    ctx = f["ctx_768"]
    ones = np.ones((B, SC, 1), np.float32)
    aug = np.concatenate([ctx, ones], 2)
    t["ctxT"] = aug.transpose(0, 2, 1)
    pad = np.concatenate([aug, np.zeros((B, KT * 128 - SC, DC + 1), np.float32)], 1)
    t["ctx_tok"] = pad.reshape(B, KT, 128, DC + 1).transpose(0, 2, 1, 3)
    w = np.zeros((DH0, H0, 4, 128), np.float32)
    w[:, :, 0, :] = f["L0_xattn_Wq"].reshape(D, H0, DH0).transpose(2, 1, 0)
    w[:, :, 1, :DC] = f["L0_xattn_Wk"].reshape(DC, H0, DH0).transpose(2, 1, 0)
    w[:, :, 2, :DC] = f["L0_xattn_Wv"].reshape(DC, H0, DH0).transpose(2, 1, 0)
    w[:, :, 3, :] = f["L0_xattn_Wo"].reshape(H0, DH0, D).transpose(1, 0, 2)
    t["l0_wT"] = w
    for n, src in (("l1", "L1_xattn_"), ("l2", "L2_xattn_")):
        t[f"{n}_Wq"] = f[src + "Wq"]
        t[f"{n}_bq"] = f[src + "bq"].reshape(128, 1)
        t[f"{n}_Wk"] = np.concatenate([f[src + "Wk"], f[src + "bk"].reshape(1, 128)])
        t[f"{n}_Wv"] = np.concatenate([f[src + "Wv"], f[src + "bv"].reshape(1, 128)])
    t["l1_Wo"], t["l1_bo"] = f["L1_xattn_Wo"], f["L1_xattn_bo"].reshape(1, D)
    t["l2_W1"] = f["L2_xattn_W1"].reshape(D, 2, 128)
    t["l2_b1"] = f["L2_xattn_b1"].reshape(2, 128).T
    t["l2_W2"] = f["L2_xattn_W2"].reshape(2, 128, D).transpose(1, 0, 2)
    t["l2_b2"] = f["L2_xattn_b2"].reshape(1, D)
    t["f0_gate"] = f["L0_ffn_gate_w"].T
    t["f0_bias"] = f["L0_ffn_gate_bias"].reshape(1, E0)
    t["before_e"] = np.tril(np.ones((1, E0, E0), np.float32), -1)
    t["before_g"] = np.tril(np.ones((1, NG0, NG0), np.float32), -1)
    nm = E0 // 2 + 1
    w13, w2 = np.zeros((D, nm, 2, 128), np.float32), np.zeros((128, nm, D), np.float32)
    for x, (many, one) in enumerate((("w1", "ws1"), ("w3", "ws3"))):
        w13[:, :nm - 1, x, :] = f["L0_ffn_" + many].reshape(nm - 1, 128, D).transpose(2, 0, 1)
        w13[:, nm - 1, x, :I0] = f["L0_ffn_" + one].T
    w2[:, :nm - 1, :] = f["L0_ffn_w2"].transpose(0, 2, 1).reshape(nm - 1, 128, D).transpose(1, 0, 2)
    w2[:I0, nm - 1, :] = f["L0_ffn_ws2"].T
    t["f0_w13"], t["f0_w2"] = w13, w2
    sel = np.zeros((E0, nm - 1, 128), np.float32)
    for e in range(E0):
        sel[e, e // 2, I0 * (e % 2):I0 * (e % 2) + I0] = 1
    t["f0_sel"] = sel
    t["b_w1"] = f["L2_ffn_w1"].T
    t["b_w2"] = f["L2_ffn_w2"].T.reshape(NJ, 128, D).transpose(1, 0, 2).reshape(128, NJ * D)
    t["b_taps"] = np.concatenate([f["L2_ffn_conv_w"].reshape(HID, 3), f["L2_ffn_conv_b"].reshape(HID, 1)], 1) \
        .reshape(NJ, 128, 4).transpose(1, 0, 2)
    t["m_Wg"] = np.broadcast_to(f["L1_ffn_Wg"], (D, 128))
    for n, src in (("m_q_Wq", "Wq"), ("m_k_Wq", "Wk"), ("m_Wv", "Wv"), ("m_Wo", "Wo")):
        t[n] = f["L1_ffn_" + src]
    t["m_before"] = np.tril(np.ones((S, S), np.float32), -1).reshape(TPB, 128, S).transpose(1, 0, 2)
    t["mask"] = np.pad(f["mask_BxS2_bk0"], ((0, 0), (0, -SC % 4))).view(np.int32)
    t["y_gains"] = np.concatenate([f["L3_xattn_" + n] for n in ("ln_x_g", "ln_x_b", "ln_l_g", "ln_l_b", "qn_g", "kn_g")])[None]
    t["y_wall"] = np.concatenate([f["L3_xattn_Wq"], f["L3_xattn_Wlkv"]]).T
    t["y_wkv"] = f["L3_xattn_Wkv"].T
    wo = np.zeros((DH3 + 1, H3, D + 1), np.float32)
    wo[:DH3, :, :D] = f["L3_xattn_Wo"].T.reshape(H3, DH3, D).transpose(1, 0, 2)
    wo[DH3, :, D] = 1
    t["y_wo"] = wo
    t["y_bo"] = f["L3_xattn_bo"].reshape(1, D)
    t["w_gate"] = f["L3_ffn_gate_w"].T
    t["w_gateb"] = f["L3_ffn_gate_b"].reshape(E3, 1)
    t["w_w1"] = f["L3_ffn_w1"][:, :D, :]
    t["w_b1"] = f["L3_ffn_w1"][:, D, :].reshape(E3, NJ3, 128).transpose(2, 1, 0)
    t["w_w2"] = f["L3_ffn_w2"][:, :I3, :].reshape(E3, NJ3, 128, D).transpose(0, 2, 1, 3)
    t["w_b2"] = f["L3_ffn_w2"][:, I3, :].T
    t["l0_bo"] = f["L0_xattn_bo"].reshape(1, D)
    return {k: np.ascontiguousarray(v) for k, v in t.items()}


def kernel(**inputs):
    import concourse.bacc as _bacc
    from concourse.bass_utils import run_bass_kernel_spmd as _run

    nc = _bacc.Bacc("TRN2", target_bir_lowering=False, num_devices=1)
    arrays = _layouts(inputs)
    d = {n: nc.dram_tensor(f"in_{n}", a.shape, mybir.dt.from_np(a.dtype), kind="ExternalInput").ap()
         for n, a in arrays.items()}
    d["out"] = nc.dram_tensor("out_0_dram", (128, NT, D), F32, kind="ExternalOutput").ap()
    build(nc, d)
    r = _run(nc, [{f"in_{n}": a for n, a in arrays.items()}], core_ids=[0])
    out = np.asarray(r.results[0]["out_0_dram"])
    return np.ascontiguousarray(out.transpose(1, 0, 2).reshape(B, S, D))
```

```python
from collections import namedtuple
from contextlib import ExitStack

import numpy as np

import concourse.bass as bass
from concourse import mybir

ALU = mybir.AluOpType
ACT = mybir.ActivationFunctionType
F32 = mybir.dt.float32
BF16 = mybir.dt.bfloat16
U8 = mybir.dt.uint8
AX = mybir.AxisListType

B, S, D = 8, 256, 128
SC, DC = 1601, 96
NT = B * S // 128
TPB = S // 128
KT = -(-SC // 128)
KL = SC - (KT - 1) * 128
EPS = 1e-5
CHUNKS = [(0, 401), (401, 400), (801, 400), (1201, 400)]
GROUPS = [(0, 4), (4, 4), (8, 4), (12, 1)]


def key_rows(j):
    return KL if j == KT - 1 else 128


class Link:

    def __init__(self, eng, sem):
        self.eng, self.sem, self.base, self.n = eng, sem, 0, 0

    def __call__(self, ins):
        ins.then_inc(self.sem, 1)
        self.n += 1
        self.eng.wait_ge(self.sem, self.base + self.n)

    def enter(self, i, per):
        self.outer = (self.base, self.n)
        self.base, self.n, self.per = self.base + self.n + i * per, 0, per

    def leave(self, rounds):
        assert self.n == self.per, (self.n, self.per)
        base, n = self.outer
        self.base, self.n = base, n + rounds * self.per


class Chip:
    pass


NAMES = {}
USED = []


def uniq(name):
    NAMES[name] = NAMES.get(name, 0) + 1
    return name if NAMES[name] == 1 else f"{name}_{NAMES[name]}"


def sems(ctx, nc, names):
    names = names.split()
    made = [nc.alloc_semaphore(name=uniq(name)) for name in names]
    USED.extend(made)
    return namedtuple("Semaphores", names)(*made)


def clear_semaphores(nc):
    nc.clear_and_free_semaphores(list(USED))
    nc.all_engine_barrier()
    USED.clear()


def bcast(ap, shape):
    return ap.unsqueeze(len(ap.shape)).to_broadcast(shape)


def start(nc, c, d):
    with ExitStack() as ctx:
        s = sems(ctx, nc, "st_x st_gates st_zero st_ident st_negh")
        graw = ctx.enter_context(nc.sbuf_tensor(uniq("graw"), [128, 8], F32))
        block = ctx.enter_context(nc.Block())

        @block.sync
        def _(sp):
            sp.dma_start(c.x_res[:], d["x_tok"]).then_inc(s.st_x, 16)
            sp.dma_start(graw[:], d["gates"].partition_broadcast(128)).then_inc(s.st_gates, 16)
            sp.wait_ge(s.st_x, 16)

        @block.gpsimd
        def _(pool):
            nc.gpsimd.memset(c.ident[:], 0.0).then_inc(s.st_zero, 1)
            nc.gpsimd.memset(c.neg_half[:], -0.5)
            pool.wait_ge(s.st_zero, 1)
            nc.gpsimd.affine_select(out=c.ident[:], in_=c.ident[:], compare_op=ALU.not_equal, fill=1.0,
                                    base=0, pattern=[[-1, 128]], channel_multiplier=1).then_inc(s.st_ident, 1)

        @block.vector
        def _(dve):
            nc.vector.memset(c.ones_row[:], 1.0)
            dve.wait_ge(s.st_ident, 1)
            nc.vector.tensor_copy(c.ident_b[:], c.ident[:])
            nc.vector.reduce_sum(c.strip_sum[:], c.ident[:].rearrange("p (y n) -> p n y", y=4), AX.X)

        @block.scalar
        def _(act):
            act.wait_ge(s.st_gates, 16)
            nc.scalar.activation(c.tanh_g[:], graw[:], ACT.Tanh)


def finish(nc, c, d):
    with ExitStack() as ctx:
        s = sems(ctx, nc, "fin_out")
        block = ctx.enter_context(nc.Block())

        @block.sync
        def _(sp):
            sp.dma_start(d["out"], c.x_res[:]).then_inc(s.fin_out, 16)
            sp.wait_ge(s.fin_out, 16)


def layer_norm(nc, c, src, dst, dstT, gain=None, shift=None):
    with ExitStack() as ctx:
        s = sems(ctx, nc, "ln_link ln_var ln_rstd ln_xn ln_turned ln_copied")
        parts = ctx.enter_context(nc.sbuf_tensor(uniq("ln_parts"), [128, NT, 6], F32))
        stat = ctx.enter_context(nc.sbuf_tensor(uniq("ln_stat"), [128, NT, 2], F32))
        rstd = ctx.enter_context(nc.sbuf_tensor(uniq("ln_rstd_t"), [128, 2, NT], F32))
        turned = ctx.enter_context(nc.psum_tensor(uniq("ln_ps"), [128, 4, 512], F32))
        block = ctx.enter_context(nc.Block())

        @block.vector
        def _(dve):
            link = Link(dve, s.ln_link)
            for n in range(NT):
                ins = nc.vector.bn_stats(parts[:, n, :], src[:, n, :])
            link(ins)
            for n in range(NT):
                ins = nc.vector.bn_aggr(stat[:, n, :], parts[:, n, :])
            link(ins)
            nc.vector.tensor_scalar(rstd[:, 0, :], stat[:, :, 1], EPS, None, ALU.add).then_inc(s.ln_var, 1)
            dve.wait_ge(s.ln_rstd, 1)
            for k in range(4):
                t = slice(4 * k, 4 * k + 4)
                for n in range(4 * k, 4 * k + 4):
                    ins = nc.vector.tensor_scalar(dst[:, n, :], src[:, n, :], stat[:, n, 0:1], rstd[:, 1, n:n + 1],
                                                  ALU.subtract, ALU.mult)
                if gain is not None:
                    link(ins)
                    link(nc.vector.tensor_tensor(dst[:, t, :], dst[:, t, :],
                                                 gain.unsqueeze(1).to_broadcast([128, 4, D]), ALU.mult))
                    ins = nc.vector.tensor_tensor(dst[:, t, :], dst[:, t, :],
                                                  shift.unsqueeze(1).to_broadcast([128, 4, D]), ALU.add)
                ins.then_inc(s.ln_xn, 1)

        @block.gpsimd
        def _(pool):
            pool.wait_ge(s.ln_var, 1)
            nc.gpsimd.tensor_tensor(rstd[:, 1, :], rstd[:, 0, :], c.neg_half[:, 0:NT],
                                    ALU.pow).then_inc(s.ln_rstd, 1)

        @block.tensor
        def _(pe):
            for k in range(4):
                pe.wait_ge(s.ln_xn, k + 1)
                for j in range(4):
                    ins = nc.tensor.transpose(turned[:, k, 128 * j:128 * j + 128], dst[:, 4 * k + j, :],
                                              c.ident[:])
                ins.then_inc(s.ln_turned, 1)

        @block.scalar
        def _(act):
            for k in range(4):
                act.wait_ge(s.ln_turned, k + 1)
                nc.scalar.copy(dstT[:, 512 * k:512 * k + 512], turned[:, k, :])


H0, DH0 = 8, 64


def l0_attention(nc, c, d):
    SCALE = DH0 ** -0.5
    with ExitStack() as ctx:
        def sb(name, shape, dt=F32):
            return ctx.enter_context(nc.sbuf_tensor(uniq(name), shape, dt))
        qp = sb("l0_qp", [DC + 1, B, H0, S])
        qpb = sb("l0_qpb", [DC, B, H0, S], BF16)
        w_vo = sb("l0_wvo", [DC + 1, H0, D + 1])
        bo = sb("l0_bo", [1, D])
        with ExitStack() as cx:
            _l0_project(nc, c, d, qp, qpb, w_vo, bo, cx)
        with ExitStack() as cx:
            _l0_core(nc, c, d, qp, qpb, cx, SCALE)
        with ExitStack() as cx:
            heads_out(nc, c, qp, w_vo, bo, cx, DC, H0, 0)


def _l0_project(nc, c, d, qp, qpb, w_vo, bo, ctx):
    s = sems(ctx, nc, "l0_w l0_wps l0_wcopied l0_qps l0_qcopied")
    wT = ctx.enter_context(nc.sbuf_tensor(uniq("l0_wT"), [DH0, H0, 4, 128], F32))
    w_qk = ctx.enter_context(nc.sbuf_tensor(uniq("l0_wqk"), [D, H0, DC], F32))
    pw = ctx.enter_context(nc.psum_tensor(uniq("l0_pw"), [128, 4, 512], F32))
    pq = ctx.enter_context(nc.psum_tensor(uniq("l0_pq"), [128, 4, 512], F32))
    block = ctx.enter_context(nc.Block())

    @block.sync
    def _(sp):
        sp.dma_start(wT[:], d["l0_wT"]).then_inc(s.l0_w, 16)
        sp.dma_start(bo[:], d["l0_bo"]).then_inc(s.l0_w, 16)
        sp.wait_ge(s.l0_w, 32)

    @block.tensor
    def _(pe):
        pe.wait_ge(s.l0_w, 32)
        for h in range(H0):
            nc.tensor.matmul(pw[:, h // 4, 128 * (h % 4):128 * (h % 4) + DC], wT[:, h, 0, :],
                             wT[:, h, 1, 0:DC], start=True, stop=True)
            ins = nc.tensor.matmul(pw[0:DC, 2 + h // 4, 128 * (h % 4):128 * (h % 4) + 128], wT[:, h, 2, 0:DC],
                                   wT[:, h, 3, :], start=True, stop=True)
        ins.then_inc(s.l0_wps, 1)
        pe.wait_ge(s.l0_wcopied, 1)
        for n in range(4 * H0):
            h, k = n // 4, n % 4
            if n >= 4:
                pe.wait_ge(s.l0_qcopied, n - 3)
            nc.tensor.matmul(pq[0:DC, n % 4, :], w_qk[:, h, :], c.xnT[:, 512 * k:512 * k + 512],
                             start=True, stop=True).then_inc(s.l0_qps, 1)

    @block.scalar
    def _(act):
        act.wait_ge(s.l0_wps, 1)
        for g in range(2):
            nc.scalar.copy(w_vo[0:DC, 4 * g:4 * g + 4, 0:D],
                           pw[0:DC, 2 + g, :].rearrange("p (h n) -> p h n", h=4))
        for n in range(4 * H0):
            h, k = n // 4, n % 4
            act.wait_ge(s.l0_qps, n + 1)
            nc.scalar.copy(qp[0:DC, 2 * k:2 * k + 2, h, :],
                           pq[0:DC, n % 4, :].rearrange("p (b t) -> p b t", b=2)).then_inc(s.l0_qcopied, 1)

    @block.vector
    def _(dve):
        dve.wait_ge(s.l0_wps, 1)
        for g in range(2):
            ins = nc.vector.tensor_copy(w_qk[:, 4 * g:4 * g + 4, :],
                                        pw[:, g, :].rearrange("p (h n) -> p h n", h=4)[:, :, 0:DC])
        ins.then_inc(s.l0_wcopied, 1)
        for h in range(H0):
            dve.wait_ge(s.l0_qcopied, 4 * h + 4)
            nc.vector.tensor_copy(qpb[:, :, h, :], qp[0:DC, :, h, :])

    @block.gpsimd
    def _(pool):
        nc.gpsimd.memset(w_vo[0:DC, :, D:D + 1], 0.0)
        nc.gpsimd.memset(w_vo[DC:DC + 1, :, 0:D], 0.0)
        nc.gpsimd.memset(w_vo[DC:DC + 1, :, D:D + 1], 1.0)


class At:
    def __init__(self, cfg, p, i, h):
        self.p, self.i, self.h = p, i, h
        self.b = cfg.parities * i + p
        self.n = self.b * cfg.heads + h
        self.cfg = cfg

    def ahead(self, k, last):
        cfg, h, p = self.cfg, self.h + k, self.p
        if h < cfg.heads:
            return At(cfg, p, self.i, h)
        if last:
            return None
        return At(cfg, (p + 1) % cfg.parities, self.i + (p + 1) // cfg.parities, h - cfg.heads)


class Core:

    def __init__(self, nc, ctx, c, cfg):
        self.nc, self.cfg, self.c = nc, cfg, c
        self.s = sems(ctx, nc, "max_made max_read max_found max_turned shift_ready "
                               "scores_made exp_done values_used heads_out")
        self.NCH, self.NG = len(cfg.chunks), len(cfg.groups)
        dt = cfg.row_dt
        self.max_cols = ctx.enter_context(nc.sbuf_tensor(uniq("max_cols"), [128, TPB, self.NCH], F32))
        self.neg_max = ctx.enter_context(nc.sbuf_tensor(uniq("neg_max"), [128, TPB], F32))
        self.shift_cols = ctx.enter_context(nc.sbuf_tensor(uniq("shift_cols"), [128, TPB, cfg.row + cfg.rows], dt))
        self.probs = ctx.enter_context(nc.sbuf_tensor(uniq("probs"), [128, 2, 4 * S], F32))
        self.ps_max = ctx.enter_context(nc.psum_tensor(uniq("ps_max"), [128, 2, 512], F32))
        self.ps_scores = ctx.enter_context(nc.psum_tensor(uniq("ps_scores"), [128, 2, 4 * S], F32))
        self.ps_out = ctx.enter_context(nc.psum_tensor(uniq("ps_out"), [128, 512], F32))
        self.ps_turn = ctx.enter_context(nc.psum_tensor(uniq("ps_turn"), [128, 2, 256], F32))
        self.bound, self.limits, self.cs, self.shift_sum = None, None, None, None
        turn = self.ps_turn[:, 0, :]
        if dt != F32:
            turn = turn.bitcast(dt)[:, 0:TPB * 128]
        self.shift_turn = turn.rearrange("p (t q) -> p t q", t=TPB)

    def begin_dve(self, dve):
        dve.sem_inc(self.s.max_read, 2)

    def begin_act(self, act):
        act.sem_inc(self.s.exp_done, 2)

    def begin_pe(self, pe):
        pe.sem_inc(self.s.values_used, 2)
        pe.sem_inc(self.cfg.out_copied, 1)

    def pe_max(self, pe, at, which):
        s, n = self.s, 2 * self.NCH
        for k in which:
            t, chunk = k // self.NCH, k % self.NCH
            k0, size = self.cfg.chunks[chunk]
            pe.wait_ge(s.max_read, at.n * n + k + 1)
            self.nc.tensor.matmul(self.ps_max[:, k % 2, 0:size], self.cfg.max_q(at, t),
                                  self.cfg.max_k(at, k0, size), start=True, stop=True).then_inc(s.max_made, 1)

    def pe_turn(self, pe, at):
        cfg, s = self.cfg, self.s
        pe.wait_ge(s.max_found, at.n + 1)
        ident = self.c.ident if cfg.row_dt == F32 else self.c.ident_b
        for t in range(TPB):
            ins = self.nc.tensor.transpose(self.shift_turn[0:cfg.row + cfg.rows, t, :],
                                           self.shift_cols[:, t, :], ident[:])
        ins.then_inc(s.max_turned, 1)

    def pe_scores(self, pe, at, g):
        cfg, s = self.cfg, self.s
        if g == 0:
            pe.wait_ge(s.shift_ready, at.n + 1)
        pe.wait_ge(s.exp_done, at.n * self.NG + g + 1)
        j0, nj = cfg.groups[g]
        for j in range(j0, j0 + nj):
            ins = self.nc.tensor.matmul(self.ps_scores[0:cfg.keys(j), self.buf(at, g), (j - j0) * S:(j - j0 + 1) * S],
                                        cfg.score_k(at, j), cfg.score_q(at), start=True, stop=True)
        ins.then_inc(s.scores_made, 1)

    def pe_values(self, pe, at, g):
        cfg, s = self.cfg, self.s
        pe.wait_ge(s.exp_done, at.n * self.NG + g + 3)
        if g == 0:
            pe.wait_ge(cfg.out_copied, at.n + 1)
        j0, nj = cfg.groups[g]
        last = cfg.groups[-1][0] + cfg.groups[-1][1] - 1
        for j in range(j0, j0 + nj):
            ins = self.nc.tensor.matmul(cfg.out(at, j), cfg.value(at, j),
                                        self.probs[0:cfg.keys(j), self.buf(at, g), (j - j0) * S:(j - j0 + 1) * S],
                                        start=(j < cfg.strips), stop=(j + cfg.strips > last), skip_group_check=True)
        ins.then_inc(s.values_used, 1)

    def buf(self, at, g):
        return g % 2 if self.NG % 2 == 0 else (at.p * self.cfg.heads + at.h + g) % 2

    def max_chunks(self, slot):
        total, slots = 2 * self.NCH, self.cfg.slots or 2 * self.NG
        return range(total * slot // slots, total * (slot + 1) // slots) if slot < slots else []

    def early(self):
        return self.cfg.early and self.bound is None

    def pe_limits(self, pe, at):
        pe.wait_ge(self.s.shift_ready, at.n + 1)
        self.nc.tensor.matmul(self.ps_turn[:, 1, :], self.shift_sum[:], self.cfg.score_q(at), start=True,
                              stop=True).then_inc(self.cs.limits_made, 1)

    def pe_first(self, pe, at):
        self.pe_max(pe, at, range(2 * self.NCH))
        self.pe_turn(pe, at)
        self.pe_max(pe, at.ahead(1, False), range(2 * self.NCH))

    def pe_heads(self, pe, p, i, last, turn_free=None, next_ready=None):
        H, NG = self.cfg.heads, self.NG
        for h in range(H):
            at = At(self.cfg, p, i, h)
            one, two = at.ahead(1, last), at.ahead(2, last)
            if h == H - 2 and two is not None:
                next_ready(two)
            if self.bound is not None:
                if h == 0:
                    turn_free(pe, at.b)
                self.pe_limits(pe, at)
            for g in range(NG):
                if h or g or not self.early():
                    self.pe_scores(pe, at, g)
                if two is not None:
                    self.pe_max(pe, two, self.max_chunks(2 * g))
                if one is not None and 2 * g == self.cfg.turn_slot:
                    if h == 0 and turn_free is not None:
                        turn_free(pe, at.b)
                    if self.bound is not None:
                        pe.wait_ge(self.cs.limits_read, at.n + 1)
                    self.pe_turn(pe, one)
                if g >= 1:
                    self.pe_values(pe, at, g - 1)
                elif h >= 1:
                    self.pe_values(pe, At(self.cfg, p, i, h - 1), NG - 1)
                if two is not None:
                    self.pe_max(pe, two, self.max_chunks(2 * g + 1))
        self.pe_values(pe, At(self.cfg, p, i, H - 1), NG - 1)

    def dve_reduce(self, dve, at, which):
        cfg, s, nc = self.cfg, self.s, self.nc
        for k in which:
            t, chunk = k // self.NCH, k % self.NCH
            dve.wait_ge(s.max_made, at.n * 2 * self.NCH + k + 1)
            nc.vector.reduce_max(self.max_cols[:, t, chunk:chunk + 1], self.ps_max[:, k % 2, 0:cfg.chunks[chunk][1]],
                                 AX.X).then_inc(s.max_read, 1)

    def dve_combine(self, dve, at, link):
        cfg, s, nc = self.cfg, self.s, self.nc
        n = 2 * self.NCH
        dve.wait_ge(s.max_read, at.n * n + n + 2)
        if cfg.rows == 1:
            nc.vector.tensor_reduce(self.shift_cols[:, :, cfg.row], self.max_cols[:], axis=AX.X, op=ALU.max,
                                    negate=True).then_inc(s.max_found, 1)
            dve.wait_ge(s.max_found, at.n + 1)
        else:
            link(nc.vector.tensor_reduce(self.neg_max[:], self.max_cols[:], axis=AX.X, op=ALU.max, negate=True))
            if self.bound is not None:
                link(nc.vector.tensor_scalar(self.neg_max[:], self.neg_max[:], self.bound, -self.bound, ALU.min, ALU.max))
            link(nc.vector.tensor_copy(self.shift_cols[:, :, cfg.row], self.neg_max[:]))
            nc.vector.tensor_tensor(self.shift_cols[:, :, cfg.row + 1], self.neg_max[:],
                                    self.shift_cols[:, :, cfg.row], ALU.subtract).then_inc(s.max_found, 1)

    def dve_shift(self, dve, at):
        cfg, s = self.cfg, self.s
        dve.wait_ge(s.max_turned, at.n + 1)
        self.nc.vector.tensor_copy(cfg.shift_rows(at), self.shift_turn[cfg.row:cfg.row + cfg.rows, :, :]
                                   .rearrange("p t q -> p (t q)")).then_inc(s.shift_ready, 1)

    def dve_limits(self, dve, at):
        nc, cs = self.nc, self.cs
        dve.wait_ge(cs.limits_made, at.n + 1)
        dve.wait_ge(cs.clipped, at.n * self.NG + 1)
        nc.vector.tensor_scalar(self.limits[:, 0, :], self.ps_turn[:, 1, :], self.bound, None, ALU.add)
        nc.vector.tensor_scalar(self.limits[:, 1, :], self.ps_turn[:, 1, :], -self.bound, None,
                                ALU.add).then_inc(cs.limits_read, 1)
        dve.wait_ge(cs.limits_read, at.n + 1)

    def dve_clip(self, dve, at, g):
        nc, cs = self.nc, self.cs
        j0, nj = self.cfg.groups[g]
        rows = self.cfg.keys(j0)
        scores = self.ps_scores[0:rows, self.buf(at, g), 0:nj * S].rearrange("p (j q) -> p j q", q=S)
        high, low = (self.limits[0:rows, x, :].unsqueeze(1).to_broadcast([rows, nj, S]) for x in range(2))
        dve.wait_ge(self.s.scores_made, at.n * self.NG + g + 1)
        nc.vector.tensor_tensor(scores, scores, high, ALU.min).then_inc(cs.clip_link, 1)
        dve.wait_ge(cs.clip_link, at.n * self.NG + g + 1)
        nc.vector.tensor_tensor(scores, scores, low, ALU.max).then_inc(cs.clipped, 1)

    def dve_first(self, dve, at, link_of):
        self.dve_reduce(dve, at, range(2 * self.NCH))
        self.dve_combine(dve, at, link_of(at))
        self.dve_shift(dve, at)
        one = at.ahead(1, False)
        self.dve_reduce(dve, one, range(2 * self.NCH))
        self.dve_combine(dve, one, link_of(one))

    def dve_heads(self, dve, p, i, last, link_of, next_ready=None):
        for h in range(self.cfg.heads):
            at = At(self.cfg, p, i, h)
            one, two = at.ahead(1, last), at.ahead(2, last)
            if h == self.cfg.heads - 2 and two is not None and next_ready is not None:
                next_ready(two)
            if self.bound is not None:
                self.dve_limits(dve, at)
            for g in range(self.NG):
                if self.bound is not None:
                    self.dve_clip(dve, at, g)
                for slot in (2 * g, 2 * g + 1):
                    if two is not None:
                        self.dve_reduce(dve, two, self.max_chunks(slot))
                    if one is not None and slot == self.cfg.turn_slot:
                        self.dve_shift(dve, one)
            if two is not None:
                self.dve_combine(dve, two, link_of(two))

    def act_exp(self, act, at, groups=None):
        cfg, s = self.cfg, self.s
        for g in (range(self.NG) if groups is None else groups):
            j0, nj = cfg.groups[g]
            rows = cfg.keys(j0)
            if self.bound is None:
                act.wait_ge(s.scores_made, at.n * self.NG + g + 1)
            else:
                act.wait_ge(self.cs.clipped, at.n * self.NG + g + 2)
            act.wait_ge(s.values_used, at.n * self.NG + g + 1)
            self.nc.scalar.activation(self.probs[0:rows, self.buf(at, g), 0:nj * S],
                                      self.ps_scores[0:rows, self.buf(at, g), 0:nj * S], ACT.Exp,
                                      scale=cfg.scale).then_inc(s.exp_done, 1)

    def act_heads(self, act, p, i, copy_out):
        for h in range(self.cfg.heads):
            at = At(self.cfg, p, i, h)
            if h or not self.early():
                self.act_exp(act, at, range(0, 1))
            if h:
                self.act_out(act, At(self.cfg, p, i, h - 1), copy_out)
            self.act_exp(act, at, range(1, self.NG))
        self.act_out(act, At(self.cfg, p, i, self.cfg.heads - 1), copy_out)

    def act_out(self, act, at, copy_out):
        act.wait_ge(self.s.values_used, (at.n + 1) * self.NG + 2)
        copy_out(at).then_inc(self.cfg.out_copied, 1)


def batches(eng, prep, run):
    prep(0, 0, True)
    with eng.Fori(0, B // 2 - 1) as i:
        prep(1, i, False)
        run(0, i, False)
        prep(0, i + 1, False)
        run(1, i, False)
    i = B // 2 - 1
    prep(1, i, False)
    run(0, i, False)
    run(1, i, True)


class Cfg:
    parities = 2
    slots = None
    early = False
    turn_slot = 2


def _l0_core(nc, c, d, qp, qpb, ctx, scale):
    s = sems(ctx, nc, "l0_ctx0 l0_ctx1 l0_ctxb l0_batch l0_out l0_zero")
    loaded = [s.l0_ctx0, s.l0_ctx1]
    ctxT = [ctx.enter_context(nc.sbuf_tensor(uniq(f"l0_ctxT{p}"), [DC + 1, SC], F32)) for p in range(2)]
    ctxk = [ctx.enter_context(nc.sbuf_tensor(uniq(f"l0_ctxk{p}"), [128, KT, DC + 1], F32)) for p in range(2)]
    ctxb = [ctx.enter_context(nc.sbuf_tensor(uniq(f"l0_ctxb{p}"), [DC, SC], BF16)) for p in range(2)]
    qpn = qp[:].rearrange("p b h t -> p (b h) t")
    qpbn = qpb[:].rearrange("p b h t -> p (b h) t")

    cfg = Cfg()
    cfg.heads, cfg.chunks, cfg.groups, cfg.keys, cfg.scale = H0, CHUNKS, GROUPS, key_rows, scale
    cfg.row, cfg.rows, cfg.row_dt = DC, 1, F32
    cfg.max_q = lambda at, t: qpbn[:, bass.ds(at.n, 1), 128 * t:128 * t + 128].rearrange("p a t -> p (a t)")
    cfg.max_k = lambda at, k0, size: ctxb[at.p][:, k0:k0 + size]
    cfg.score_k = lambda at, j: ctxT[at.p][:, 128 * j:128 * j + key_rows(j)]
    cfg.score_q = lambda at: qpn[:, bass.ds(at.n, 1), :].rearrange("p a t -> p (a t)")
    cfg.shift_rows = lambda at: qpn[DC:DC + 1, bass.ds(at.n, 1), :].rearrange("p a t -> p (a t)")
    cfg.value = lambda at, j: ctxk[at.p][0:key_rows(j), j, :]
    core = Core(nc, ctx, c, cfg)
    cfg.strips = 1
    cfg.out = lambda at, j: core.ps_out[0:DC + 1, 0:S]
    cfg.out_copied = s.l0_out
    block = ctx.enter_context(nc.Block())

    @block.sync
    def _(sp):
        sp.sem_inc(s.l0_batch, 2)
        with sp.Fori(0, B // 2) as i:
            for p in range(2):
                sp.wait_ge(s.l0_batch, 2 * i + p + 1)
                sp.dma_start(ctxT[p][:], d["ctxT"][bass.ds(2 * i + p, 1)].rearrange("b p n -> (b p) n")) \
                    .then_inc(loaded[p], 16)
                sp.dma_start(ctxk[p][:], d["ctx_tok"][bass.ds(2 * i + p, 1)].rearrange("b p j n -> (b p) j n")) \
                    .then_inc(loaded[p], 16)

    @block.gpsimd
    def _(pool):
        nc.gpsimd.memset(core.shift_cols[:], 0.0).then_inc(s.l0_zero, 1)

    @block.tensor
    def _(pe):
        core.begin_pe(pe)

        def ready(at):
            pe.wait_ge(loaded[at.p], 32 * at.i + 32)
            pe.wait_ge(s.l0_ctxb, at.b + 1)

        def prep(p, i, first):
            if first:
                ready(At(cfg, p, i, 0))
                core.pe_first(pe, At(cfg, p, i, 0))
        batches(pe, prep, lambda p, i, last: core.pe_heads(pe, p, i, last, next_ready=ready))

    @block.vector
    def _(dve):
        core.begin_dve(dve)
        dve.wait_ge(s.l0_zero, 1)

        def cast(at):
            dve.wait_ge(loaded[at.p], 32 * at.i + 32)
            nc.vector.tensor_copy(ctxb[at.p][:], ctxT[at.p][0:DC, :]).then_inc(s.l0_ctxb, 1)

        def prep(p, i, first):
            if first:
                cast(At(cfg, p, i, 0))
                core.dve_first(dve, At(cfg, p, i, 0), lambda at: None)
        batches(dve, prep, lambda p, i, last: core.dve_heads(dve, p, i, last, lambda at: None, cast))

    @block.scalar
    def _(act):
        core.begin_act(act)

        def copy_out(at):
            return nc.scalar.copy(qpn[:, bass.ds(at.n, 1), :].rearrange("p a t -> p (a t)"), core.ps_out[0:DC + 1, 0:S])

        with act.Fori(0, B // 2) as i:
            for p in range(2):
                core.act_heads(act, p, i, copy_out)
                act.sem_inc(s.l0_batch, 1)


def heads_out(nc, c, heads, w_o, bo, ctx, dh, H, gate):
    s = sems(ctx, nc, "ho_y ho_inv ho_sum ho_bias")
    py = ctx.enter_context(nc.psum_tensor(uniq("ho_py"), [128, 4, 2, 256], F32))
    pb = ctx.enter_context(nc.psum_tensor(uniq("ho_pb"), [128, 512], F32))
    inv = ctx.enter_context(nc.sbuf_tensor(uniq("ho_inv_t"), [128, NT, H], F32))
    total = ctx.enter_context(nc.sbuf_tensor(uniq("ho_total"), [128, NT, D], F32))
    PAIRS = H // 2
    block = ctx.enter_context(nc.Block())

    @block.tensor
    def _(pe):
        nc.tensor.matmul(pb[:, 0:D], c.ones_row[:], bo[:], start=True, stop=True).then_inc(s.ho_bias, 1)
        for x in range(NT * PAIRS):
            n, t = x // PAIRS, 128 * (x // PAIRS % 2)
            if x >= 4:
                pe.wait_ge(s.ho_sum, 2 * x - 5)
            for y in range(2):
                h = 2 * (x % PAIRS) + y
                ins = nc.tensor.matmul(py[:, x % 4, y, 0:D + 1], heads[0:dh + 1, n // 2, h, t:t + 128], w_o[:, h, :],
                                       start=True, stop=True)
            ins.then_inc(s.ho_y, 1)

    @block.vector
    def _(dve):
        dve.wait_ge(s.ho_bias, 1)
        nc.vector.tensor_copy(total[:], pb[:, 0:D].unsqueeze(1).to_broadcast([128, NT, D])).then_inc(s.ho_sum, 1)
        for x in range(NT * PAIRS):
            n, h = x // PAIRS, 2 * (x % PAIRS)
            dve.wait_ge(s.ho_y, x + 1)
            nc.vector.reciprocal(inv[:, n, h:h + 2], py[:, x % 4, :, D]).then_inc(s.ho_inv, 1)
            dve.wait_ge(s.ho_inv, x + 1)
            for y in range(2):
                dve.wait_ge(s.ho_sum, 1 + 2 * x + y)
                nc.vector.scalar_tensor_tensor(out=total[:, n, :], in0=py[:, x % 4, y, 0:D], scalar=inv[:, n, h + y:h + y + 1],
                                               in1=total[:, n, :], op0=ALU.mult, op1=ALU.add).then_inc(s.ho_sum, 1)
        dve.wait_ge(s.ho_sum, 1 + 2 * NT * PAIRS)
        nc.vector.scalar_tensor_tensor(out=c.x_res[:], in0=total[:], scalar=c.tanh_g[:, gate:gate + 1], in1=c.x_res[:],
                                       op0=ALU.mult, op1=ALU.add)


H8, DH8 = 16, 8
VCOLS = (H8 - 1) * (DH8 + 1) + 32
Q_PIECES = [0, 0, 0, 1, 1, 2]
K_PIECES = [0, 1, 2, 0, 1, 0]
ROW_MASK, ROW_SHIFT, ROWS8 = 48, 64, 128
NP = 3


def words(rows):
    return rows.rearrange("p h n -> p (h n)").bitcast(F32)


class Strips:

    def __init__(self, nc, ctx, c, core, strips):
        self.nc, self.c, self.core, self.rows = nc, c, core, 32 * strips
        self.s = sems(ctx, nc, "strips_link strips_copied strips_made strips_summed strips_parts strips_normed "
                               "strips_turned strips_out strips_rden")

        def sb(n, shape):
            return ctx.enter_context(nc.sbuf_tensor(uniq(f"strips_{n}_t"), shape, F32))
        self.product = sb("product", [128, H8, S])
        self.summed = sb("summed", [128, H8 // 4, S])
        self.rden = sb("rden", [128, TPB, H8])
        self.heads = sb("heads", [128, TPB, H8, DH8])
        cfg = core.cfg
        cfg.strips, cfg.early = strips, True
        cfg.out = lambda at, j: core.ps_out[32 * (j % strips):32 * (j % strips) + 32, 0:S]
        cfg.out_copied = self.s.strips_copied
        self.turn = core.ps_turn[:, 1, :].rearrange("p (t q) -> p t q", t=TPB)
        self.ps_sum = core.ps_scores[:, 0, :].rearrange("p (x q) -> p x q", x=H8 // 4)
        self.ps_parts = core.ps_scores[:, 1, :].rearrange("p (t x n) -> p t x n", t=TPB, x=H8 // 4)

    def begin_pe(self, pe):
        self.core.begin_pe(pe)
        pe.sem_inc(self.s.strips_out, 1)

    def begin_dve(self, dve):
        self.core.begin_dve(dve)
        dve.sem_inc(self.s.strips_turned, 1)

    def pe_first(self, pe):
        at = At(self.core.cfg, 0, 0, 0)
        self.core.pe_first(pe, at)
        if self.core.early():
            self.core.pe_scores(pe, at, 0)

    def act_batches(self, act, done):
        def prep(p, i, first):
            if first and self.core.early():
                self.core.act_exp(act, At(self.core.cfg, p, i, 0), range(0, 1))

        def run(p, i, last):
            self.act(act, p, i, last)
            done()
        batches(act, prep, run)

    def pe_turn_free(self, pe, b):
        pe.wait_ge(self.s.strips_out, b + 1)

    def pe(self, pe, p, i, last):
        b = 2 * i + p
        s, core, nc, c = self.s, self.core, self.nc, self.c
        pe.wait_ge(s.strips_copied, H8 * (b + 1) + 1)
        pe.wait_ge(core.s.exp_done, H8 * core.NG * (b + 1) + 2)
        for x in range(H8 // 4):
            for y in range(4):
                ins = nc.tensor.matmul(self.ps_sum[32 * y:32 * y + 32, x, :], c.strip_sum[:],
                                       self.product[:, 4 * x + y, :], start=True, stop=True)
        ins.then_inc(s.strips_made, 1)
        pe.wait_ge(s.strips_summed, b + 1)
        for x in range(H8 // 4):
            for t in range(TPB):
                ins = nc.tensor.transpose(self.ps_parts[:, t, x, :], self.summed[:, x, 128 * t:128 * t + 128], c.ident[:])
        ins.then_inc(s.strips_parts, 1)
        if core.early() and not last:
            core.pe_scores(pe, At(core.cfg, p, i, H8 - 1).ahead(1, False), 0)
        pe.wait_ge(s.strips_normed, b + 1)
        for t in range(TPB):
            ins = nc.tensor.transpose(self.turn[:, t, :], self.heads[:, t, :, :].rearrange("p h n -> p (h n)"), c.ident[:])
        ins.then_inc(s.strips_turned, 1)

    def act(self, act, p, i, last):
        b = 2 * i + p
        s, core, nc = self.s, self.core, self.nc

        core.act_heads(act, p, i, lambda at: nc.scalar.copy(self.product[0:self.rows, at.h, :],
                                                            core.ps_out[0:self.rows, 0:S]))
        act.wait_ge(s.strips_made, b + 1)
        nc.scalar.copy(self.summed[:], self.ps_sum).then_inc(s.strips_summed, 1)
        if core.early() and not last:
            core.act_exp(act, At(core.cfg, p, i, H8 - 1).ahead(1, False), range(0, 1))
        act.wait_ge(s.strips_turned, b + 2)
        nc.scalar.copy(self.c.xnT[:, bass.ds(b * S, S)], core.ps_turn[:, 1, :]).then_inc(s.strips_out, 1)

    def link_of(self, dve):
        def counted(at):
            link = Link(dve, self.s.strips_link)
            link.base = (2 if self.core.bound is None else 3) * at.n
            return link
        return counted

    def dve(self, dve, p, i, b, last):
        s, core, nc = self.s, self.core, self.nc
        core.dve_heads(dve, p, i, last, self.link_of(dve))
        dve.wait_ge(s.strips_parts, b + 1)
        heads_of = self.ps_parts.rearrange("p t x (y n) -> p t (x y) n", y=4)
        nc.vector.reciprocal(self.rden[:], heads_of[:, :, :, DH8]).then_inc(s.strips_rden, 1)
        dve.wait_ge(s.strips_rden, b + 1)
        dve.wait_ge(s.strips_turned, b + 1)
        for t in range(TPB):
            ins = nc.vector.tensor_tensor(self.heads[:, t, :, :], heads_of[:, t, :, 0:DH8],
                                          bcast(self.rden[:, t, :], [128, H8, DH8]), ALU.mult)
        ins.then_inc(s.strips_normed, 1)


def l8_attention(nc, c, d, name, finish_layer, clamp=None):
    with ExitStack() as ctx:
        peaks = None
        if clamp is not None:
            peaks = ctx.enter_context(nc.sbuf_tensor(uniq("peaks"), [128, 2 + B], F32))
            clip_flag = ctx.enter_context(nc.sbuf_tensor(uniq("clip_flag"), [1, 1], mybir.dt.int32))
        q_pieces = nc.dram_tensor(f"{name}_qpieces", (NP, 128, NT * 128), BF16, kind="Internal").ap()
        k_pieces = nc.dram_tensor(f"{name}_kpieces", (B, NP, 128, SC), BF16, kind="Internal").ap()
        values = nc.dram_tensor(f"{name}_values", (B, 128, KT, VCOLS), F32, kind="Internal").ap()
        with ExitStack() as cx:
            _l8_queries(nc, c, d, name, q_pieces, cx, peaks=peaks)
        with ExitStack() as cx:
            _l8_keys(nc, c, d, name, k_pieces, values, peaks, cx)
        if clamp is not None:
            with ExitStack() as cx:
                _l8_flag(nc, c, peaks, clip_flag, clamp, cx)
        with ExitStack() as cx:
            clip = None if clamp is None else (clip_flag, clamp / DH8 ** -0.5)
            _l8_core(nc, c, name, q_pieces, k_pieces, values, clip, cx)
        with ExitStack() as cx:
            finish_layer(nc, c, d, cx)


def _l8_queries(nc, c, d, name, q_pieces, ctx, biased=True, peaks=None):
    s = sems(ctx, nc, "q_w q_made q_biased q_high q_rest q_middle q_low q_out")
    wq = ctx.enter_context(nc.sbuf_tensor(uniq("q_wq"), [D, 128], F32))
    bq = ctx.enter_context(nc.sbuf_tensor(uniq("q_bq"), [128, 1], F32))
    qf = ctx.enter_context(nc.sbuf_tensor(uniq("q_f"), [128, 4, 512], F32))
    rest = ctx.enter_context(nc.sbuf_tensor(uniq("q_rest"), [128, 4, 512], F32))
    piece = [ctx.enter_context(nc.sbuf_tensor(uniq(f"q_piece{i}"), [128, 4, 512], BF16)) for i in range(NP)]
    pq = ctx.enter_context(nc.psum_tensor(uniq("q_ps"), [128, 4, 512], F32))
    block = ctx.enter_context(nc.Block())

    @block.sync
    def _(sp):
        sp.dma_start(wq[:], d[f"{name}_Wq"]).then_inc(s.q_w, 16)
        if biased:
            sp.dma_start(bq[:], d[f"{name}_bq"]).then_inc(s.q_w, 16)
        for i, done in enumerate([s.q_high, s.q_middle, s.q_low]):
            sp.wait_ge(done, 4)
            sp.dma_start(q_pieces[i], piece[i][:].rearrange("p k n -> p (k n)")).then_inc(s.q_out, 16)
        sp.wait_ge(s.q_out, 16 * NP)

    @block.tensor
    def _(pe):
        pe.wait_ge(s.q_w, 32 if biased else 16)
        for k in range(4):
            nc.tensor.matmul(pq[:, k, :], wq[:], c.xnT[:, 512 * k:512 * k + 512],
                             start=True, stop=True).then_inc(s.q_made, 1)

    @block.scalar
    def _(act):
        act.wait_ge(s.q_w, 32 if biased else 16)
        for k in range(4):
            act.wait_ge(s.q_made, k + 1)
            if biased:
                ins = nc.scalar.activation(qf[:, k, :], pq[:, k, :], ACT.Identity, bias=bq[:])
            else:
                ins = nc.scalar.copy(qf[:, k, :], pq[:, k, :])
            ins.then_inc(s.q_biased, 1)
        for k in range(4):
            act.wait_ge(s.q_biased, k + 1)
            nc.scalar.copy(piece[0][:, k, :], qf[:, k, :]).then_inc(s.q_high, 1)
        for k in range(4):
            act.wait_ge(s.q_rest, k + 1)
            nc.scalar.copy(piece[1][:, k, :], rest[:, k, :]).then_inc(s.q_middle, 1)

    @block.vector
    def _(dve):
        if peaks is not None:
            dve.wait_ge(s.q_biased, 4)
            nc.vector.tensor_reduce(peaks[:, 0:1], qf[:].rearrange("p k n -> p (k n)"), axis=AX.X, op=ALU.max,
                                    apply_absolute_value=True)
        for k in range(4):
            dve.wait_ge(s.q_high, k + 1)
            nc.vector.tensor_tensor(rest[:, k, :], qf[:, k, :], piece[0][:, k, :], ALU.subtract).then_inc(s.q_rest, 1)
        for k in range(4):
            dve.wait_ge(s.q_middle, k + 1)
            nc.vector.tensor_tensor(piece[2][:, k, :], rest[:, k, :], piece[1][:, k, :],
                                    ALU.subtract).then_inc(s.q_low, 1)


KCH = [(0, 512), (512, 512), (1024, 512), (1536, SC - 1536)]


def _l8_keys(nc, c, d, name, k_pieces, values, peaks, ctx):
    s = sems(ctx, nc, "k_w k_ctx0 k_ctx1 k_init k_made k_high k_rest k_middle k_low k_vmade k_vcopied k_out0 k_out1")
    loaded, out = [s.k_ctx0, s.k_ctx1], [s.k_out0, s.k_out1]

    def sb(n, shape, dt=F32):
        return [ctx.enter_context(nc.sbuf_tensor(uniq(f"k_{n}{p}"), shape, dt)) for p in range(2)]
    ctxT, rest, vals, (wk, wv) = sb("ctxT", [DC + 1, SC]), sb("rest", [128, SC]), sb("vals", [128, KT, VCOLS]), sb("w", [DC + 1, 128])
    piece = sb("piece", [128, NP, SC], BF16)
    ps_k = ctx.enter_context(nc.psum_tensor(uniq("k_psk"), [128, 4, 512], F32))
    ps_v = ctx.enter_context(nc.psum_tensor(uniq("k_psv"), [128, 4, 512], F32))
    block = ctx.enter_context(nc.Block())
    NK = len(KCH)

    @block.sync
    def _(sp):
        sp.dma_start(wk[:], d[f"{name}_Wk"]).then_inc(s.k_w, 16)
        sp.dma_start(wv[:], d[f"{name}_Wv"]).then_inc(s.k_w, 16)
        for b in range(B + 1):
            if b < B:
                if b >= 2:
                    sp.wait_ge(s.k_vmade, 4 * (b - 1))
                sp.dma_start(ctxT[b % 2][:], d["ctxT"][b]).then_inc(loaded[b % 2], 16)
            if b:
                a = b - 1
                sp.wait_ge(s.k_vcopied, 4 * a + 8)
                sp.dma_start(values[a], vals[a % 2][:]).then_inc(out[a % 2], 16)
                sp.wait_ge(s.k_middle, NK * a + NK)
                sp.wait_ge(s.k_low, NK * a + NK + 2 * NK)
                sp.dma_start(k_pieces[a].rearrange("y p n -> p y n"), piece[a % 2][:]).then_inc(out[a % 2], 16)
        for x in out:
            sp.wait_ge(x, 32 * B // 2 + 1)

    @block.gpsimd
    def _(pool):
        link = Link(pool, s.k_init)
        for p in range(2):
            link(nc.gpsimd.memset(vals[p][:], 0.0))
            link(nc.gpsimd.memset(vals[p][:, :, 0:H8 * 9].rearrange("p j (h n) -> p j h n", n=9)[:, :, :, DH8:], 1.0))

    @block.tensor
    def _(pe):
        pe.wait_ge(s.k_w, 32)
        with pe.Fori(0, B // 2) as i:
            for p in range(2):
                b = 2 * i + p
                pe.wait_ge(loaded[p], 16 * i + 16)
                for x, (k0, size) in enumerate(KCH):
                    pe.wait_ge(s.k_rest, NK * b + x + 1)
                    nc.tensor.matmul(ps_k[:, x, 0:size], wk[:], ctxT[p][:, k0:k0 + size],
                                     start=True, stop=True).then_inc(s.k_made, 1)
                for x, (j0, nj) in enumerate(GROUPS):
                    pe.wait_ge(s.k_vcopied, 4 * b + x + 1)
                    for j in range(j0, j0 + nj):
                        ins = nc.tensor.matmul(ps_v[0:key_rows(j), x, 128 * (j - j0):128 * (j - j0) + 128],
                                               ctxT[p][:, 128 * j:128 * j + key_rows(j)], wv[:], start=True, stop=True)
                    ins.then_inc(s.k_vmade, 1)

    @block.scalar
    def _(act):
        act.wait_ge(s.k_init, 4)
        act.sem_inc(s.k_vcopied, 4)
        act.sem_inc(s.k_out0, 1)
        act.sem_inc(s.k_out1, 1)
        with act.Fori(0, B // 2) as i:
            for p in range(2):
                b = 2 * i + p
                act.wait_ge(out[p], 32 * i + 1)
                for x, (k0, size) in enumerate(KCH):
                    act.wait_ge(s.k_made, NK * b + x + 1)
                    nc.scalar.copy(piece[p][:, 0, k0:k0 + size], ps_k[:, x, 0:size]).then_inc(s.k_high, 1)
                for x, (k0, size) in enumerate(KCH):
                    act.wait_ge(s.k_rest, NK * b + x + 5)
                    nc.scalar.copy(piece[p][:, 1, k0:k0 + size], rest[p][:, k0:k0 + size]).then_inc(s.k_middle, 1)
                for x, (j0, nj) in enumerate(GROUPS):
                    rows = key_rows(j0)
                    act.wait_ge(s.k_vmade, 4 * b + x + 1)
                    nc.scalar.copy(vals[p][0:rows, j0:j0 + nj, 0:H8 * 9].rearrange("p j (h n) -> p j h n", n=9)[:, :, :, 0:DH8],
                                   ps_v[0:rows, x, 0:128 * nj].rearrange("p (j h n) -> p j h n", j=nj, n=DH8)) \
                        .then_inc(s.k_vcopied, 1)

    @block.vector
    def _(dve):
        dve.sem_inc(s.k_rest, 4)
        dve.sem_inc(s.k_low, 8)
        with dve.Fori(0, B // 2) as i:
            for p in range(2):
                b = 2 * i + p
                dve.wait_ge(out[p], 32 * i + 1)
                dve.wait_ge(s.k_low, NK * b + NK)
                for x, (k0, size) in enumerate(KCH):
                    dve.wait_ge(s.k_high, NK * b + x + 1)
                    nc.vector.tensor_tensor(rest[p][:, k0:k0 + size], ps_k[:, x, 0:size],
                                            piece[p][:, 0, k0:k0 + size], ALU.subtract).then_inc(s.k_rest, 1)
                if peaks is not None:
                    nc.vector.tensor_reduce(peaks[:, bass.ds(2 + b, 1)], piece[p][:, 0, :], axis=AX.X, op=ALU.max,
                                            apply_absolute_value=True)
                for x, (k0, size) in enumerate(KCH):
                    dve.wait_ge(s.k_middle, NK * b + x + 1)
                    nc.vector.tensor_tensor(piece[p][:, 2, k0:k0 + size], rest[p][:, k0:k0 + size],
                                            piece[p][:, 1, k0:k0 + size], ALU.subtract).then_inc(s.k_low, 1)


def _l8_flag(nc, c, peaks, clip_flag, clamp, ctx):
    s = sems(ctx, nc, "fl_peaks fl_turned fl_link")
    ps = ctx.enter_context(nc.psum_tensor(uniq("fl_ps"), [1, 2, 128], F32))
    top = ctx.enter_context(nc.sbuf_tensor(uniq("fl_top"), [1, 3], F32))
    block = ctx.enter_context(nc.Block())

    @block.tensor
    def _(pe):
        pe.wait_ge(s.fl_peaks, 1)
        for x in range(2):
            ins = nc.tensor.matmul(ps[:, x, :], peaks[:, x:x + 1], c.ident[:], start=True, stop=True)
        ins.then_inc(s.fl_turned, 1)

    @block.vector
    def _(dve):
        link = Link(dve, s.fl_link)
        nc.vector.reduce_max(peaks[:, 1:2], peaks[:, 2:2 + B], AX.X).then_inc(s.fl_peaks, 1)
        dve.wait_ge(s.fl_turned, 1)
        link(nc.vector.reduce_max(top[:, 0:2], ps[:], AX.X))
        link(nc.vector.tensor_tensor(top[:, 2:3], top[:, 0:1], top[:, 1:2], ALU.mult))
        nc.vector.tensor_scalar(clip_flag[:], top[:, 2:3], 0.9 * clamp / (DH8 * DH8 ** -0.5), None, ALU.is_ge)


def _l8_core(nc, c, name, q_pieces, k_pieces, values, clip, ctx):
    s = sems(ctx, nc, "a8_init a8_zero0 a8_zero1 a8_ones0 a8_ones1 a8_rows0 a8_rows1 a8_batch")
    rows_in, zeroed, ones_in = [s.a8_rows0, s.a8_rows1], [s.a8_zero0, s.a8_zero1], [s.a8_ones0, s.a8_ones1]

    def sb(n, shape, dt=F32, count=2):
        return [ctx.enter_context(nc.sbuf_tensor(uniq(f"a8_{n}{p}"), shape, dt)) for p in range(count)]
    kaug = sb("kaug", [ROWS8, H8, SC + SC % 2], BF16)
    qaug = sb("qaug", [ROWS8, H8, S], BF16)
    vaug = sb("vaug", [128, KT, VCOLS])
    zero_rows, = sb("zero", [2, S], BF16, 1)
    one_rows, = sb("one", [2, SC], BF16, 1)
    INIT = 6 if clip is None else 8
    N_ROWS = 2 * len(K_PIECES) + 2

    def head(x, at, cols):
        return x[:, at.h, cols]

    cfg = Cfg()
    cfg.heads, cfg.chunks, cfg.groups, cfg.keys, cfg.scale = H8, CHUNKS, GROUPS, key_rows, DH8 ** -0.5
    cfg.row, cfg.rows, cfg.row_dt = ROW_SHIFT, 2, BF16
    cfg.max_q = lambda at, t: head(qaug[at.p], at, slice(128 * t, 128 * t + 128))
    cfg.max_k = lambda at, k0, size: head(kaug[at.p], at, slice(k0, k0 + size))
    cfg.score_k = lambda at, j: head(kaug[at.p], at, slice(128 * j, 128 * j + key_rows(j)))
    cfg.score_q = lambda at: head(qaug[at.p], at, slice(0, S))
    cfg.shift_rows = lambda at: qaug[at.p][ROW_SHIFT:ROW_SHIFT + 2, at.h, :]
    cfg.value = lambda at, j: vaug[at.p][0:key_rows(j), j, 9 * at.h:9 * at.h + 32]
    core = Core(nc, ctx, c, cfg)
    strips = Strips(nc, ctx, c, core, 4)
    if clip is not None:
        clip_flag, bound = clip
        core.cs = sems(ctx, nc, "limits_made limits_read clip_link clipped")
        core.limits = ctx.enter_context(nc.sbuf_tensor(uniq("limits"), [128, 2, S], F32))
        core.shift_sum = ctx.enter_context(nc.sbuf_tensor(uniq("shift_sum"), [128, 128], BF16))

    def either(eng, program):
        if clip is None:
            program()
            return
        flag = eng.value_load(clip_flag[0:1, 0:1], min_val=0, max_val=1)
        with eng.If(flag):
            core.bound = bound
            program()
        with eng.Else():
            core.bound = None
            program()
    block = ctx.enter_context(nc.Block())

    @block.sync
    def _(sp):
        sp.sem_inc(s.a8_batch, 2)
        low = 32 // DH8
        for b in range(B):
            p = b % 2
            loads = [(kaug[p][8 * x:8 * x + 8, :, 0:SC], k_pieces[b, y].rearrange("(h e) n -> e h n", e=DH8))
                     for x, y in enumerate(K_PIECES)]
            loads_q = [(qaug[p][8 * x:8 * x + 8, :, :],
                        q_pieces[y].rearrange("(h e) n -> e h n", e=DH8)[:, :, b * S:(b + 1) * S])
                       for x, y in enumerate(Q_PIECES)]
            sp.wait_ge(s.a8_batch, b + 1)
            for dst, src in loads[:low] + loads_q[:low]:
                sp.dma_start(dst, src).then_inc(rows_in[p], 16)
            sp.dma_start(vaug[p][:], values[b]).then_inc(rows_in[p], 16)
            if b < 2:
                sp.wait_ge(zeroed[b], 2 + b)
                sp.wait_ge(s.a8_init, INIT)
                sp.dma_start(kaug[p][ROW_SHIFT:ROW_SHIFT + 2, :, 0:SC],
                             one_rows[:].unsqueeze(1).to_broadcast([2, H8, SC])).then_inc(ones_in[p], 16)
            for dst, src in loads[low:] + loads_q[low:]:
                sp.dma_start(dst, src).then_inc(rows_in[p], 16)
            sp.dma_start(qaug[p][ROW_SHIFT:ROW_SHIFT + 2, :, :], zero_rows[:].unsqueeze(1).to_broadcast([2, H8, S])) \
                .then_inc(rows_in[p], 16)

    @block.gpsimd
    def _(pool):
        link = Link(pool, s.a8_init)
        link(nc.gpsimd.memset(words(kaug[0][64:128, :, :]), 0.0))
        if clip is not None:
            link(nc.gpsimd.memset(core.shift_sum[:], 0.0))
            link(nc.gpsimd.memset(core.shift_sum[ROW_SHIFT:ROW_SHIFT + 2, :], 1.0))
        link(nc.gpsimd.memset(zero_rows[:], 0.0))
        link(nc.gpsimd.memset(one_rows[:], 1.0))
        link(nc.gpsimd.memset(core.shift_cols[:], 0.0))
        for p in range(2):
            link(nc.gpsimd.memset(words(qaug[p][64:128, :, :]), 0.0))
        link = Link(pool, zeroed[1])
        link(nc.gpsimd.memset(words(qaug[1][32:64, :, :]), 0.0))
        link(nc.gpsimd.memset(words(kaug[1][32:64, :, :]), 0.0))
        link(nc.gpsimd.memset(words(kaug[1][64:128, :, :]), 0.0))

    @block.tensor
    def _(pe):
        strips.begin_pe(pe)
        pe.wait_ge(s.a8_init, INIT)

        def rows_ready(at):
            pe.wait_ge(ones_in[at.p], 16)
            pe.wait_ge(rows_in[at.p], 16 * N_ROWS * (at.i + 1))

        def prep(p, i, first):
            if first:
                rows_ready(At(cfg, p, i, 0))
                strips.pe_first(pe)

        def run(p, i, last):
            core.pe_heads(pe, p, i, last, strips.pe_turn_free, rows_ready)
            strips.pe(pe, p, i, last)
        either(pe, lambda: batches(pe, prep, run))

    @block.scalar
    def _(act):
        core.begin_act(act)

        either(act, lambda: strips.act_batches(act, lambda: act.sem_inc(s.a8_batch, 1)))

    @block.vector
    def _(dve):
        strips.begin_dve(dve)
        link = Link(dve, zeroed[0])
        link(nc.vector.memset(words(qaug[0][32:64, :, :]), 0.0))
        link(nc.vector.memset(words(kaug[0][32:64, :, :]), 0.0))
        dve.wait_ge(s.a8_init, INIT)

        def prep(p, i, first):
            if first:
                core.dve_first(dve, At(cfg, p, i, 0), strips.link_of(dve))
        if clip is not None:
            dve.sem_inc(core.cs.clipped, 1)
        either(dve, lambda: batches(dve, prep, lambda p, i, last: strips.dve(dve, p, i, 2 * i + p, last)))


def add_tiles(nc, c, s_made, s_added, py, gate, dve):
    for n in range(NT):
        dve.wait_ge(s_made, n + 1)
        nc.vector.scalar_tensor_tensor(out=c.x_res[:, n, :], in0=py[:, n % 4, 0:D], scalar=c.tanh_g[:, gate:gate + 1],
                                       in1=c.x_res[:, n, :], op0=ALU.mult, op1=ALU.add).then_inc(s_added, 1)


def l1_attention(nc, c, d):
    def out(nc, c, d, ctx):
        s = sems(ctx, nc, "o_w o_made o_added")
        wo = ctx.enter_context(nc.sbuf_tensor(uniq("o_w"), [128, D], F32))
        bo = ctx.enter_context(nc.sbuf_tensor(uniq("o_b"), [1, D], F32))
        py = ctx.enter_context(nc.psum_tensor(uniq("o_py"), [128, 4, 512], F32))
        block = ctx.enter_context(nc.Block())

        @block.sync
        def _(sp):
            sp.dma_start(wo[:], d["l1_Wo"]).then_inc(s.o_w, 16)
            sp.dma_start(bo[:], d["l1_bo"]).then_inc(s.o_w, 16)

        @block.tensor
        def _(pe):
            pe.wait_ge(s.o_w, 32)
            for n in range(NT):
                if n >= 4:
                    pe.wait_ge(s.o_added, n - 3)
                nc.tensor.matmul(py[:, n % 4, 0:D], c.xnT[:, 128 * n:128 * n + 128], wo[:], start=True, stop=False)
                nc.tensor.matmul(py[:, n % 4, 0:D], c.ones_row[:], bo[:], start=False, stop=True).then_inc(s.o_made, 1)

        @block.vector
        def _(dve):
            add_tiles(nc, c, s.o_made, s.o_added, py, 1, dve)
    l8_attention(nc, c, d, "l1", out, clamp=1e4)


def l2_attention(nc, c, d):
    def mlp(nc, c, d, ctx):
        s = sems(ctx, nc, "o_w o_hmade o_hidden o_made o_added")
        w1 = ctx.enter_context(nc.sbuf_tensor(uniq("o_w1"), [128, 2, 128], F32))
        b1 = ctx.enter_context(nc.sbuf_tensor(uniq("o_b1"), [128, 2], F32))
        w2 = ctx.enter_context(nc.sbuf_tensor(uniq("o_w2"), [128, 2, D], F32))
        b2 = ctx.enter_context(nc.sbuf_tensor(uniq("o_b2"), [1, D], F32))
        hid = ctx.enter_context(nc.sbuf_tensor(uniq("o_hid"), [128, 2, 4, 512], F32))
        ph = ctx.enter_context(nc.psum_tensor(uniq("o_ph"), [128, 4, 512], F32))
        py = ctx.enter_context(nc.psum_tensor(uniq("o_py"), [128, 4, 512], F32))
        block = ctx.enter_context(nc.Block())

        @block.sync
        def _(sp):
            for dst, src in ((w1, "l2_W1"), (b1, "l2_b1"), (w2, "l2_W2"), (b2, "l2_b2")):
                sp.dma_start(dst[:], d[src]).then_inc(s.o_w, 16)

        @block.tensor
        def _(pe):
            pe.wait_ge(s.o_w, 64)
            for x in range(8):
                k, j = x // 2, x % 2
                if x >= 4:
                    pe.wait_ge(s.o_hidden, x - 3)
                nc.tensor.matmul(ph[:, x % 4, :], w1[:, j, :], c.xnT[:, 512 * k:512 * k + 512],
                                 start=True, stop=True).then_inc(s.o_hmade, 1)
            for n in range(NT):
                pe.wait_ge(s.o_hidden, 2 * (n // 4) + 2)
                if n >= 4:
                    pe.wait_ge(s.o_added, n - 3)
                for j in range(2):
                    nc.tensor.matmul(py[:, n % 4, 0:D], hid[:, j, n // 4, 128 * (n % 4):128 * (n % 4) + 128],
                                     w2[:, j, :], start=(j == 0), stop=False)
                nc.tensor.matmul(py[:, n % 4, 0:D], c.ones_row[:], b2[:], start=False, stop=True).then_inc(s.o_made, 1)

        @block.scalar
        def _(act):
            act.wait_ge(s.o_w, 64)
            for x in range(8):
                act.wait_ge(s.o_hmade, x + 1)
                nc.scalar.activation(hid[:, x % 2, x // 2, :], ph[:, x % 4, :], ACT.Relu,
                                     bias=b1[:, x % 2:x % 2 + 1]).then_inc(s.o_hidden, 1)

        @block.vector
        def _(dve):
            add_tiles(nc, c, s.o_made, s.o_added, py, 2, dve)
    l8_attention(nc, c, d, "l2", mlp)


E0, I0, NG0, TOPG, TOPK = 16, 64, 4, 2, 4
BIG = 1e30


def l0_ffn(nc, c, d):
    with ExitStack() as ctx:
        comb = ctx.enter_context(nc.sbuf_tensor(uniq("f0_comb"), [128, NT, E0], F32))
        with ExitStack() as cx:
            _l0_route(nc, c, d, comb, cx)
        with ExitStack() as cx:
            _l0_experts(nc, c, d, comb, cx)


def _l0_route(nc, c, d, comb, ctx):
    s = sems(ctx, nc, "r_in r_made r_scored r_link")

    def sb(name, shape):
        return ctx.enter_context(nc.sbuf_tensor(uniq(name), shape, F32))
    gate, bias = sb("r_gate", [D, E0]), sb("r_bias", [128, E0])
    before_e, before_g = sb("r_before_e", [128, E0, E0]), sb("r_before_g", [128, NG0, NG0])
    scores, biased = sb("r_scores", [128, NT, E0]), sb("r_biased", [128, NT, E0])
    gmax, grank, penalty = sb("r_gmax", [128, NT, NG0]), sb("r_grank", [128, NT, NG0]), sb("r_pen", [128, NT, NG0])
    g_more, g_same = sb("r_gmore", [128, NT, NG0, NG0]), sb("r_gsame", [128, NT, NG0, NG0])
    more, same, rank = sb("r_more", [128, NT, E0, E0]), sb("r_same", [128, NT, E0, E0]), sb("r_rank", [128, NT, E0])
    ps = ctx.enter_context(nc.psum_tensor(uniq("r_ps"), [128, NT, E0], F32))
    block = ctx.enter_context(nc.Block())

    @block.sync
    def _(sp):
        for dst, src in ((gate[:], d["f0_gate"]), (bias[:], d["f0_bias"].partition_broadcast(128)),
                         (before_e[:], d["before_e"].partition_broadcast(128)),
                         (before_g[:], d["before_g"].partition_broadcast(128))):
            sp.dma_start(dst, src).then_inc(s.r_in, 16)

    @block.tensor
    def _(pe):
        pe.wait_ge(s.r_in, 64)
        for n in range(NT):
            ins = nc.tensor.matmul(ps[:, n, :], c.xnT[:, 128 * n:128 * n + 128], gate[:], start=True, stop=True)
        ins.then_inc(s.r_made, 1)

    @block.scalar
    def _(act):
        act.wait_ge(s.r_made, 1)
        nc.scalar.activation(scores[:], ps[:], ACT.Sigmoid).then_inc(s.r_scored, 1)

    @block.vector
    def _(dve):
        link = Link(dve, s.r_link)

        def ranks(v, n, before, more, same, rank):
            shape = [128, NT, n, n]
            rival, own = v[:].unsqueeze(2).to_broadcast(shape), v[:].unsqueeze(3).to_broadcast(shape)
            nc.vector.tensor_tensor(more[:], rival, own, ALU.is_gt)
            link(nc.vector.tensor_tensor(same[:], rival, own, ALU.is_equal))
            link(nc.vector.tensor_tensor(same[:], same[:], before[:].unsqueeze(1).to_broadcast(shape), ALU.mult))
            link(nc.vector.tensor_tensor(more[:], more[:], same[:], ALU.add))
            link(nc.vector.reduce_sum(rank[:], more[:], AX.X))

        dve.wait_ge(s.r_in, 64)
        dve.wait_ge(s.r_scored, 1)
        link(nc.vector.tensor_tensor(biased[:], scores[:], bias[:].unsqueeze(1).to_broadcast([128, NT, E0]), ALU.add))
        grouped = biased[:].rearrange("p n (g e) -> p n g e", g=NG0)
        link(nc.vector.reduce_max(gmax[:], grouped, AX.X))
        ranks(gmax, NG0, before_g, g_more, g_same, grank)
        link(nc.vector.tensor_scalar(penalty[:], grank[:], float(TOPG), -BIG, ALU.is_ge, ALU.mult))
        link(nc.vector.tensor_tensor(grouped, grouped, bcast(penalty[:], [128, NT, NG0, E0 // NG0]), ALU.add))
        ranks(biased, E0, before_e, more, same, rank)
        link(nc.vector.tensor_scalar(rank[:], rank[:], float(TOPK), None, ALU.is_lt))
        nc.vector.tensor_tensor(comb[:], rank[:], scores[:], ALU.mult)


def _l0_experts(nc, c, d, comb, ctx):
    s = sems(ctx, nc, "e_in e_combT e_comb_copied e_made e_silu e_mul e_hidden e_y e_ycopied e_yT e_added")
    NM = E0 // 2 + 1
    w13 = ctx.enter_context(nc.sbuf_tensor(uniq("e_w13"), [D, NM, 2, 128], F32))
    w2 = ctx.enter_context(nc.sbuf_tensor(uniq("e_w2"), [128, NM, D], F32))
    sel = ctx.enter_context(nc.sbuf_tensor(uniq("e_sel"), [E0, E0 // 2, 128], F32))
    combT = ctx.enter_context(nc.sbuf_tensor(uniq("e_combT"), [E0, NT * 128], F32))
    silu = ctx.enter_context(nc.sbuf_tensor(uniq("e_silu_t"), [128, 2, 512], F32))
    hid = ctx.enter_context(nc.sbuf_tensor(uniq("e_hid"), [128, 2, 512], F32))
    yT = ctx.enter_context(nc.sbuf_tensor(uniq("e_yT_t"), [D, 2, 512], F32))
    p1 = ctx.enter_context(nc.psum_tensor(uniq("e_p1"), [128, 2, 512], F32))
    p3 = ctx.enter_context(nc.psum_tensor(uniq("e_p3"), [128, 2, 512], F32))
    pc = ctx.enter_context(nc.psum_tensor(uniq("e_pc"), [128, 2, 512], F32))
    py = ctx.enter_context(nc.psum_tensor(uniq("e_py"), [128, 512], F32))
    pt = ctx.enter_context(nc.psum_tensor(uniq("e_pt"), [128, 512], F32))
    steps = [(k, m) for k in range(4) for m in range(NM)]
    rows = lambda m: 128 if m < NM - 1 else I0
    block = ctx.enter_context(nc.Block())

    @block.sync
    def _(sp):
        for dst, src in ((w13, "f0_w13"), (w2, "f0_w2"), (sel, "f0_sel")):
            sp.dma_start(dst[:], d[src]).then_inc(s.e_in, 16)

    @block.tensor
    def _(pe):
        for k in range(4):
            if k:
                pe.wait_ge(s.e_comb_copied, k)
            for n in range(4 * k, 4 * k + 4):
                ins = nc.tensor.transpose(pt[0:E0, 128 * (n % 4):128 * (n % 4) + 128], comb[:, n, :], c.ident[:])
            ins.then_inc(s.e_combT, 1)
        pe.wait_ge(s.e_in, 48)
        pe.wait_ge(s.e_comb_copied, 4)

        def down(x):
            k, m = steps[x]
            pe.wait_ge(s.e_hidden, x + 1)
            if m == 0 and k:
                pe.wait_ge(s.e_ycopied, k)
            ins = nc.tensor.matmul(py[:], w2[0:rows(m), m, :], hid[0:rows(m), x % 2, :], start=(m == 0), stop=(m == NM - 1))
            if m == NM - 1:
                ins.then_inc(s.e_y, 1)

        def turn(k):
            pe.wait_ge(s.e_ycopied, k + 1)
            if k:
                pe.wait_ge(s.e_added, 4 * k)
            for j in range(4):
                ins = nc.tensor.transpose(pt[:, 128 * j:128 * j + 128], yT[:, k % 2, 128 * j:128 * j + 128], c.ident[:])
            ins.then_inc(s.e_yT, 1)
        for x, (k, m) in enumerate(steps):
            r, tok = rows(m), slice(512 * k, 512 * k + 512)
            if x >= 2:
                pe.wait_ge(s.e_hidden, x - 1)
            nc.tensor.matmul(p1[0:r, x % 2, :], w13[:, m, 0, 0:r], c.xnT[:, tok], start=True, stop=True)
            ins = nc.tensor.matmul(p3[0:r, x % 2, :], w13[:, m, 1, 0:r], c.xnT[:, tok], start=True, stop=True)
            if m < NM - 1:
                ins = nc.tensor.matmul(pc[:, x % 2, :], sel[:, m, :], combT[:, tok], start=True, stop=True)
            ins.then_inc(s.e_made, 1)
            if x:
                down(x - 1)
            if m == 2 and k:
                turn(k - 1)
        down(len(steps) - 1)
        turn(3)

    @block.scalar
    def _(act):
        for k in range(4):
            act.wait_ge(s.e_combT, k + 1)
            nc.scalar.copy(combT[:, 512 * k:512 * k + 512], pt[0:E0, :]).then_inc(s.e_comb_copied, 1)
        for x, (k, m) in enumerate(steps):
            act.wait_ge(s.e_made, x + 1)
            if x >= 2:
                act.wait_ge(s.e_mul, x - 1)
            nc.scalar.activation(silu[0:rows(m), x % 2, :], p1[0:rows(m), x % 2, :], ACT.Silu).then_inc(s.e_silu, 1)
            if m == 1 and k:
                act.wait_ge(s.e_y, k)
                nc.scalar.copy(yT[:, (k - 1) % 2, :], py[:]).then_inc(s.e_ycopied, 1)
        act.wait_ge(s.e_y, 4)
        nc.scalar.copy(yT[:, 1, :], py[:]).then_inc(s.e_ycopied, 1)

    @block.vector
    def _(dve):
        def add(k):
            dve.wait_ge(s.e_yT, k + 1)
            for j in range(4):
                n = 4 * k + j
                nc.vector.scalar_tensor_tensor(out=c.x_res[:, n, :], in0=pt[:, 128 * j:128 * j + 128],
                                               scalar=c.tanh_g[:, 4:5], in1=c.x_res[:, n, :], op0=ALU.mult,
                                               op1=ALU.add).then_inc(s.e_added, 1)
        for x, (k, m) in enumerate(steps):
            r = rows(m)
            dve.wait_ge(s.e_silu, x + 1)
            nc.vector.tensor_tensor(silu[0:r, x % 2, :], silu[0:r, x % 2, :], p3[0:r, x % 2, :],
                                    ALU.mult).then_inc(s.e_mul, 1)
            dve.wait_ge(s.e_mul, x + 1)
            if m < NM - 1:
                ins = nc.vector.tensor_tensor(hid[0:r, x % 2, :], silu[0:r, x % 2, :], pc[0:r, x % 2, :], ALU.mult)
            else:
                ins = nc.vector.tensor_copy(hid[0:r, x % 2, :], silu[0:r, x % 2, :])
            ins.then_inc(s.e_hidden, 1)
            if m == 3 and k:
                add(k - 1)
        add(3)


HID, NJ = 512, 4
ROUND = 1.5 * 2 ** 23


def l2_ffn(nc, c, d):
    with ExitStack() as ctx:
        def sb(name, shape, dt=F32):
            return ctx.enter_context(nc.sbuf_tensor(uniq(name), shape, dt))
        w1q, w2q = sb("b_w1q", [D, HID]), sb("b_w2q", [128, NJ, D], BF16)
        wmean = sb("b_wmean", [128, 2])
        hidden = sb("b_hidden", [128, NJ, B, S])
        taps = sb("b_taps", [128, NJ, 4])
        with ExitStack() as cx:
            _l2_quantise(nc, c, d, w1q, w2q, wmean, taps, cx)
        with ExitStack() as cx:
            _l2_conv(nc, c, w1q, hidden, taps, cx)
        with ExitStack() as cx:
            _l2_down(nc, c, w2q, wmean, hidden, cx)


def _l2_quantise(nc, c, d, w1q, w2q, wmean, taps, ctx):
    s = sems(ctx, nc, "b_in b_sums b_total b_link b_round b_xq b_turned b_xnT")

    def sb(name, shape):
        return ctx.enter_context(nc.sbuf_tensor(uniq(name), shape, F32))
    w1, w2 = sb("b_w1", [D, HID]), sb("b_w2", [128, NJ * D])
    ones, part = sb("b_ones", [128, 128]), sb("b_part", [128, 2])
    wscale, xmax, xscale, xinv = sb("b_ws", [128, 2]), sb("b_xm", [128, NT]), sb("b_xs", [128, NT]), sb("b_xi", [128, NT])
    ps = ctx.enter_context(nc.psum_tensor(uniq("b_ps"), [128, 2], F32))
    pt = ctx.enter_context(nc.psum_tensor(uniq("b_pt"), [128, 4, 512], F32))
    block = ctx.enter_context(nc.Block())

    @block.sync
    def _(sp):
        for dst, src in ((w1, "b_w1"), (w2, "b_w2"), (taps, "b_taps")):
            sp.dma_start(dst[:], d[src]).then_inc(s.b_in, 16)

    @block.tensor
    def _(pe):
        pe.wait_ge(s.b_sums, 1)
        nc.tensor.matmul(ps[:], ones[:], part[:], start=True, stop=True).then_inc(s.b_total, 1)
        for k in range(4):
            pe.wait_ge(s.b_xq, k + 1)
            for j in range(4):
                ins = nc.tensor.transpose(pt[:, k, 128 * j:128 * j + 128], c.xn[:, 4 * k + j, :], c.ident[:])
            ins.then_inc(s.b_turned, 1)

    @block.scalar
    def _(act):
        for k in range(4):
            act.wait_ge(s.b_turned, k + 1)
            nc.scalar.copy(c.xnT[:, 512 * k:512 * k + 512], pt[:, k, :]).then_inc(s.b_xnT, 1)

    @block.vector
    def _(dve):
        link = Link(dve, s.b_link)
        link(nc.vector.tensor_reduce(xmax[:], c.xn[:], axis=AX.X, op=ALU.max, apply_absolute_value=True))
        link(nc.vector.tensor_scalar(xmax[:], xmax[:], 1e-5, None, ALU.max))
        link(nc.vector.reciprocal(xscale[:], xmax[:]))
        link(nc.vector.tensor_scalar(xscale[:], xscale[:], 127.0, None, ALU.mult))
        link(nc.vector.reciprocal(xinv[:], xscale[:]))
        link(nc.vector.tensor_tensor(c.xn[:], c.xn[:], bcast(xscale[:], [128, NT, D]), ALU.mult))
        link(nc.vector.tensor_scalar(c.xn[:], c.xn[:], ROUND, -ROUND, ALU.add, ALU.add))
        link(nc.vector.tensor_scalar(c.xn[:], c.xn[:], -128.0, 127.0, ALU.max, ALU.min))
        for k in range(4):
            t = slice(4 * k, 4 * k + 4)
            nc.vector.tensor_tensor(c.xn[:, t, :], c.xn[:, t, :], bcast(xinv[:, t], [128, 4, D]),
                                    ALU.mult).then_inc(s.b_xq, 1)
        dve.wait_ge(s.b_in, 48)
        nc.vector.memset(ones[:], 1.0)
        nc.vector.tensor_reduce(part[:, 0:1], w1[:], axis=AX.X, op=ALU.add, apply_absolute_value=True)
        nc.vector.tensor_reduce(part[:, 1:2], w2[:], axis=AX.X, op=ALU.add,
                                apply_absolute_value=True).then_inc(s.b_sums, 1)
        dve.wait_ge(s.b_total, 1)
        link(nc.vector.tensor_scalar(wmean[:], ps[:], 1.0 / (D * HID), 1e-5, ALU.mult, ALU.max))
        link(nc.vector.reciprocal(wscale[:], wmean[:]))
        link(nc.vector.reciprocal(wmean[:], wscale[:]))
        for x, w in enumerate((w1, w2)):
            link(nc.vector.tensor_scalar(w[:], w[:], wscale[:, x:x + 1], None, ALU.mult))
            link(nc.vector.tensor_scalar(w[:], w[:], ROUND, -ROUND, ALU.add, ALU.add))
            link(nc.vector.tensor_scalar(w[:], w[:], -1.0, 1.0, ALU.max, ALU.min))
        nc.vector.tensor_scalar(w1q[:], w1[:], wmean[:, 0:1], None, ALU.mult)
        nc.vector.tensor_copy(w2q[:].rearrange("p j n -> p (j n)"), w2[:])


def _l2_conv(nc, c, w1q, hidden, taps, ctx):
    s = sems(ctx, nc, "c_zero c_made c_copied c_middle c_left c_right c_silu")
    padded = ctx.enter_context(nc.sbuf_tensor(uniq("c_pad"), [128, 2, B, S + 2], F32))
    ph = ctx.enter_context(nc.psum_tensor(uniq("c_ph"), [128, 2, 4, 512], F32))
    block = ctx.enter_context(nc.Block())

    @block.tensor
    def _(pe):
        for j in range(NJ):
            if j >= 2:
                pe.wait_ge(s.c_copied, j - 1)
            for k in range(4):
                ins = nc.tensor.matmul(ph[:, j % 2, k, :], w1q[:, 128 * j:128 * j + 128],
                                       c.xnT[:, 512 * k:512 * k + 512], start=True, stop=True)
            ins.then_inc(s.c_made, 1)

    @block.scalar
    def _(act):
        act.wait_ge(s.c_zero, 1)
        for j in range(NJ):
            act.wait_ge(s.c_made, j + 1)
            if j >= 2:
                act.wait_ge(s.c_right, j - 1)
            nc.scalar.copy(padded[:, j % 2, :, 1:S + 1],
                           ph[:, j % 2, :, :].rearrange("p k (b t) -> p (k b) t", b=2)).then_inc(s.c_copied, 1)
            act.wait_ge(s.c_copied, j + 1)
            nc.scalar.activation(hidden[:, j, :, :], padded[:, j % 2, :, 1:S + 1], ACT.Identity,
                                 scale=taps[:, j, 1:2], bias=taps[:, j, 3:4]).then_inc(s.c_middle, 1)
        for j in range(NJ):
            act.wait_ge(s.c_right, j + 1)
            nc.scalar.activation(hidden[:, j, :, :], hidden[:, j, :, :], ACT.Silu).then_inc(s.c_silu, 1)

    @block.vector
    def _(dve):
        for p in range(2):
            nc.vector.memset(padded[:, p, :, 0:1], 0.0)
            ins = nc.vector.memset(padded[:, p, :, S + 1:S + 2], 0.0)
        ins.then_inc(s.c_zero, 1)
        for j in range(NJ):
            dve.wait_ge(s.c_middle, j + 1)
            nc.vector.scalar_tensor_tensor(out=hidden[:, j, :, :], in0=padded[:, j % 2, :, 0:S], scalar=taps[:, j, 0:1],
                                           in1=hidden[:, j, :, :], op0=ALU.mult, op1=ALU.add).then_inc(s.c_left, 1)
            dve.wait_ge(s.c_left, j + 1)
            nc.vector.scalar_tensor_tensor(out=hidden[:, j, :, :], in0=padded[:, j % 2, :, 2:S + 2], scalar=taps[:, j, 2:3],
                                           in1=hidden[:, j, :, :], op0=ALU.mult, op1=ALU.add).then_inc(s.c_right, 1)


def _l2_down(nc, c, w2q, wmean, hidden, ctx):
    s = sems(ctx, nc, "d_turned d_scaled d_rounded d_clipped d_q d_back d_copied d_y d_added d_link")

    def sb(name, shape, dt=F32):
        return ctx.enter_context(nc.sbuf_tensor(uniq(name), shape, dt))
    hmax, hscale, hinv = sb("d_max", [128, NT]), sb("d_scale", [128, NT]), sb("d_inv", [128, NT])
    rounded, q = sb("d_r", [128, 2, HID]), sb("d_qt", [128, 2, HID], BF16)
    qT = sb("d_qT", [128, 2, NJ, 128], BF16)
    factor, rnd, neg_rnd = sb("d_factor", [128, 1]), sb("d_rnd", [128, 1]), sb("d_nrnd", [128, 1])
    pt = ctx.enter_context(nc.psum_tensor(uniq("d_pt"), [128, 2, HID], F32))
    pb = ctx.enter_context(nc.psum_tensor(uniq("d_pb"), [128, 2, 2 * HID], BF16))
    py = ctx.enter_context(nc.psum_tensor(uniq("d_py"), [128, 2, 512], F32))
    hid = hidden[:].rearrange("p j b t -> p j (b t)")
    block = ctx.enter_context(nc.Block())

    @block.tensor
    def _(pe):
        def turn(n):
            if n >= 2:
                pe.wait_ge(s.d_rounded, n - 1)
            for j in range(NJ):
                ins = nc.tensor.transpose(pt[:, n % 2, 128 * j:128 * j + 128], hid[:, j, 128 * n:128 * n + 128], c.ident[:])
            ins.then_inc(s.d_turned, 1)
        turn(0)
        for n in range(NT):
            if n + 1 < NT:
                turn(n + 1)
            pe.wait_ge(s.d_q, n + 1)
            if n >= 2:
                pe.wait_ge(s.d_copied, n - 1)
            for j in range(NJ):
                ins = nc.tensor.transpose(pb[:, n % 2, 128 * j:128 * j + 128], q[:, n % 2, 128 * j:128 * j + 128], c.ident_b[:])
            ins.then_inc(s.d_back, 1)
            pe.wait_ge(s.d_copied, n + 1)
            if n >= 2:
                pe.wait_ge(s.d_added, n - 1)
            for j in range(NJ):
                ins = nc.tensor.matmul(py[:, n % 2, 0:D], qT[:, n % 2, j, :], w2q[:, j, :], start=(j == 0), stop=(j == NJ - 1))
            ins.then_inc(s.d_y, 1)

    @block.scalar
    def _(act):
        for n in range(NT):
            act.wait_ge(s.d_scaled, n + 1)
            nc.scalar.activation(rounded[:, n % 2, :], pt[:, n % 2, :], ACT.Identity, scale=hscale[:, n:n + 1],
                                 bias=rnd[:]).then_inc(s.d_rounded, 1)
            act.wait_ge(s.d_clipped, n + 1)
            nc.scalar.activation(q[:, n % 2, :], rounded[:, n % 2, :], ACT.Identity, bias=neg_rnd[:]).then_inc(s.d_q, 1)
            act.wait_ge(s.d_back, n + 1)
            nc.scalar.copy(qT[:, n % 2, :, :].rearrange("p j n -> p (j n)"), pb[:, n % 2, 0:HID]).then_inc(s.d_copied, 1)

    @block.vector
    def _(dve):
        link = Link(dve, s.d_link)
        nc.vector.memset(rnd[:], ROUND)
        nc.vector.memset(neg_rnd[:], -ROUND)
        link(nc.vector.tensor_tensor(factor[:], wmean[:, 1:2], c.tanh_g[:, 6:7], ALU.mult))

        def scale(n):
            t = slice(n, n + 1)
            dve.wait_ge(s.d_turned, n + 1)
            link(nc.vector.tensor_reduce(hmax[:, t], pt[:, n % 2, :], axis=AX.X, op=ALU.max, apply_absolute_value=True))
            link(nc.vector.tensor_scalar(hmax[:, t], hmax[:, t], 1e-5, None, ALU.max))
            link(nc.vector.reciprocal(hscale[:, t], hmax[:, t]))
            nc.vector.tensor_scalar(hscale[:, t], hscale[:, t], 127.0, None, ALU.mult).then_inc(s.d_scaled, 1)
            dve.wait_ge(s.d_scaled, n + 1)
            link(nc.vector.reciprocal(hinv[:, t], hscale[:, t]))
            nc.vector.tensor_scalar(hinv[:, t], hinv[:, t], factor[:], None, ALU.mult)
            dve.wait_ge(s.d_rounded, n + 1)
            nc.vector.tensor_scalar(rounded[:, n % 2, :], rounded[:, n % 2, :], ROUND - 128.0, ROUND + 127.0, ALU.max,
                                    ALU.min).then_inc(s.d_clipped, 1)

        def add(n):
            dve.wait_ge(s.d_y, n + 1)
            nc.vector.scalar_tensor_tensor(out=c.x_res[:, n, :], in0=py[:, n % 2, 0:D], scalar=hinv[:, n:n + 1],
                                           in1=c.x_res[:, n, :], op0=ALU.mult, op1=ALU.add).then_inc(s.d_added, 1)
        for n in range(NT):
            scale(n)
            if n:
                add(n - 1)
        add(NT - 1)


CAP = S // 2


def l1_ffn(nc, c, d):
    with ExitStack() as ctx:
        gate = ctx.enter_context(nc.sbuf_tensor(uniq("m_gate"), [128, NT], F32))
        values = ctx.enter_context(nc.sbuf_tensor(uniq("m_values"), [128, NT, VCOLS], F32))
        pieces = [nc.dram_tensor(f"m_{x}pieces", (NP, 128, NT * 128), BF16, kind="Internal").ap() for x in "qk"]
        mask = nc.dram_tensor("m_mask", (NT, 128), BF16, kind="Internal").ap()
        with ExitStack() as cx:
            _l1_choose(nc, c, d, gate, values, mask, cx)
        for x, name in enumerate(("m_q", "m_k")):
            with ExitStack() as cx:
                _l8_queries(nc, c, d, name, pieces[x], cx, biased=False)
        with ExitStack() as cx:
            _l1_core(nc, c, d, values, pieces, mask, cx)
        with ExitStack() as cx:
            _l1_out(nc, c, d, gate, cx)


def _l1_choose(nc, c, d, gate, values, mask, ctx):
    s = sems(ctx, nc, "h_in h_made h_gates h_link h_chosen h_turned h_masked h_out h_vmade h_vcopied")

    def sb(name, shape, dt=F32):
        return ctx.enter_context(nc.sbuf_tensor(uniq(name), shape, dt))
    wg, wv, before = sb("h_wg", [D, 128]), sb("h_wv", [D, 128]), sb("h_before", [128, TPB, S])
    rows, diag = sb("h_rows", [128, B, S]), sb("h_diag", [128, NT, 128])
    own, rank, chosen = sb("h_own", [128, NT]), sb("h_rank", [128, NT]), sb("h_chosen_t", [128, NT])
    more, same = sb("h_more", [128, B, TPB, S]), sb("h_same", [128, B, TPB, S])
    masked = sb("h_masked_t", [NT, 128], BF16)
    ps = ctx.enter_context(nc.psum_tensor(uniq("h_ps"), [128, 4, 512], F32))
    pv = ctx.enter_context(nc.psum_tensor(uniq("h_pv"), [128, 2, 512], F32))
    pm = ctx.enter_context(nc.psum_tensor(uniq("h_pm"), [NT, 128], F32))
    block = ctx.enter_context(nc.Block())

    @block.sync
    def _(sp):
        for dst, src in ((wg[:], d["m_Wg"]), (wv[:], d["m_Wv"]), (before[:], d["m_before"])):
            sp.dma_start(dst, src).then_inc(s.h_in, 16)
        sp.wait_ge(s.h_masked, 1)
        sp.dma_start(mask, masked[:]).then_inc(s.h_out, 16)
        sp.wait_ge(s.h_out, 16)

    @block.tensor
    def _(pe):
        pe.wait_ge(s.h_in, 48)
        for k in range(4):
            nc.tensor.matmul(ps[:, k, :], wg[:], c.xnT[:, 512 * k:512 * k + 512], start=True,
                             stop=True).then_inc(s.h_made, 1)
        for k in range(4):
            if k >= 2:
                pe.wait_ge(s.h_vcopied, k - 1)
            for j in range(4):
                n = 4 * k + j
                ins = nc.tensor.matmul(pv[:, k % 2, 128 * j:128 * j + 128], c.xnT[:, 128 * n:128 * n + 128], wv[:],
                                       start=True, stop=True)
            ins.then_inc(s.h_vmade, 1)
        pe.wait_ge(s.h_chosen, 1)
        nc.tensor.transpose(pm[:], chosen[:], c.ident[:]).then_inc(s.h_turned, 1)

    @block.scalar
    def _(act):
        for k in range(4):
            act.wait_ge(s.h_made, k + 1)
            nc.scalar.activation(rows[:, 2 * k:2 * k + 2, :], ps[:, k, :].rearrange("p (b t) -> p b t", b=2),
                                 ACT.Sigmoid).then_inc(s.h_gates, 1)
        for k in range(4):
            act.wait_ge(s.h_vmade, k + 1)
            nc.scalar.copy(values[:, 4 * k:4 * k + 4, 0:H8 * 9].rearrange("p j (h n) -> p j h n", n=9)[:, :, :, 0:DH8],
                           pv[:, k % 2, :].rearrange("p (j h n) -> p j h n", j=4, n=DH8)).then_inc(s.h_vcopied, 1)

    @block.gpsimd
    def _(pool):
        nc.gpsimd.memset(values[:, :, H8 * 9:], 0.0)
        nc.gpsimd.memset(values[:, :, 0:H8 * 9].rearrange("p j (h n) -> p j h n", n=9)[:, :, :, DH8:], 1.0)

    @block.vector
    def _(dve):
        link = Link(dve, s.h_link)
        dve.wait_ge(s.h_in, 48)
        dve.wait_ge(s.h_gates, 4)
        link(nc.vector.tensor_tensor(diag[:], rows[:].rearrange("p b (t n) -> p (b t) n", t=TPB),
                                     c.ident[:].unsqueeze(1).to_broadcast([128, NT, 128]), ALU.mult))
        link(nc.vector.reduce_sum(own[:], diag[:], AX.X))
        shape = [128, B, TPB, S]
        rival = rows[:].unsqueeze(2).to_broadcast(shape)
        mine = own[:].rearrange("p (b t) -> p b t", t=TPB).unsqueeze(3).to_broadcast(shape)
        nc.vector.tensor_tensor(more[:], rival, mine, ALU.is_gt)
        link(nc.vector.tensor_tensor(same[:], rival, mine, ALU.is_equal))
        link(nc.vector.tensor_tensor(same[:], same[:], before[:].unsqueeze(1).to_broadcast(shape), ALU.mult))
        link(nc.vector.tensor_tensor(more[:], more[:], same[:], ALU.add))
        link(nc.vector.reduce_sum(rank[:], more[:].rearrange("p b t n -> p (b t) n"), AX.X))
        nc.vector.tensor_scalar(chosen[:], rank[:], float(CAP), None, ALU.is_lt).then_inc(s.h_chosen, 1)
        dve.wait_ge(s.h_chosen, 1)
        nc.vector.tensor_tensor(gate[:], chosen[:], own[:], ALU.mult)
        dve.wait_ge(s.h_turned, 1)
        nc.vector.tensor_scalar(masked[:], pm[:], 1.0, BIG, ALU.subtract, ALU.mult).then_inc(s.h_masked, 1)


def _l1_core(nc, c, d, values, pieces, mask, ctx):
    s = sems(ctx, nc, "g_init g_rows g_zero_k")

    def sb(n, shape, dt=F32):
        return ctx.enter_context(nc.sbuf_tensor(uniq(f"g_{n}"), shape, dt))
    kaug, qaug = sb("kaug", [ROWS8, H8, B * S], BF16), sb("qaug", [ROWS8, H8, B * S], BF16)
    one_row = sb("one", [2, B * S], BF16)

    def head(x, at, k0, size):
        return x[:, at.h, bass.ds(at.b * S + k0, size)]
    cfg = Cfg()
    cfg.heads, cfg.scale, cfg.slots, cfg.turn_slot = H8, DH8 ** -0.5, 1, 0
    cfg.chunks, cfg.groups, cfg.keys = [(0, S)], [(0, 1), (1, 1)], lambda j: 128
    cfg.row, cfg.rows, cfg.row_dt = ROW_SHIFT, 2, BF16
    cfg.max_q = lambda at, t: head(qaug, at, 128 * t, 128)
    cfg.max_k = lambda at, k0, size: head(kaug, at, k0, size)
    cfg.score_k = lambda at, j: head(kaug, at, 128 * j, 128)
    cfg.score_q = lambda at: head(qaug, at, 0, S)
    cfg.shift_rows = lambda at: qaug[ROW_SHIFT:ROW_SHIFT + 2, at.h, bass.ds(at.b * S, S)]
    cfg.value = lambda at, j: stage[:, j, 9 * at.h:9 * at.h + 32]
    stage = sb("stage", [128, TPB, VCOLS])
    sv = sems(ctx, nc, "g_staged")
    core = Core(nc, ctx, c, cfg)
    strips = Strips(nc, ctx, c, core, TPB)
    block = ctx.enter_context(nc.Block())

    @block.gpsimd
    def _(pool):
        link = Link(pool, s.g_init)
        link(nc.gpsimd.memset(words(qaug[32:64, :, :]), 0.0))
        link(nc.gpsimd.memset(words(qaug[64:128, :, :]), 0.0))
        link(nc.gpsimd.memset(one_row[:], 1.0))
        link(nc.gpsimd.memset(strips.product[64:128, :, :], 0.0))
        link(nc.gpsimd.memset(core.shift_cols[:], 0.0))

    N_ROWS = 12 + 3

    def load(eng, aug, src, order):
        for x, y in enumerate(order):
            if 8 * x == 32:
                eng.wait_ge(s.g_init, 5)
                eng.wait_ge(s.g_zero_k, 2)
            eng.dma_start(aug[8 * x:8 * x + 8, :, :], src[y].rearrange("(h e) n -> e h n", e=DH8)).then_inc(s.g_rows, 16)

    @block.sync
    def _(sp):
        load(sp, kaug, pieces[1], K_PIECES)
        sp.dma_start(kaug[ROW_MASK:ROW_MASK + 1, :, :],
                     mask.rearrange("n t -> (n t)").unsqueeze(0).unsqueeze(0).to_broadcast([1, H8, B * S])) \
            .then_inc(s.g_rows, 16)
        sp.dma_start(qaug[ROW_MASK:ROW_MASK + 1, :, :],
                     one_row[0:1, :].unsqueeze(1).to_broadcast([1, H8, B * S])).then_inc(s.g_rows, 16)
        sp.dma_start(kaug[ROW_SHIFT:ROW_SHIFT + 2, :, :],
                     one_row[:].unsqueeze(1).to_broadcast([2, H8, B * S])).then_inc(s.g_rows, 16)

    @block.tensor
    def _(pe):
        strips.begin_pe(pe)
        pe.wait_ge(s.g_init, 5)
        pe.wait_ge(s.g_rows, 16 * N_ROWS)

        def prep(p, i, first):
            if first:
                strips.pe_first(pe)

        def run(p, i, last):
            pe.wait_ge(sv.g_staged, 2 * i + p + 1)
            core.pe_heads(pe, p, i, last, strips.pe_turn_free, lambda at: None)
            strips.pe(pe, p, i, last)
        batches(pe, prep, run)

    @block.scalar
    def _(act):
        core.begin_act(act)
        load(act, qaug, pieces[0], Q_PIECES)
        strips.act_batches(act, lambda: None)

    @block.vector
    def _(dve):
        strips.begin_dve(dve)
        link = Link(dve, s.g_zero_k)
        link(nc.vector.memset(words(kaug[32:64, :, :]), 0.0))
        link(nc.vector.memset(words(kaug[64:128, :, :]), 0.0))
        dve.wait_ge(s.g_init, 5)

        def prep(p, i, first):
            if first:
                core.dve_first(dve, At(cfg, p, i, 0), strips.link_of(dve))

        def run(p, i, last):
            b = 2 * i + p
            dve.wait_ge(core.s.values_used, b * H8 * core.NG + 2)
            nc.vector.tensor_copy(stage[:], values[:, bass.ds(TPB * b, TPB), :]).then_inc(sv.g_staged, 1)
            strips.dve(dve, p, i, b, last)
        batches(dve, prep, run)


def _l1_out(nc, c, d, gate, ctx):
    s = sems(ctx, nc, "j_w j_gated j_made j_added")
    wo = ctx.enter_context(nc.sbuf_tensor(uniq("j_w_t"), [128, D], F32))
    factor = ctx.enter_context(nc.sbuf_tensor(uniq("j_factor"), [128, NT], F32))
    py = ctx.enter_context(nc.psum_tensor(uniq("j_py"), [128, 4, 512], F32))
    block = ctx.enter_context(nc.Block())

    @block.sync
    def _(sp):
        sp.dma_start(wo[:], d["m_Wo"]).then_inc(s.j_w, 16)

    @block.tensor
    def _(pe):
        pe.wait_ge(s.j_w, 16)
        for n in range(NT):
            if n >= 4:
                pe.wait_ge(s.j_added, n - 3)
            nc.tensor.matmul(py[:, n % 4, 0:D], c.xnT[:, 128 * n:128 * n + 128], wo[:], start=True,
                             stop=True).then_inc(s.j_made, 1)

    @block.vector
    def _(dve):
        nc.vector.tensor_scalar(factor[:], gate[:], c.tanh_g[:, 5:6], None, ALU.mult).then_inc(s.j_gated, 1)
        dve.wait_ge(s.j_gated, 1)
        for n in range(NT):
            dve.wait_ge(s.j_made, n + 1)
            nc.vector.scalar_tensor_tensor(out=c.x_res[:, n, :], in0=py[:, n % 4, 0:D], scalar=factor[:, n:n + 1],
                                           in1=c.x_res[:, n, :], op0=ALU.mult, op1=ALU.add).then_inc(s.j_added, 1)


H3, DH3 = 2, 64
S3 = S + SC
KT3 = TPB + KT
GROUPS3 = [(0, 4), (4, 4), (8, 4), (12, 2), (14, 1)]
CHUNKS3 = [(0, 465), (465, 464), (929, 464), (1393, 464)]
R_ONE, R_MASK = DH3, DH3 + 1


def rows3(j):
    return KL if j == KT3 - 1 else 128


def l3_attention(nc, c, d):
    with ExitStack() as ctx:
        def sb(name, shape, dt=F32):
            return ctx.enter_context(nc.sbuf_tensor(uniq(name), shape, dt))
        qf, qb = sb("y_qf", [128, B, H3, S]), sb("y_qb", [128, B, H3, S], BF16)
        kv_own = sb("y_kvown", [128, NT, 2, H3, DH3])
        mask_rows = nc.dram_tensor("y_mask", (B, S3), F32, kind="Internal").ap()
        gains = sb("y_gains", [128, 2 * DC + 2 * D + 2 * DH3])
        w_all = sb("y_wall", [D, 3 * 128])
        w_kv = sb("y_wkv", [DC, 2 * 128])
        w_o = sb("y_wo", [DH3 + 1, H3, D + 1])
        bo = sb("y_bo", [1, D])
        at, views = 0, []
        for n in (DC, DC, D, D, DH3, DH3):
            views.append(gains[:, at:at + n])
            at += n
        gx, bx, gl, bl, gq, gk = views
        with ExitStack() as cx:
            _l3_load(nc, c, d, gains, w_all, w_kv, w_o, bo, mask_rows, cx)
        layer_norm(nc, c, c.xn, c.xn, c.xnT, gl, bl)
        with ExitStack() as cx:
            _l3_own(nc, c, w_all, gq, gk, qf, qb, kv_own, cx)
        with ExitStack() as cx:
            _l3_core(nc, c, d, qf, qb, kv_own, mask_rows, gx, bx, w_kv, cx)
        with ExitStack() as cx:
            heads_out(nc, c, qf, w_o, bo, cx, DH3, H3, 3)


def _l3_load(nc, c, d, gains, w_all, w_kv, w_o, bo, mask_rows, ctx):
    s = sems(ctx, nc, "y_in y_m y_masked y_mout")
    m32 = ctx.enter_context(nc.sbuf_tensor(uniq("y_m32"), [B, -(-SC // 4)], mybir.dt.int32))
    mf = ctx.enter_context(nc.sbuf_tensor(uniq("y_mf"), [B, S3], F32))
    block = ctx.enter_context(nc.Block())

    @block.sync
    def _(sp):
        sp.dma_start(m32[:], d["mask"]).then_inc(s.y_m, 16)
        sp.dma_start(gains[:], d["y_gains"].partition_broadcast(128)).then_inc(s.y_in, 16)
        for dst, src in ((w_all, "y_wall"), (w_kv, "y_wkv"), (w_o, "y_wo"), (bo, "y_bo")):
            sp.dma_start(dst[:], d[src]).then_inc(s.y_in, 16)
        sp.wait_ge(s.y_masked, 2)
        sp.dma_start(mask_rows, mf[:]).then_inc(s.y_mout, 16)
        sp.wait_ge(s.y_mout, 16)
        sp.wait_ge(s.y_in, 80)

    @block.vector
    def _(dve):
        nc.vector.memset(mf[:, 0:S], 0.0).then_inc(s.y_masked, 1)
        dve.wait_ge(s.y_m, 16)
        nc.vector.tensor_scalar(mf[:, S:S3], m32[:].bitcast(U8)[:, 0:SC], 1.0, BIG, ALU.subtract, ALU.mult).then_inc(s.y_masked, 1)


def _l3_own(nc, c, w_all, gq, gk, qf, qb, kv_own, ctx):
    s = sems(ctx, nc, "z_made z_copied z_link z_ss z_root z_q z_turned z_qf z_init")

    def sb(name, shape, dt=F32):
        return ctx.enter_context(nc.sbuf_tensor(uniq(name), shape, dt))
    q, sq, ss, root = sb("z_q_t", [128, NT, H3, DH3]), sb("z_sq", [128, NT, H3, DH3]), sb("z_ss_t", [128, NT * H3]), sb("z_r", [128, NT * H3])
    ps = ctx.enter_context(nc.psum_tensor(uniq("z_ps"), [128, 4, 512], F32))
    pt = ctx.enter_context(nc.psum_tensor(uniq("z_pt"), [128, 4, 512], F32))
    block = ctx.enter_context(nc.Block())

    @block.tensor
    def _(pe):
        for n in range(NT):
            if n >= 4:
                pe.wait_ge(s.z_copied, 2 * (n - 3))
            nc.tensor.matmul(ps[:, n % 4, 0:384], c.xnT[:, 128 * n:128 * n + 128], w_all[:], start=True,
                             stop=True).then_inc(s.z_made, 1)
        pe.wait_ge(s.z_q, 1)
        for b in range(B):
            if b >= 4:
                pe.wait_ge(s.z_qf, b - 3)
            for t in range(TPB):
                for h in range(H3):
                    ins = nc.tensor.transpose(pt[0:DH3, b % 4, h * S + 128 * t:h * S + 128 * t + 128],
                                              q[:, 2 * b + t, h, :], c.ident[:])
            ins.then_inc(s.z_turned, 1)

    @block.scalar
    def _(act):
        for n in range(NT):
            act.wait_ge(s.z_made, n + 1)
            nc.scalar.copy(q[:, n, :, :].rearrange("p h n -> p (h n)"), ps[:, n % 4, 0:128]).then_inc(s.z_copied, 1)
            nc.scalar.copy(kv_own[:, n, :, :, :].rearrange("p a h n -> p (a h n)"), ps[:, n % 4, 128:384]).then_inc(s.z_copied, 1)
        act.wait_ge(s.z_init, 2)
        for b in range(B):
            act.wait_ge(s.z_turned, b + 1)
            nc.scalar.copy(qf[0:DH3, b, :, :].rearrange("p h t -> p (h t)"), pt[0:DH3, b % 4, :]).then_inc(s.z_qf, 1)

    @block.gpsimd
    def _(pool):
        nc.gpsimd.memset(qf[DH3:128, :, :, :], 1.0).then_inc(s.z_init, 1)
        pool.wait_ge(s.z_init, 1)
        nc.gpsimd.memset(qb[DH3:128, :, :, :], 1.0).then_inc(s.z_init, 1)
        pool.wait_ge(s.z_init, 2)
        pool.wait_ge(s.z_ss, 1)
        nc.gpsimd.tensor_tensor(root[:], ss[:], c.neg_half[:, 0:NT * H3], ALU.pow).then_inc(s.z_root, 1)

    @block.vector
    def _(dve):
        link = Link(dve, s.z_link)
        flat = q[:].rearrange("p n h e -> p (n h) e")
        dve.wait_ge(s.z_copied, 2 * NT)
        link(nc.vector.tensor_tensor(sq[:], q[:], q[:], ALU.mult))
        link(nc.vector.reduce_sum(ss[:], sq[:].rearrange("p n h e -> p (n h) e"), AX.X))
        nc.vector.tensor_scalar(ss[:], ss[:], 1.0 / DH3, None, ALU.mult).then_inc(s.z_ss, 1)
        dve.wait_ge(s.z_root, 1)
        link(nc.vector.tensor_scalar(root[:], root[:], 1e8, None, ALU.min))
        link(nc.vector.tensor_tensor(flat, flat, bcast(root[:], [128, NT * H3, DH3]), ALU.mult))
        link(nc.vector.tensor_tensor(flat, flat, gq.unsqueeze(1).to_broadcast([128, NT * H3, DH3]), ALU.mult))
        nc.vector.tensor_tensor(flat, flat, gk.unsqueeze(1).to_broadcast([128, NT * H3, DH3]), ALU.mult).then_inc(s.z_q, 1)
        for b in range(B):
            dve.wait_ge(s.z_qf, b + 1)
            nc.vector.tensor_copy(qb[0:DH3, b, :, :], qf[0:DH3, b, :, :])


def _l3_core(nc, c, d, qf, qb, kv_own, mask_rows, gx, bx, w_kv, ctx):
    s = sems(ctx, nc, "x_ctx x_mask x_init x_link x_var x_rstd x_normed x_turned x_xT x_kv x_kvcopied "
                      "x_ss x_root x_k x_kturned x_kT x_kb x_batch x_out x_ksq")

    def sb(name, shape, dt=F32):
        return ctx.enter_context(nc.sbuf_tensor(uniq(name), shape, dt))
    raw = sb("x_raw", [128, KT, DC + 1])
    xc, sq = sb("x_xc", [128, KT, DC]), sb("x_sq_t", [128, KT3 * H3, DH3])
    stat = sb("x_stat", [128, 4, KT])
    xT = sb("x_xT_t", [DC, KT * 128])
    k = sb("x_k_t", [128, KT3, H3, DH3])
    v = sb("x_v", [128, KT3, H3, DH3 + 1])
    ss, root = sb("x_ss_t", [128, KT3 * H3]), sb("x_root_t", [128, KT3 * H3])
    kT, kb = sb("x_kT_t", [128, H3, KT3 * 128]), sb("x_kb_t", [128, H3, S3], BF16)
    mrow = sb("x_mrow", [DH3 + 1, S3])
    cfg = Cfg()
    cfg.heads, cfg.parities, cfg.scale = H3, 1, DH3 ** -0.5
    cfg.chunks, cfg.groups, cfg.keys = CHUNKS3, GROUPS3, rows3
    cfg.row, cfg.rows, cfg.row_dt = R_ONE, 1, F32
    cfg.max_q = lambda at, t: qb[:, bass.ds(at.b, 1), at.h, 128 * t:128 * t + 128].rearrange("p b t -> p (b t)")
    cfg.max_k = lambda at, k0, size: kb[:, at.h, k0:k0 + size]
    cfg.score_k = lambda at, j: kT[:, at.h, 128 * j:128 * j + rows3(j)]
    cfg.score_q = lambda at: qf[:, bass.ds(at.b, 1), at.h, :].rearrange("p b t -> p (b t)")
    cfg.shift_rows = lambda at: qf[R_ONE:R_ONE + 1, bass.ds(at.b, 1), at.h, :].rearrange("p b t -> p (b t)")
    cfg.value = lambda at, j: v[0:rows3(j), j, at.h, :]
    core = Core(nc, ctx, c, cfg)
    cfg.strips = 1
    cfg.out = lambda at, j: core.ps_out[0:DH3 + 1, 0:S]
    cfg.out_copied = s.x_out
    banks = core.ps_scores[:].rearrange("p a (x n) -> p (a x) n", n=512)
    NKV = -(-KT // 2)
    tiles4 = [range(4 * x, min(4 * x + 4, KT)) for x in range(4)]
    tiles3 = [range(4 * x, min(4 * x + 4, KT3)) for x in range(4)]
    block = ctx.enter_context(nc.Block())

    @block.sync
    def _(sp):
        for b in range(B):
            if b:
                sp.wait_ge(s.x_normed, b)
            sp.dma_start(raw[:], d["ctx_tok"][b]).then_inc(s.x_ctx, 16)
            if b:
                sp.wait_ge(s.x_batch, b)
            else:
                sp.wait_ge(s.x_init, 3)
            sp.dma_start(mrow[DH3:DH3 + 1, :], mask_rows[b:b + 1, :]).then_inc(s.x_mask, 16)
            for h in range(H3):
                sp.dma_start(kT[R_MASK:R_MASK + 1, h, 0:S3], mask_rows[b:b + 1, :]).then_inc(s.x_mask, 16)

    @block.gpsimd
    def _(pool):
        link = Link(pool, s.x_init)
        link(nc.gpsimd.memset(kb[DH3:128, :, :], 0.0))
        link(nc.gpsimd.memset(kT[DH3:128, :, :], 0.0))
        link(nc.gpsimd.memset(kT[DH3:DH3 + 1, :, :], 1.0))
        link(nc.gpsimd.memset(v[:, :, :, DH3:DH3 + 1], 1.0))
        link(nc.gpsimd.memset(core.shift_cols[:], 0.0))
        with pool.Fori(0, B) as b:
            pool.wait_ge(s.x_var, b + 1)
            nc.gpsimd.tensor_tensor(stat[:, 3, :], stat[:, 2, :], c.neg_half[:, 0:KT], ALU.pow).then_inc(s.x_rstd, 1)
            pool.wait_ge(s.x_ss, b + 1)
            nc.gpsimd.tensor_tensor(root[:], ss[:], c.neg_half[:, 0:KT3 * H3], ALU.pow).then_inc(s.x_root, 1)

    @block.tensor
    def _(pe):
        core.begin_pe(pe)
        pe.wait_ge(s.x_init, 5)

        with pe.Fori(0, B) as b:
            pe.wait_ge(core.s.exp_done, b * H3 * core.NG + 2)
            pe.wait_ge(s.x_normed, b + 1)
            for x in range(4):
                for y, j in enumerate(tiles4[x]):
                    ins = nc.tensor.transpose(banks[0:DC, x, 128 * y:128 * y + 128], xc[:, j, :], c.ident[:])
                ins.then_inc(s.x_turned, 1)
            for x in range(NKV):
                if x < 4:
                    pe.wait_ge(s.x_xT, 4 * b + 4)
                else:
                    pe.wait_ge(s.x_kvcopied, 2 * (NKV * b + x - 3))
                for y, j in enumerate(range(2 * x, min(2 * x + 2, KT))):
                    ins = nc.tensor.matmul(banks[:, x % 4, 256 * y:256 * y + 256], xT[:, 128 * j:128 * j + 128], w_kv[:],
                                           start=True, stop=True)
                ins.then_inc(s.x_kv, 1)
            pe.wait_ge(s.x_k, b + 1)
            for x in range(4):
                for y, j in enumerate(tiles3[x]):
                    ins = nc.tensor.transpose(banks[:, x, 128 * y:128 * y + 128],
                                              k[:, j, :, :].rearrange("p h e -> p (h e)"), c.ident[:])
                ins.then_inc(s.x_kturned, 1)
            pe.wait_ge(s.x_mask, 48 * (b + 1))
            pe.wait_ge(s.x_kT, 8 * (b + 1))
            pe.wait_ge(s.x_kb, b + 1)
            core.pe_first(pe, At(cfg, 0, b, 0))
            core.pe_heads(pe, 0, b, True)

    @block.scalar
    def _(act):
        core.begin_act(act)
        act.wait_ge(s.x_init, 5)

        def copy_out(at):
            return nc.scalar.copy(qf[0:DH3 + 1, bass.ds(at.b, 1), at.h, :].rearrange("p b t -> p (b t)"),
                                  core.ps_out[0:DH3 + 1, 0:S])
        with act.Fori(0, B) as b:
            nc.scalar.copy(k[:, 0:TPB, :, :], kv_own[:, bass.ds(TPB * b, TPB), 0, :, :])
            nc.scalar.copy(v[:, 0:TPB, :, 0:DH3], kv_own[:, bass.ds(TPB * b, TPB), 1, :, :])
            for x in range(4):
                act.wait_ge(s.x_turned, 4 * b + x + 1)
                n = 128 * len(tiles4[x])
                nc.scalar.copy(xT[:, 512 * x:512 * x + n], banks[0:DC, x, 0:n]).then_inc(s.x_xT, 1)
            for x in range(NKV):
                act.wait_ge(s.x_kv, NKV * b + x + 1)
                n = min(2, KT - 2 * x)
                both = banks[:, x % 4, 0:256 * n].rearrange("p (j a h e) -> p j a h e", j=n, a=2, h=H3)
                j = slice(TPB + 2 * x, TPB + 2 * x + n)
                nc.scalar.copy(k[:, j, :, :].rearrange("p j h e -> p j (h e)"),
                               both[:, :, 0, :, :].rearrange("p j h e -> p j (h e)")).then_inc(s.x_kvcopied, 1)
                nc.scalar.copy(v[:, j, :, 0:DH3], both[:, :, 1, :, :]).then_inc(s.x_kvcopied, 1)
            act.wait_ge(s.x_kvcopied, 2 * NKV * (b + 1))
            nc.scalar.activation(sq[:], k[:].rearrange("p j h e -> p (j h) e"), ACT.Square).then_inc(s.x_ksq, 1)
            for x in range(4):
                act.wait_ge(s.x_kturned, 4 * b + x + 1)
                n = 128 * len(tiles3[x])
                for h in range(H3):
                    nc.scalar.copy(kT[0:DH3, h, 512 * x:512 * x + n],
                                   banks[DH3 * h:DH3 * h + DH3, x, 0:n]).then_inc(s.x_kT, 1)
            core.act_heads(act, 0, b, copy_out)
            act.sem_inc(s.x_batch, 1)

    @block.vector
    def _(dve):
        core.begin_dve(dve)
        link = Link(dve, s.x_link)
        with dve.Fori(0, B) as b:
            link.enter(b, 10)
            dve.wait_ge(s.x_ctx, 16 * (b + 1))
            link(nc.vector.reduce_sum(stat[:, 0, :], raw[:, :, 0:DC], AX.X))
            link(nc.vector.tensor_scalar(stat[:, 0, :], stat[:, 0, :], 1.0 / DC, None, ALU.mult))
            link(nc.vector.tensor_tensor(xc[:], raw[:, :, 0:DC], bcast(stat[:, 0, :], [128, KT, DC]), ALU.subtract))
            squares = sq[:].rearrange("p a e -> p (a e)")[:, 0:KT * DC].rearrange("p (j n) -> p j n", j=KT)
            link(nc.vector.tensor_tensor(squares, xc[:], xc[:], ALU.mult))
            link(nc.vector.reduce_sum(stat[:, 1, :], squares, AX.X))
            nc.vector.tensor_scalar(stat[:, 2, :], stat[:, 1, :], 1.0 / DC, EPS, ALU.mult, ALU.add).then_inc(s.x_var, 1)
            dve.wait_ge(s.x_rstd, b + 1)
            link(nc.vector.tensor_tensor(xc[:], xc[:], bcast(stat[:, 3, :], [128, KT, DC]), ALU.mult))
            link(nc.vector.tensor_tensor(xc[:], xc[:], gx.unsqueeze(1).to_broadcast([128, KT, DC]), ALU.mult))
            nc.vector.tensor_tensor(xc[:], xc[:], bx.unsqueeze(1).to_broadcast([128, KT, DC]), ALU.add).then_inc(s.x_normed, 1)
            dve.wait_ge(s.x_ksq, b + 1)
            link(nc.vector.reduce_sum(ss[:], sq[:], AX.X))
            nc.vector.tensor_scalar(ss[:], ss[:], 1.0 / DH3, None, ALU.mult).then_inc(s.x_ss, 1)
            dve.wait_ge(s.x_root, b + 1)
            link(nc.vector.tensor_scalar(root[:], root[:], 1e8, None, ALU.min))
            flat = k[:].rearrange("p j h e -> p (j h) e")
            nc.vector.tensor_tensor(flat, flat, bcast(root[:], [128, KT3 * H3, DH3]), ALU.mult).then_inc(s.x_k, 1)
            dve.wait_ge(s.x_init, 5)
            dve.wait_ge(s.x_mask, 48 * (b + 1))
            for h in range(H3):
                nc.vector.tensor_copy(kb[DH3:DH3 + 1, h, :], mrow[DH3:DH3 + 1, :])
            dve.wait_ge(s.x_kT, 8 * (b + 1))
            link(nc.vector.tensor_copy(kb[0:DH3, :, :], kT[0:DH3, :, 0:S3]))
            dve.sem_inc(s.x_kb, 1)
            link.leave(B)
            core.dve_first(dve, At(cfg, 0, b, 0), lambda at: None)
            core.dve_heads(dve, 0, b, True, lambda at: None)


E3, I3, K3 = 32, 512, 8
WG3 = 4
NJ3 = I3 // 128


def l3_ffn(nc, c, d):
    with ExitStack() as ctx:
        def sb(name, shape, dt=F32):
            return ctx.enter_context(nc.sbuf_tensor(uniq(name), shape, dt))
        s = sems(ctx, nc, "w_in w_w2a w_w2b w_logit w_biased w_link w_exp w_top w_parts w_aT w_aTcopied w_mix "
                          "w_mixcopied w_h w_hbias w_gelu w_o w_ocopied w_oT w_oTcopied w_y w_ycopied")
        gate, gate_b = sb("w_gate", [D, E3]), sb("w_gateb", [E3, 1])
        b1, b2 = sb("w_b1", [128, NJ3, E3]), sb("w_b2", [D, E3])
        w1, w2 = sb("w_w1", [128, E3, I3]), sb("w_w2", [128, 2 * WG3, NJ3, D])
        logits = sb("w_logits", [E3, B, S])
        probs, rest, parts = sb("w_probs", [E3, B, S]), sb("w_rest", [E3, B, S]), sb("w_parts_t", [E3, B, S])
        top = sb("w_top_t", [E3, B, K3])
        stat = sb("w_stat", [E3, 4, B])
        aT = sb("w_aT_t", [128, NT, E3])
        mixed = sb("w_mixed", [D, E3, B])
        hidden = sb("w_hid", [128, NJ3, E3, B])
        hact = sb("w_hact", [128, NJ3, E3, B])
        oT, o = sb("w_oT_t", [D, E3, B]), sb("w_o_t", [E3, B, D])
        ps = ctx.enter_context(nc.psum_tensor(uniq("w_ps"), [128, 4, 512], F32))
        ph = ctx.enter_context(nc.psum_tensor(uniq("w_ph"), [128, 2, 512], F32))
        po = ctx.enter_context(nc.psum_tensor(uniq("w_po"), [128, 512], F32))
        pa = ctx.enter_context(nc.psum_tensor(uniq("w_pa"), [128, 512], F32))
        phv = ph[:].rearrange("p x (y e b) -> p (x y) e b", y=2, e=E3)
        pov = po[:, 0:E3 * B].rearrange("p (e b) -> p e b", b=B)
        w1_in, w2_in = sems(ctx, nc, " ".join(f"w_w1_{x}" for x in range(E3 // WG3))), [s.w_w2a, s.w_w2b]
        block = ctx.enter_context(nc.Block())

        @block.sync
        def _(sp):
            for dst, src in ((gate, "w_gate"), (gate_b, "w_gateb"), (b1, "w_b1"), (b2, "w_b2")):
                sp.dma_start(dst[:], d[src]).then_inc(s.w_in, 16)
            for x in range(E3 // WG3):
                e = slice(WG3 * x, WG3 * x + WG3)
                sp.dma_start(w1[:, e, :], d["w_w1"][:, e, :]).then_inc(w1_in[x], 16)
            for x in range(E3 // WG3):
                if x >= 2:
                    sp.wait_ge(s.w_o, WG3 * (x - 1))
                y = WG3 * (x % 2)
                sp.dma_start(w2[:, y:y + WG3, :, :], d["w_w2"][:, WG3 * x:WG3 * x + WG3, :, :]).then_inc(w2_in[x % 2], 16)

        @block.tensor
        def _(pe):
            pe.wait_ge(s.w_in, 64)
            for k in range(4):
                nc.tensor.matmul(ps[0:E3, k, :], gate[:], c.xnT[:, 512 * k:512 * k + 512], start=True,
                                 stop=True).then_inc(s.w_logit, 1)
            pe.wait_ge(s.w_parts, 1)
            for n in range(NT):
                ins = nc.tensor.transpose(pa[:, E3 * n:E3 * n + E3], parts[:, n // 2, 128 * (n % 2):128 * (n % 2) + 128],
                                          c.ident[0:E3, 0:E3])
            ins.then_inc(s.w_aT, 1)
            pe.wait_ge(s.w_aTcopied, 1)
            for b in range(B):
                for t in range(TPB):
                    n = TPB * b + t
                    ins = nc.tensor.matmul(po[:, E3 * b:E3 * b + E3], c.xn[:, n, :], aT[:, n, :], start=(t == 0), stop=(t == 1))
            ins.then_inc(s.w_mix, 1)
            pe.wait_ge(s.w_mixcopied, 1)
            for e in range(E3):
                pe.wait_ge(w1_in[e // WG3], 16)
                for j in range(NJ3):
                    ins = nc.tensor.matmul(phv[:, j, e, :], w1[:, e, 128 * j:128 * j + 128], mixed[:, e, :],
                                           start=True, stop=True)
                ins.then_inc(s.w_h, 1)
            pe.wait_ge(s.w_gelu, 1)
            for e in range(E3):
                x = e // WG3
                pe.wait_ge(w2_in[x % 2], 16 * (x // 2 + 1))
                for j in range(NJ3):
                    ins = nc.tensor.matmul(pov[:, e, :], w2[:, e % (2 * WG3), j, :], hact[:, j, e, :], start=(j == 0), stop=(j == NJ3 - 1))
                ins.then_inc(s.w_o, 1)
            pe.wait_ge(s.w_ocopied, 1)
            for b in range(B):
                ins = nc.tensor.transpose(ps[0:E3, b // 4, 128 * (b % 4):128 * (b % 4) + 128], oT[:, :, b], c.ident[:])
            ins.then_inc(s.w_oT, 1)
            pe.wait_ge(s.w_oTcopied, 1)
            for n in range(NT):
                if n >= 2:
                    pe.wait_ge(s.w_ycopied, n - 1)
                nc.tensor.matmul(ps[:, 2 + n % 2, 0:D], parts[:, n // 2, 128 * (n % 2):128 * (n % 2) + 128], o[:, n // 2, :],
                                 start=True, stop=True).then_inc(s.w_y, 1)

        @block.scalar
        def _(act):
            act.wait_ge(s.w_in, 64)
            for k in range(4):
                act.wait_ge(s.w_logit, k + 1)
                nc.scalar.activation(logits[:, 2 * k:2 * k + 2, :], ps[0:E3, k, :].rearrange("p (b t) -> p b t", b=2),
                                     ACT.Identity, bias=gate_b[:]).then_inc(s.w_biased, 1)
            act.wait_ge(s.w_link, 2)
            nc.scalar.activation(probs[:], logits[:], ACT.Exp).then_inc(s.w_exp, 1)
            act.wait_ge(s.w_hbias, 1)
            nc.scalar.activation(hact[:], hidden[:], ACT.Gelu).then_inc(s.w_gelu, 1)

        @block.vector
        def _(dve):
            link = Link(dve, s.w_link)
            dve.wait_ge(s.w_biased, 4)
            link(nc.vector.reduce_max(stat[:, 0, :], logits[:], AX.X))
            link(nc.vector.tensor_tensor(logits[:], logits[:], bcast(stat[:, 0, :], [E3, B, S]), ALU.subtract))
            dve.wait_ge(s.w_exp, 1)
            link(nc.vector.reduce_sum(stat[:, 1, :], probs[:], AX.X))
            link(nc.vector.reciprocal(stat[:, 2, :], stat[:, 1, :]))
            link(nc.vector.tensor_tensor(probs[:], probs[:], bcast(stat[:, 2, :], [E3, B, S]), ALU.mult))
            for b in range(B):
                ins = nc.vector.max(top[:, b, :], probs[:, b, :])
            link(ins)
            for b in range(B):
                ins = nc.vector.match_replace(rest[:, b, :], top[:, b, :], probs[:, b, :], -1.0)
            link(ins)
            nc.vector.scalar_tensor_tensor(out=parts[:], in0=rest[:], scalar=0.0, in1=probs[:], op0=ALU.is_lt,
                                           op1=ALU.mult).then_inc(s.w_parts, 1)
            dve.wait_ge(s.w_aT, 1)
            nc.vector.tensor_copy(aT[:].rearrange("p n e -> p (n e)"), pa[:]).then_inc(s.w_aTcopied, 1)
            dve.wait_ge(s.w_mix, 1)
            nc.vector.tensor_copy(mixed[:], po[:, 0:E3 * B].rearrange("p (b e) -> p e b", b=B)).then_inc(s.w_mixcopied, 1)
            dve.wait_ge(s.w_h, E3)
            for j in range(NJ3):
                ins = nc.vector.tensor_tensor(hidden[:, j, :, :], phv[:, j, :, :], bcast(b1[:, j, :], [128, E3, B]), ALU.add)
            ins.then_inc(s.w_hbias, 1)
            dve.wait_ge(s.w_o, E3)
            nc.vector.tensor_tensor(oT[:], pov, bcast(b2[:], [D, E3, B]), ALU.add).then_inc(s.w_ocopied, 1)
            dve.wait_ge(s.w_oT, 1)
            nc.vector.tensor_copy(o[:].rearrange("p b n -> p (b n)"), ps[0:E3, 0:2, :].rearrange("p x n -> p (x n)")) \
                .then_inc(s.w_oTcopied, 1)
            for n in range(NT):
                dve.wait_ge(s.w_y, n + 1)
                nc.vector.scalar_tensor_tensor(out=c.x_res[:, n, :], in0=ps[:, 2 + n % 2, 0:D], scalar=c.tanh_g[:, 7:8],
                                               in1=c.x_res[:, n, :], op0=ALU.mult, op1=ALU.add).then_inc(s.w_ycopied, 1)


def build(nc, d, stages=None):
    NAMES.clear()
    USED.clear()
    with ExitStack() as ctx:
        c = Chip()
        def sb(name, shape, dt=F32):
            return ctx.enter_context(nc.sbuf_tensor(uniq(name), shape, dt))
        c.x_res = sb("x_res", [128, NT, D])
        c.ident = sb("ident", [128, 128])
        c.ident_b = sb("ident_b", [128, 128], BF16)
        c.ones_row = sb("ones_row", [1, 128])
        c.strip_sum = sb("strip_sum", [128, 32])
        c.neg_half = sb("neg_half", [128, 128])
        c.tanh_g = sb("tanh_g", [128, 8])
        def normed(layer, *more):
            with ExitStack() as cx:
                c.xnT = cx.enter_context(nc.sbuf_tensor(uniq("xnT"), [D, NT * 128], F32))
                with ExitStack() as cy:
                    c.xn = (cx if layer in needs_xn else cy).enter_context(nc.sbuf_tensor(uniq("xn"), [128, NT, D], F32))
                    c.scratch = (cx if layer is l3_attention else cy).enter_context(
                        nc.sbuf_tensor(uniq("scratch"), [128, NT, D], F32))
                    layer_norm(nc, c, c.x_res, c.xn, c.xnT)
                layer(nc, c, d)
        needs_xn = [l2_ffn, l3_attention, l3_ffn]
        todo = [l0_attention, l0_ffn, l1_attention, l1_ffn, l2_attention, l2_ffn, l3_attention, l3_ffn]
        start(nc, c, d)
        for layer in todo[stages or slice(None)]:
            normed(layer)
            clear_semaphores(nc)
        finish(nc, c, d)


def _layouts(inp):
    f = {k: np.asarray(v) for k, v in inp.items()}
    t = {}
    t["x_tok"] = f["x"].reshape(NT, 128, D).transpose(1, 0, 2)
    t["gates"] = np.concatenate([f["g_xattn"], f["g_ffn"]]).reshape(1, 8)
    ctx = f["ctx_768"]
    ones = np.ones((B, SC, 1), np.float32)
    aug = np.concatenate([ctx, ones], 2)
    t["ctxT"] = aug.transpose(0, 2, 1)
    pad = np.concatenate([aug, np.zeros((B, KT * 128 - SC, DC + 1), np.float32)], 1)
    t["ctx_tok"] = pad.reshape(B, KT, 128, DC + 1).transpose(0, 2, 1, 3)
    w = np.zeros((DH0, H0, 4, 128), np.float32)
    w[:, :, 0, :] = f["L0_xattn_Wq"].reshape(D, H0, DH0).transpose(2, 1, 0)
    w[:, :, 1, :DC] = f["L0_xattn_Wk"].reshape(DC, H0, DH0).transpose(2, 1, 0)
    w[:, :, 2, :DC] = f["L0_xattn_Wv"].reshape(DC, H0, DH0).transpose(2, 1, 0)
    w[:, :, 3, :] = f["L0_xattn_Wo"].reshape(H0, DH0, D).transpose(1, 0, 2)
    t["l0_wT"] = w
    for n, src in (("l1", "L1_xattn_"), ("l2", "L2_xattn_")):
        t[f"{n}_Wq"] = f[src + "Wq"]
        t[f"{n}_bq"] = f[src + "bq"].reshape(128, 1)
        t[f"{n}_Wk"] = np.concatenate([f[src + "Wk"], f[src + "bk"].reshape(1, 128)])
        t[f"{n}_Wv"] = np.concatenate([f[src + "Wv"], f[src + "bv"].reshape(1, 128)])
    t["l1_Wo"], t["l1_bo"] = f["L1_xattn_Wo"], f["L1_xattn_bo"].reshape(1, D)
    t["l2_W1"] = f["L2_xattn_W1"].reshape(D, 2, 128)
    t["l2_b1"] = f["L2_xattn_b1"].reshape(2, 128).T
    t["l2_W2"] = f["L2_xattn_W2"].reshape(2, 128, D).transpose(1, 0, 2)
    t["l2_b2"] = f["L2_xattn_b2"].reshape(1, D)
    t["f0_gate"] = f["L0_ffn_gate_w"].T
    t["f0_bias"] = f["L0_ffn_gate_bias"].reshape(1, E0)
    t["before_e"] = np.tril(np.ones((1, E0, E0), np.float32), -1)
    t["before_g"] = np.tril(np.ones((1, NG0, NG0), np.float32), -1)
    nm = E0 // 2 + 1
    w13, w2 = np.zeros((D, nm, 2, 128), np.float32), np.zeros((128, nm, D), np.float32)
    for x, (many, one) in enumerate((("w1", "ws1"), ("w3", "ws3"))):
        w13[:, :nm - 1, x, :] = f["L0_ffn_" + many].reshape(nm - 1, 128, D).transpose(2, 0, 1)
        w13[:, nm - 1, x, :I0] = f["L0_ffn_" + one].T
    w2[:, :nm - 1, :] = f["L0_ffn_w2"].transpose(0, 2, 1).reshape(nm - 1, 128, D).transpose(1, 0, 2)
    w2[:I0, nm - 1, :] = f["L0_ffn_ws2"].T
    t["f0_w13"], t["f0_w2"] = w13, w2
    sel = np.zeros((E0, nm - 1, 128), np.float32)
    for e in range(E0):
        sel[e, e // 2, I0 * (e % 2):I0 * (e % 2) + I0] = 1
    t["f0_sel"] = sel
    t["b_w1"] = f["L2_ffn_w1"].T
    t["b_w2"] = f["L2_ffn_w2"].T.reshape(NJ, 128, D).transpose(1, 0, 2).reshape(128, NJ * D)
    t["b_taps"] = np.concatenate([f["L2_ffn_conv_w"].reshape(HID, 3), f["L2_ffn_conv_b"].reshape(HID, 1)], 1) \
        .reshape(NJ, 128, 4).transpose(1, 0, 2)
    t["m_Wg"] = np.broadcast_to(f["L1_ffn_Wg"], (D, 128))
    for n, src in (("m_q_Wq", "Wq"), ("m_k_Wq", "Wk"), ("m_Wv", "Wv"), ("m_Wo", "Wo")):
        t[n] = f["L1_ffn_" + src]
    t["m_before"] = np.tril(np.ones((S, S), np.float32), -1).reshape(TPB, 128, S).transpose(1, 0, 2)
    t["mask"] = np.pad(f["mask_BxS2_bk0"], ((0, 0), (0, -SC % 4))).view(np.int32)
    t["y_gains"] = np.concatenate([f["L3_xattn_" + n] for n in ("ln_x_g", "ln_x_b", "ln_l_g", "ln_l_b", "qn_g", "kn_g")])[None]
    t["y_wall"] = np.concatenate([f["L3_xattn_Wq"], f["L3_xattn_Wlkv"]]).T
    t["y_wkv"] = f["L3_xattn_Wkv"].T
    wo = np.zeros((DH3 + 1, H3, D + 1), np.float32)
    wo[:DH3, :, :D] = f["L3_xattn_Wo"].T.reshape(H3, DH3, D).transpose(1, 0, 2)
    wo[DH3, :, D] = 1
    t["y_wo"] = wo
    t["y_bo"] = f["L3_xattn_bo"].reshape(1, D)
    t["w_gate"] = f["L3_ffn_gate_w"].T
    t["w_gateb"] = f["L3_ffn_gate_b"].reshape(E3, 1)
    t["w_w1"] = f["L3_ffn_w1"][:, :D, :].transpose(1, 0, 2)
    t["w_b1"] = f["L3_ffn_w1"][:, D, :].reshape(E3, NJ3, 128).transpose(2, 1, 0)
    t["w_w2"] = f["L3_ffn_w2"][:, :I3, :].reshape(E3, NJ3, 128, D).transpose(2, 0, 1, 3)
    t["w_b2"] = f["L3_ffn_w2"][:, I3, :].T
    t["l0_bo"] = f["L0_xattn_bo"].reshape(1, D)
    return {k: np.ascontiguousarray(v) for k, v in t.items()}


def kernel(**inputs):
    import concourse.bacc as _bacc
    from concourse.bass_utils import run_bass_kernel_spmd as _run

    nc = _bacc.Bacc("TRN2", target_bir_lowering=False, num_devices=1)
    arrays = _layouts(inputs)
    d = {n: nc.dram_tensor(f"in_{n}", a.shape, mybir.dt.from_np(a.dtype), kind="ExternalInput").ap()
         for n, a in arrays.items()}
    d["out"] = nc.dram_tensor("out_0_dram", (128, NT, D), F32, kind="ExternalOutput").ap()
    build(nc, d)
    r = _run(nc, [{f"in_{n}": a for n, a in arrays.items()}], core_ids=[0])
    out = np.asarray(r.results[0]["out_0_dram"])
    return np.ascontiguousarray(out.transpose(1, 0, 2).reshape(B, S, D))
```
